# Optimizing a Trainium2 kernel written in Bass

```python
import numpy as np
import jax
import jax.numpy as jnp

def _softmax(x, axis=-1):
    return jax.nn.softmax(x, axis=axis)

def _gelu(x):
    return jax.nn.gelu(x, approximate=True)

def _silu(x):
    return jax.nn.silu(x)

def _sigmoid(x):
    return jax.nn.sigmoid(x)

def _layernorm(x, axis=-1, eps=1e-05):
    m = jnp.mean(x, axis=axis, keepdims=True)
    v = jnp.var(x, axis=axis, keepdims=True)
    return (x - m) / jnp.sqrt(v + eps)

def _scatter_add(tgt, idx, src, axis=0):
    return tgt.at[idx].add(src)

def _segment_sum(src, seg, n):
    return jax.ops.segment_sum(src, seg, n)
kernel_name = 'mk_gnn_preln_d4_gnn_r32_a3d53d'

def setup_inputs(seed: int=0):
    np.random.seed(seed)
    _w = jnp.asarray

    def _rec_inputs():
        import jax
        import jax.numpy as jnp
        _gk = jax.random.key(seed)
        x = -0.0009044 + 1 * jax.random.normal(jax.random.fold_in(_gk, 1), (3125, 16), jnp.float32)
        _s = jax.random.randint(jax.random.fold_in(_gk, 2), (50000,), 0, 3125, jnp.int32)
        _d = jax.random.randint(jax.random.fold_in(_gk, 3), (50000,), 0, 3125, jnp.int32)
        _loop = jnp.arange(3125, dtype=jnp.int32)
        src = jnp.concatenate([_s, _d, _loop])
        dst = jnp.concatenate([_d, _s, _loop])
        _o = jnp.argsort(dst, stable=True)
        src = src[_o]
        dst = dst[_o]
        edge_attr_4 = -0.000192005 + 0.999979 * jax.random.normal(jax.random.fold_in(_gk, 12), (103125, 4), jnp.float32)
        edge_attr_8 = -0.00019784 + 0.999804 * jax.random.normal(jax.random.fold_in(_gk, 13), (103125, 8), jnp.float32)
        return (x, src, dst, edge_attr_4, edge_attr_8)
    x, src, dst, edge_attr_4, edge_attr_8 = _rec_inputs()

    def _L0_gnn_setup():
        import jax, jax.numpy as jnp
        import numpy as np
        N_NODES = 3125
        N_EDGES = 100000
        NODE_DIM = 16
        EDGE_IN = 2 * NODE_DIM
        EDGE_OUT = 9
        HIDDEN = 9
        MSG_ROUNDS = 3

        def _mlp_params(key, d_in, d_hid, d_out):
            k1, k2, k3 = jax.random.split(key, 3)
            s1 = 1.0 / np.sqrt(d_in)
            s2 = 1.0 / np.sqrt(d_hid)
            return (jax.random.normal(k1, (d_in, d_hid), jnp.float32) * s1, jnp.zeros((d_hid,), jnp.float32), jax.random.normal(k2, (d_hid, d_hid), jnp.float32) * s2, jnp.zeros((d_hid,), jnp.float32), jax.random.normal(k3, (d_hid, d_out), jnp.float32) * s2, jnp.zeros((d_out,), jnp.float32))

        def _mlp3(h, W1, b1, W2, b2, W3, b3):
            h = jax.nn.relu(h @ W1 + b1)
            h = jax.nn.relu(h @ W2 + b2)
            return h @ W3 + b3
        key = jax.random.key(seed)
        kx, ks, kd, kfe, kfx = jax.random.split(key, 5)
        X = jax.random.normal(kx, (N_NODES, NODE_DIM), jnp.float32)
        edge_src = jax.random.randint(ks, (N_EDGES,), 0, N_NODES, jnp.int32)
        edge_dst = jax.random.randint(kd, (N_EDGES,), 0, N_NODES, jnp.int32)
        fe = _mlp_params(kfe, EDGE_IN, HIDDEN, EDGE_OUT)
        fx = _mlp_params(kfx, EDGE_OUT + NODE_DIM, HIDDEN, NODE_DIM)
        return {'X': X, 'edge_src': edge_src, 'edge_dst': edge_dst, 'fe_W1': fe[0], 'fe_b1': fe[1], 'fe_W2': fe[2], 'fe_b2': fe[3], 'fe_W3': fe[4], 'fe_b3': fe[5], 'fx_W1': fx[0], 'fx_b1': fx[1], 'fx_W2': fx[2], 'fx_b2': fx[3], 'fx_W3': fx[4], 'fx_b3': fx[5]}
    _L0_gnn_all = _L0_gnn_setup()
    _L0_gnn_in = {k: v for k, v in _L0_gnn_all.items() if k in ('fe_W1', 'fe_b1', 'fe_W2', 'fe_b2', 'fe_W3', 'fe_b3', 'fx_W1', 'fx_b1', 'fx_W2', 'fx_b2', 'fx_W3', 'fx_b3')}
    del _L0_gnn_all

    def _L1_gnn_setup():
        import jax, jax.numpy as jnp
        import numpy as np
        N = 3125
        E = 31250
        IN_V = 16
        OUT_V = 16
        IN_E = 4
        EPS = 1e-05
        SLOPE = 0.01
        key = jax.random.key(seed)
        ks = jax.random.split(key, 9)
        v = jax.random.normal(ks[0], (N, IN_V), jnp.float32)
        e = jax.random.normal(ks[1], (E, IN_E), jnp.float32)
        edge_index = jax.random.randint(ks[2], (2, E), 0, N, jnp.int32)
        enet_w = jax.random.normal(ks[3], (IN_V * OUT_V, IN_E), jnp.float32) / np.sqrt(IN_E)
        enet_b = jax.random.normal(ks[4], (IN_V * OUT_V,), jnp.float32) * 0.01
        root = jax.random.normal(ks[5], (IN_V, OUT_V), jnp.float32) / np.sqrt(IN_V)
        bias = jax.random.normal(ks[6], (OUT_V,), jnp.float32) * 0.01
        gamma = jnp.ones((OUT_V,), jnp.float32) + 0.1 * jax.random.normal(ks[7], (OUT_V,), jnp.float32)
        beta = 0.1 * jax.random.normal(ks[8], (OUT_V,), jnp.float32)
        return {'v': v, 'e': e, 'edge_index': edge_index, 'enet_w': enet_w, 'enet_b': enet_b, 'root': root, 'bias': bias, 'gamma': gamma, 'beta': beta}
    _L1_gnn_all = _L1_gnn_setup()
    _L1_gnn_in = {k: v for k, v in _L1_gnn_all.items() if k in ('enet_w', 'enet_b', 'root', 'bias', 'gamma', 'beta')}
    del _L1_gnn_all

    def _L2_gnn_setup():
        import jax, jax.numpy as jnp
        import numpy as np
        N_NODES = 3125
        N_EDGES = 25000
        NFC = 16
        EFC = 8
        key = jax.random.key(seed)
        k1, k2, k3, k4 = jax.random.split(key, 4)
        node_features = jax.random.normal(k1, (N_NODES, NFC), dtype=jnp.float32)
        edge_features = jax.random.normal(k2, (N_EDGES, EFC), dtype=jnp.float32)
        pair_indices = jax.random.randint(k3, (N_EDGES, 2), 0, N_NODES, dtype=jnp.int32)
        kernel = jax.random.normal(k4, (EFC, NFC * NFC), dtype=jnp.float32) * (2.0 / (EFC + NFC * NFC)) ** 0.5
        bias = jnp.zeros((NFC * NFC,), dtype=jnp.float32)
        return {'node_features': node_features, 'edge_features': edge_features, 'pair_indices': pair_indices, 'kernel': kernel, 'bias': bias}
    _L2_gnn_all = _L2_gnn_setup()
    _L2_gnn_in = {k: v for k, v in _L2_gnn_all.items() if k in ('kernel', 'bias')}
    del _L2_gnn_all

    def _L3_gnn_setup():
        import jax, jax.numpy as jnp
        import numpy as np
        N_NODES = 50000
        N_EDGES = 25000
        D = 16
        key = jax.random.key(seed)
        k1, k2, k3, k4 = jax.random.split(key, 4)
        x = jax.random.normal(k1, (N_NODES, D), dtype=jnp.float32)
        edge_index = jax.random.randint(k2, (2, N_EDGES), 0, N_NODES, dtype=jnp.int64)
        W_tp = jax.random.normal(k3, (D, D, D), dtype=jnp.float32) * (1.0 / D)
        weight = jax.random.normal(k4, (D, D), dtype=jnp.float32) * 0.01
        bias = jnp.zeros((D,), dtype=jnp.float32)
        return {'x': x, 'edge_index': edge_index, 'W_tp': W_tp, 'weight': weight, 'bias': bias}
    _L3_gnn_all = _L3_gnn_setup()
    _L3_gnn_in = {k: v for k, v in _L3_gnn_all.items() if k in ('W_tp', 'weight', 'bias')}
    del _L3_gnn_all
    return {'x': x, 'src': src, 'dst': dst, 'edge_attr_4': edge_attr_4, 'edge_attr_8': edge_attr_8, 'L0_gnn_fe_W1': _L0_gnn_in['fe_W1'], 'L0_gnn_fe_b1': _L0_gnn_in['fe_b1'], 'L0_gnn_fe_W2': _L0_gnn_in['fe_W2'], 'L0_gnn_fe_b2': _L0_gnn_in['fe_b2'], 'L0_gnn_fe_W3': _L0_gnn_in['fe_W3'], 'L0_gnn_fe_b3': _L0_gnn_in['fe_b3'], 'L0_gnn_fx_W1': _L0_gnn_in['fx_W1'], 'L0_gnn_fx_b1': _L0_gnn_in['fx_b1'], 'L0_gnn_fx_W2': _L0_gnn_in['fx_W2'], 'L0_gnn_fx_b2': _L0_gnn_in['fx_b2'], 'L0_gnn_fx_W3': _L0_gnn_in['fx_W3'], 'L0_gnn_fx_b3': _L0_gnn_in['fx_b3'], 'L1_gnn_enet_w': _L1_gnn_in['enet_w'], 'L1_gnn_enet_b': _L1_gnn_in['enet_b'], 'L1_gnn_root': _L1_gnn_in['root'], 'L1_gnn_bias': _L1_gnn_in['bias'], 'L1_gnn_gamma': _L1_gnn_in['gamma'], 'L1_gnn_beta': _L1_gnn_in['beta'], 'L2_gnn_kernel': _L2_gnn_in['kernel'], 'L2_gnn_bias': _L2_gnn_in['bias'], 'L3_gnn_W_tp': _L3_gnn_in['W_tp'], 'L3_gnn_weight': _L3_gnn_in['weight'], 'L3_gnn_bias': _L3_gnn_in['bias']}

def reference(x, src, dst, edge_attr_4, edge_attr_8, L0_gnn_fe_W1, L0_gnn_fe_b1, L0_gnn_fe_W2, L0_gnn_fe_b2, L0_gnn_fe_W3, L0_gnn_fe_b3, L0_gnn_fx_W1, L0_gnn_fx_b1, L0_gnn_fx_W2, L0_gnn_fx_b2, L0_gnn_fx_W3, L0_gnn_fx_b3, L1_gnn_enet_w, L1_gnn_enet_b, L1_gnn_root, L1_gnn_bias, L1_gnn_gamma, L1_gnn_beta, L2_gnn_kernel, L2_gnn_bias, L3_gnn_W_tp, L3_gnn_weight, L3_gnn_bias):
    import jax
    import jax.numpy as jnp

    def _L0_gnn_ref(X, edge_src, edge_dst, fe_W1, fe_b1, fe_W2, fe_b2, fe_W3, fe_b3, fx_W1, fx_b1, fx_W2, fx_b2, fx_W3, fx_b3):
        import jax, jax.numpy as jnp
        import numpy as np
        N_NODES = 3125
        N_EDGES = 100000
        NODE_DIM = 16
        EDGE_IN = 2 * NODE_DIM
        EDGE_OUT = 9
        HIDDEN = 9
        MSG_ROUNDS = 3

        def _mlp_params(key, d_in, d_hid, d_out):
            k1, k2, k3 = jax.random.split(key, 3)
            s1 = 1.0 / np.sqrt(d_in)
            s2 = 1.0 / np.sqrt(d_hid)
            return (jax.random.normal(k1, (d_in, d_hid), jnp.float32) * s1, jnp.zeros((d_hid,), jnp.float32), jax.random.normal(k2, (d_hid, d_hid), jnp.float32) * s2, jnp.zeros((d_hid,), jnp.float32), jax.random.normal(k3, (d_hid, d_out), jnp.float32) * s2, jnp.zeros((d_out,), jnp.float32))

        def _mlp3(h, W1, b1, W2, b2, W3, b3):
            h = jax.nn.relu(h @ W1 + b1)
            h = jax.nn.relu(h @ W2 + b2)
            return h @ W3 + b3
        n = X.shape[0]
        for _ in range(MSG_ROUNDS):
            e_in = jnp.concatenate([X[edge_dst], X[edge_src]], axis=-1)
            msgs = _mlp3(e_in, fe_W1, fe_b1, fe_W2, fe_b2, fe_W3, fe_b3)
            m = jax.ops.segment_sum(msgs, edge_dst, num_segments=n)
            X = _mlp3(jnp.concatenate([X, m], axis=-1), fx_W1, fx_b1, fx_W2, fx_b2, fx_W3, fx_b3)
        return X

    def _L1_gnn_ref(v, e, edge_index, enet_w, enet_b, root, bias, gamma, beta):
        import jax, jax.numpy as jnp
        import numpy as np
        N = 3125
        E = 31250
        IN_V = 16
        OUT_V = 16
        IN_E = 4
        EPS = 1e-05
        SLOPE = 0.01
        n = v.shape[0]
        src, dst = (edge_index[0], edge_index[1])
        w = (e @ enet_w.T + enet_b).reshape(-1, IN_V, OUT_V)
        msg = jnp.einsum('ei,eio->eo', v[src], w)
        summed = jax.ops.segment_sum(msg, dst, num_segments=n)
        cnt = jax.ops.segment_sum(jnp.ones((msg.shape[0],), v.dtype), dst, num_segments=n)
        out = summed / jnp.clip(cnt, 1.0)[:, None]
        out = out + v @ root + bias
        mu = out.mean(axis=0)
        var = out.var(axis=0)
        out = gamma * (out - mu) * jax.lax.rsqrt(var + EPS) + beta
        return jnp.where(out >= 0, out, SLOPE * out)

    def _L2_gnn_ref(node_features, edge_features, pair_indices, kernel, bias):
        import jax, jax.numpy as jnp
        import numpy as np
        N_NODES = 3125
        N_EDGES = 25000
        NFC = 16
        EFC = 8
        nfc = node_features.shape[-1]
        num_nodes = node_features.shape[0]
        edge_mats = (edge_features @ kernel + bias).reshape(-1, nfc, nfc)
        neighbors = node_features[pair_indices[:, 1]]
        transformed = jnp.einsum('eij,ej->ei', edge_mats, neighbors)
        aggregated = jax.ops.segment_sum(transformed, pair_indices[:, 0], num_segments=num_nodes)
        return aggregated

    def _L3_gnn_ref(x, edge_index, W_tp, weight, bias):
        import jax, jax.numpy as jnp
        import numpy as np
        N_NODES = 50000
        N_EDGES = 25000
        D = 16
        row, col = (edge_index[0], edge_index[1])
        xr = x[row]
        xc = x[col]
        messages = jnp.einsum('eu,ev,uvw->ew', xr, xc, W_tp)
        out = jnp.zeros((x.shape[0], D), dtype=x.dtype).at[row].add(messages)
        return out @ weight.T + bias
    edge_index = jnp.stack([src, dst])
    edge_index_t = jnp.stack([src, dst], axis=1)
    h = jnp.maximum(_layernorm(x, axis=-1), 0.0)
    x = x + _L0_gnn_ref(h, src, dst, L0_gnn_fe_W1, L0_gnn_fe_b1, L0_gnn_fe_W2, L0_gnn_fe_b2, L0_gnn_fe_W3, L0_gnn_fe_b3, L0_gnn_fx_W1, L0_gnn_fx_b1, L0_gnn_fx_W2, L0_gnn_fx_b2, L0_gnn_fx_W3, L0_gnn_fx_b3)
    h = jnp.maximum(_layernorm(x, axis=-1), 0.0)
    x = x + _L1_gnn_ref(h, edge_attr_4, edge_index, L1_gnn_enet_w, L1_gnn_enet_b, L1_gnn_root, L1_gnn_bias, L1_gnn_gamma, L1_gnn_beta)
    h = jnp.maximum(_layernorm(x, axis=-1), 0.0)
    x = x + _L2_gnn_ref(h, edge_attr_8, edge_index_t, L2_gnn_kernel, L2_gnn_bias)
    h = jnp.maximum(_layernorm(x, axis=-1), 0.0)
    x = x + _L3_gnn_ref(h, edge_index, L3_gnn_W_tp, L3_gnn_weight, L3_gnn_bias)
    return x

_drawn_inputs = setup_inputs


def setup_inputs(seed=0):
    import zlib

    import numpy as np

    out = dict(_drawn_inputs(seed))
    spreads = {'L0_gnn_fe_b1': (0.0, 0.1),
     'L0_gnn_fe_b2': (0.0, 0.1),
     'L0_gnn_fe_b3': (0.0, 0.276),
     'L0_gnn_fx_b1': (0.0, 2.0),
     'L0_gnn_fx_b2': (0.0, 0.8),
     'L0_gnn_fx_b3': (0.0, 0.1),
     'L2_gnn_bias': (0.0, 0.1),
     'L3_gnn_bias': (0.0, 2.0)}
    factors = {'edge_attr_4': 4.236,
     'L1_gnn_enet_w': 4.692,
     'L1_gnn_enet_b': 200.0,
     'L1_gnn_root': 64.0,
     'L1_gnn_bias': 200.0,
     'L1_gnn_gamma': 39.311,
     'L1_gnn_beta': 32.575,
     'L3_gnn_W_tp': 7.726,
     'L3_gnn_weight': 4.881}
    for name, (base, spread) in spreads.items():
        noise = np.random.default_rng([zlib.crc32(name.encode()), seed]).standard_normal(out[name].shape)
        drawn = base * np.exp(spread * noise) if base else spread * noise
        out[name] = jnp.asarray(drawn.astype(out[name].dtype))
    for name, factor in factors.items():
        out[name] = (out[name] * factor).astype(out[name].dtype)
    return out
```

```python
import concourse.bass as bass
from concourse import mybir
from contextlib import ExitStack


def gnn_program(
    nc: bass.Bass,
    x_in, src_in, dst_in, ea4_in, ea8_in,
    fe_W1, fe_b1, fe_W2, fe_b2, fe_W3, fe_b3,
    fx_W1, fx_b1, fx_W2, fx_b2, fx_W3, fx_b3,
    enet_w, enet_b, root, c_bias, gamma, beta,
    k2_w, k2_b, w_tp, w_out, b_out,
    out,
):
    fp32, fp16, i32 = mybir.dt.float32, mybir.dt.float16, mybir.dt.int32
    ALU = mybir.AluOpType
    ACT = mybir.ActivationFunctionType
    AX = mybir.AxisListType

    N, F = x_in.shape
    E = src_in.shape[0]
    HID = fe_W2.shape[0]
    ROWS, BLOCKS = 114, 28
    LAST = N - ROWS * (BLOCKS - 1)
    HI = BLOCKS // 2
    GT = 8
    T = 816
    NG = T // GT
    FULL = E // T
    REST = E - FULL * T
    EC = GT * 128
    PAD_NODE = 4000
    BIG = 32768.0
    TABLE_TOP = 4096.0
    H_SCALE = 2048.0
    PART_TOP = 16384.0
    EPS = 1e-5
    Q7, Q4 = 7, 4
    SPAN7, SPAN4 = ROWS * BLOCKS // Q7, ROWS * BLOCKS // Q4
    K1, K2 = ea4_in.shape[1] + 1, ea8_in.shape[1] + 1
    ROUNDS = 3
    DENSE_PER_ROUND = 6
    assert N <= ROWS * BLOCKS and E <= 128 * T and FULL >= 96 and (NG - 4) % 2 == 0

    def dram(name, shape, dt):
        return nc.dram_tensor(name, shape, dt, kind="Internal").ap()

    lo_dram = [dram("lo_dst", [T, 128], fp16), dram("lo_src", [T, 128], fp16)]
    hi_dram = [dram("hi_dst", [T, 128], fp16), dram("hi_src", [T, 128], fp16)]

    ctx = ExitStack()
    with ctx:
        def sb(name, shape, dt=fp32):
            return ctx.enter_context(nc.sbuf_tensor(name, shape, dt))

        def sem(name):
            return ctx.enter_context(nc.semaphore(name))

        m7d = sb("m7d", [128, T])
        m4d = sb("m4d", [128, T])
        m4s = sb("m4s", [128, T])
        q7d = sb("q7d", [128, T, Q7], fp16)
        q4d = sb("q4d", [128, T, Q4], fp16)
        q4s = sb("q4s", [128, T, Q4], fp16)
        ea4 = sb("ea4", [128, T, K1 - 1])
        ea8 = sb("ea8", [128, T, K2 - 1])
        work = sb("work", [128, BLOCKS * F * F])
        idx_i = [work[:, i * T:(i + 1) * T].bitcast(i32) for i in (0, 1)]
        idx_f = [work[:, i * T:(i + 1) * T] for i in (2, 3)]
        qf = work[:, 4 * T:5 * T]
        lo_f = work[:, 5 * T:6 * T]
        hi_f = work[:, 6 * T:7 * T]
        jd = work[:, 7 * T:8 * T]
        rd = work[:, 0:T]
        outer = work[0:ROWS, :].rearrange("p (j u v) -> p j u v", u=F, v=F)
        stage = sb("stage", [128, 2, 7 * 128], fp16)

        iota_i = sb("iota_i", [128, SPAN4], i32)
        iota_m = sb("iota_m", [128, SPAN4], fp16)
        iota_f = sb("iota_f", [128, 128])
        part_i = sb("part_i", [128, 1], i32)
        part_f = sb("part_f", [128, 1])
        past = sb("past", [128, 1])
        pv = sb("pv", [128, 2])
        ident = sb("ident", [128, 128])
        ones = sb("ones", [128, 128])
        top1 = sb("top1", [1, 1])
        nmask_i = sb("nmask_i", [ROWS, BLOCKS], i32)
        nmask = sb("nmask", [ROWS, BLOCKS])
        eps_t = sb("eps_t", [128, 1])

        bd_ab = sb("bd_ab", [112, 7, 2 * HID])
        bd_m = sb("bd_m", [112, 7, HID])
        bd_x1 = sb("bd_x1", [112, 7, HID])
        bd_m1 = sb("bd_m1", [112, 7, HID])
        bd_2 = sb("bd_2", [112, 7, HID])
        bd_3 = sb("bd_3", [112, 7, F])
        bd_root = sb("bd_root", [112, 7, F])
        bd_out = sb("bd_out", [112, 7, F])
        bd_e = sb("bd_e", [128, GT, HID])
        bd_y1 = sb("bd_y1", [128, GT, K1 * F])
        bd_y2 = sb("bd_y2", [128, GT, K2 * F])
        wt = sb("wt", [128, 2, F])
        bias = {n: sb("b_" + n, [ROWS, a.shape[0]]) for n, a in
                dict(e1=fe_b1, e3=fe_b3, x1=fx_b1, x2=fx_b2, x3=fx_b3, c=c_bias, g=gamma, be=beta,
                     o=b_out).items()}

        X = sb("X", [ROWS, BLOCKS, F])
        Hn = sb("Hn", [ROWS, BLOCKS, F])
        U = sb("U", [ROWS, BLOCKS, F])
        V = sb("V", [ROWS, BLOCKS, F])
        S = sb("S", [ROWS, BLOCKS, F])
        W = sb("W", [ROWS, BLOCKS, F])
        AB = sb("AB", [ROWS, BLOCKS, 2 * HID])
        st1 = sb("st1", [ROWS, BLOCKS])
        st2 = sb("st2", [ROWS, BLOCKS])
        cnt = sb("cnt", [ROWS, BLOCKS])
        rcnt = sb("rcnt", [ROWS, BLOCKS])
        cs = sb("cs", [ROWS, F])
        cm = sb("cm", [ROWS, F])
        amax = sb("amax", [128, 8])
        aall = sb("aall", [128, 8])
        wmax = sb("wmax", [128, 8])
        sc = sb("sc", [128, 16])
        tabA = sb("tabA", [128, 2, BLOCKS, HID], fp16)
        tabB = sb("tabB", [128, 2, BLOCKS, HID], fp16)
        tabH = sb("tabH", [128, 2, BLOCKS, F], fp16)
        dT = sb("dT", [128, 4 * 128])
        accs = sb("accs", [128, SPAN4])

        bc = [[sb(f"bc{s}{b}", [128, EC], fp16) for b in range(2)] for s in "XY"]
        oh = [[sb(f"oh{s}{b}", [128, 2, EC], fp16) for b in range(2)] for s in "XY"]
        gx = [sb(f"gx{b}", [128, GT, F]) for b in range(2)]
        g0 = sb("g0", [128, GT, HID])
        g1 = sb("g1", [128, GT, HID])
        gs = sb("gs", [128, GT, HID])
        h1 = [sb(f"h1{b}", [128, GT * HID + 1]) for b in range(2)]
        tT = [sb(f"tT{b}", [128, 128]) for b in range(2)]
        zr = [sb(f"zr{b}", [128, GT, HID]) for b in range(2)]
        yw = sb("yw", [128, GT, K2, F])
        msg = [sb(f"msg{b}", [128, GT, F]) for b in range(2)]
        parts = [sb(f"parts{b}", [128, GT, 2 * F], fp16) for b in range(2)]
        spread = [sb(f"spread{b}", [128, GT, 128], fp16) for b in range(2)]
        ohm = [sb(f"ohm{b}", [128, GT, SPAN4], fp16) for b in range(2)]

        bank = [ctx.enter_context(nc.psum_tensor(f"bank{i}", [128, 512], fp32)) for i in range(8)]
        acc = bank[4:6]
        ybank = bank[6:8]

        s_idx = sem("idx_loaded")
        s_idx0 = sem("idx_padded")
        s_w0 = sem("weights_cleared")
        s_w = sem("weights_loaded")
        s_iota = sem("iota_made")
        s_const = sem("constants_made")
        s_tab0 = sem("tables_cleared")
        s_lohi = sem("lo_hi_made")
        s_loht = sem("lo_hi_transposed")
        s_stage = sem("lo_hi_staged")
        s_scr = sem("scratch_written")
        s_v = sem("vector_chain")
        s_g = sem("gpsimd_chain")
        s_coh = sem("count_onehots_made")
        s_cmm = sem("count_group_added")
        s_bc = [[sem(f"bc{s}{b}_loaded") for b in range(2)] for s in "XY"]
        s_oh = [sem("ohX_made"), sem("ohY_made")]
        s_gs = sem("sides_added")
        s_gat = sem("gather_banks_full")
        s_red = sem("gather_banks_read")
        s_in = sem("edge_input_made")
        s_tr = sem("edge_input_transposed")
        s_tc = sem("transposed_copied")
        s_z = sem("z_made")
        s_y = sem("y_banks_full")
        s_yr = sem("y_banks_read")
        s_yb = sem("y_bias_copied")
        s_msg = sem("message_made")
        s_hi = sem("part_hi_made")
        s_lo = sem("part_lo_made")
        s_sp = sem("parts_spread")
        s_om = sem("onehot_m_made")
        s_sc = sem("group_scattered")
        s_tab = sem("table_written")
        s_mx = sem("maxima_made")
        s_ma = sem("maxima_reduced")
        s_rx = sem("round_maximum_made")
        s_rt = sem("round_maximum_moved")
        s_di = sem("dense_input_made")
        s_dt = sem("dense_transposed")
        s_dc = sem("dense_copied")
        s_dm = sem("dense_made")
        s_ae = sem("sums_copied")
        s_at = sem("sums_transposed")
        s_var = sem("variance_made")
        s_std = sem("deviation_made")
        s_bn = sem("batch_input_made")
        s_bm = sem("batch_sums_made")
        s_uo = sem("outer_made")
        s_ot = sem("outer_transposed")
        s_oc = sem("outer_copied")
        s_om2 = sem("outer_multiplied")
        s_x = sem("x_made")
        s_out = sem("out_written")

        block = ctx.enter_context(nc.Block())

        PRO = 4

        def skewed(eng, stages):
            top = max(lag for lag, _ in stages)
            for s in range(PRO):
                for lag, stage_of in stages:
                    if s - lag >= 0:
                        stage_of(s - lag, (s - lag) % 2)
            with eng.Fori(0, (NG - PRO) // 2) as i:
                for h in range(2):
                    for lag, stage_of in stages:
                        stage_of(i * 2 + (PRO + h - lag), (h - lag) % 2)
            for s in range(NG, NG + top):
                for lag, stage_of in stages:
                    if s - lag < NG:
                        stage_of(s - lag, (s - lag) % 2)

        def wait_reuse(eng, sm, base, g, per, back=2):
            if isinstance(g, int) and g < back:
                if isinstance(base, int) and base > 0:
                    eng.wait_ge(sm, base * per)
            else:
                eng.wait_ge(sm, (base + g - back + 1) * per)

        L1_BASE, L2_BASE, L3_BASE = ROUNDS * NG, (ROUNDS + 1) * NG, (ROUNDS + 2) * NG
        Y2_BASE = 2 * NG

        s_w_all = [0]

        @block.sync
        def _(eng):
            eng.wait_ge(s_idx0, 2)
            for t, src in zip(idx_i, (dst_in, src_in)):
                eng.dma_start(t[0:FULL, :], src[0:FULL * T].rearrange("(p t) -> p t", t=T)).then_inc(s_idx, 16)
                eng.dma_start(t[FULL:FULL + 1, 0:REST],
                              src[FULL * T:E].rearrange("(p t) -> p t", p=1)).then_inc(s_idx, 16)
            eng.wait_ge(s_w0, 1)

            def load(dst, src):
                eng.dma_start(dst, src).then_inc(s_w, 16)
                s_w_all[0] += 16

            load(X[:, 0:BLOCKS - 1, :], x_in[0:ROWS * (BLOCKS - 1), :].rearrange("(j r) f -> r j f", r=ROWS))
            load(X[0:LAST, BLOCKS - 1, :], x_in[ROWS * (BLOCKS - 1):N, :])
            for name, a in dict(e1=fe_b1, e3=fe_b3, x1=fx_b1, x2=fx_b2, x3=fx_b3, c=c_bias, g=gamma,
                                be=beta, o=b_out).items():
                load(bias[name][:, :], a.rearrange("(z n) -> z n", z=1).broadcast_to([ROWS, a.shape[0]]))
            for j in range(7):
                at = slice(16 * j, 16 * j + F)
                hid = slice(16 * j, 16 * j + HID)
                load(bd_ab[at, j, 0:HID], fe_W1[0:F, :])
                load(bd_ab[at, j, HID:2 * HID], fe_W1[F:2 * F, :])
                load(bd_m[hid, j, :], fe_W3)
                load(bd_x1[at, j, :], fx_W1[0:F, :])
                load(bd_m1[hid, j, :], fx_W1[F:F + HID, :])
                load(bd_2[hid, j, :], fx_W2)
                load(bd_3[hid, j, :], fx_W3)
                load(bd_root[at, j, :], root)
                load(bd_out[at, j, :], w_out)
            for t in range(GT):
                load(bd_e[HID * t:HID * (t + 1), t, :], fe_W2)
                load(bd_e[GT * HID:GT * HID + 1, t, :], fe_b2.rearrange("(z n) -> z n", z=1))
                at = slice(16 * t, 16 * t + F)
                load(bd_y1[at, t, 0:(K1 - 1) * F], enet_w)
                load(bd_y1[at, t, (K1 - 1) * F:K1 * F], enet_b)
                load(bd_y2[at, t, 0:(K2 - 1) * F], k2_w)
                load(bd_y2[at, t, (K2 - 1) * F:K2 * F], k2_b)
            load(wt[:, :, :], w_tp.rearrange("(h p) w -> p h w", p=128))
            for t, src in ((ea4, ea4_in), (ea8, ea8_in)):
                load(t[0:FULL, :, :], src[0:FULL * T, :].rearrange("(p t) k -> p t k", t=T))
                load(t[FULL:FULL + 1, 0:REST, :], src[FULL * T:E, :].rearrange("(p t) k -> p t k", p=1))

            for a in range(4):
                eng.wait_ge(s_stage, 2 * (a + 1))
                if a >= 1:
                    eng.wait_ge(s_scr, 32 * a)
                to = (lo_dram, hi_dram)[a % 2][a // 2]
                st = stage[:, a % 2, :].rearrange("t (c p) -> t c p", p=128)
                eng.dma_start(to[0:768, :].rearrange("(c t) p -> t c p", t=128), st[:, 0:6, :]).then_inc(s_scr, 16)
                eng.dma_start(to[768:T, :], st[0:T - 768, 6, :]).then_inc(s_scr, 16)
            eng.wait_ge(s_scr, 128)

            def loads(base, sides):
                def load_group(g, b):
                    for slot, side in enumerate(sides):
                        wait_reuse(eng, s_oh[slot], base, g, 1)
                        lo = lo_dram[side][bass.ds(g * GT, GT), :].rearrange("(z a) p -> z (a p)", z=1)
                        hi = hi_dram[side][bass.ds(g * GT, GT), :].rearrange("(z a) p -> z (a p)", z=1)
                        eng.dma_start(bc[slot][b][0:ROWS, :], lo.broadcast_to([ROWS, EC])).then_inc(s_bc[slot][b], 16)
                        eng.dma_start(bc[slot][b][ROWS:128, :],
                                      hi.broadcast_to([128 - ROWS, EC])).then_inc(s_bc[slot][b], 16)
                skewed(eng, [(0, load_group)])

            with eng.Fori(0, ROUNDS) as r:
                eng.wait_ge(s_di, r * DENSE_PER_ROUND + 1)
                loads(r * NG, (0, 1))
            loads(L1_BASE, (1,))
            loads(L2_BASE, (0,))
            loads(L3_BASE, (0,))

            eng.wait_ge(s_x, 1)
            eng.dma_start(out[0:ROWS * (BLOCKS - 1), :].rearrange("(j r) f -> r j f", r=ROWS),
                          X[:, 0:BLOCKS - 1, :]).then_inc(s_out, 16)
            eng.dma_start(out[ROWS * (BLOCKS - 1):N, :], X[0:LAST, BLOCKS - 1, :]).then_inc(s_out, 16)
            eng.wait_ge(s_out, 32)

        @block.gpsimd
        def _(eng):
            eng.memset(idx_i[0], PAD_NODE).then_inc(s_idx0, 1)
            eng.memset(idx_i[1], PAD_NODE).then_inc(s_idx0, 1)
            eng.iota(iota_i[:, :], pattern=[[1, SPAN4]], base=0, channel_multiplier=0).then_inc(s_iota, 1)
            eng.iota(part_i[:, :], pattern=[[0, 1]], base=0, channel_multiplier=1).then_inc(s_iota, 1)
            eng.iota(nmask_i[:, :], pattern=[[ROWS, BLOCKS]], base=0, channel_multiplier=1).then_inc(s_iota, 1)
            eng.memset(ident[:, :], 0.0).then_inc(s_g, 1)
            eng.wait_ge(s_g, 1)
            eng.affine_select(out=ident[:, :], in_=ident[:, :], compare_op=ALU.not_equal, fill=1.0, base=0,
                              pattern=[[-1, 128]], channel_multiplier=1).then_inc(s_const, 1)
            tabs = (tabA, tabB, tabH)
            for t in tabs:
                eng.memset(t[:, :, :, :], 0.0).then_inc(s_g, 1)
            eng.wait_ge(s_g, 4)
            for n, t in enumerate(tabs):
                pen = t[:, 0, :, :].rearrange("p (h c) f -> p c h f", c=2)[:, 0, :, :]
                eng.memset(pen, -BIG).then_inc(s_g, 1)
                eng.wait_ge(s_g, 5 + n)
                eng.affine_select(out=pen, in_=pen, compare_op=ALU.not_equal, fill=0.0, base=ROWS,
                                  pattern=[[1, HI], [0, t.shape[3]]], channel_multiplier=-1).then_inc(s_tab0, 1)

            def spreads(base, mask, nq, two_f):
                def spread_group(g, b):
                    eng.wait_ge(s_lo, base + g + 1)
                    wait_reuse(eng, s_sc, base, g, 1)
                    out_ap = spread[b][:, :, 0:nq * two_f].rearrange("p t (q c) -> p t q c", c=two_f)
                    eng.tensor_tensor(
                        out_ap,
                        parts[b][:, :, 0:two_f].unsqueeze(2).broadcast_to([128, GT, nq, two_f]),
                        mask[:, bass.ds(g * GT, GT), :].unsqueeze(3).broadcast_to([128, GT, nq, two_f]),
                        ALU.mult).then_inc(s_sp, 1)
                skewed(eng, [(0, spread_group)])

            eng.wait_ge(s_mx, 1)
            eng.partition_all_reduce(aall[:, :], amax[:, :], 128, bass.bass_isa.ReduceOp.absmax).then_inc(s_ma, 1)
            with eng.Fori(0, ROUNDS) as r:
                spreads(r * NG, q7d, Q7, 2 * HID)
            spreads(L1_BASE, q4d, Q4, 2 * F)
            spreads(L2_BASE, q4s, Q4, 2 * F)
            spreads(L3_BASE, q4s, Q4, 2 * F)

        @block.tensor
        def _(eng):
            eng.wait_ge(s_const, 1)
            for a in range(4):
                eng.wait_ge(s_lohi, 2 * (a // 2) + 2)
                if a >= 2:
                    eng.wait_ge(s_stage, 2 * (a - 1))
                src = (lo_f, hi_f)[a % 2]
                for c in range(7):
                    w = min(128, T - 128 * c)
                    dst = bank[2 * (a % 2) + c // 4][0:w, (c % 4) * 128:(c % 4 + 1) * 128]
                    mm = eng.transpose(dst, src[:, 128 * c:128 * c + w], ident[:, :])
                    if c in (3, 6):
                        mm.then_inc(s_loht, 1)

            def count_group(g, b):
                eng.wait_ge(s_coh, g + 1)
                for t in range(GT):
                    mm = eng.matmul(acc[1][:, 0:BLOCKS], ohm[b][:, t, 0:128], ohm[b][:, t, 128:128 + BLOCKS],
                                    start=isinstance(g, int) and g == 0 and t == 0,
                                    stop=isinstance(g, int) and g == NG - 1 and t == GT - 1)
                mm.then_inc(s_cmm, 1)
            skewed(eng, [(1, count_group)])

            def dense(n, dense_in, w, spare=0):
                eng.wait_ge(s_di, n + (1 + spare))
                for k in range(4):
                    mm = eng.transpose(bank[0][0:112, k * ROWS:(k + 1) * ROWS],
                                       dense_in[:, 7 * k:7 * k + 7, :].rearrange("p j f -> p (j f)"),
                                       ident[0:ROWS, 0:ROWS])
                mm.then_inc(s_dt, 1)
                eng.wait_ge(s_dc, n + 1)
                o = 7 * w.shape[2]
                for k in range(4):
                    mm = eng.matmul(bank[1][0:ROWS, k * o:(k + 1) * o], dT[0:112, k * ROWS:(k + 1) * ROWS],
                                    w[:, :, :].rearrange("p j o -> p (j o)"), start=True, stop=True)
                mm.then_inc(s_dm, 1)

            def sums(n, nq, two_f, blocks):
                eng.wait_ge(s_ae, n + 1)
                for jj in range(blocks):
                    mm = eng.transpose(bank[2 + jj // 4][0:ROWS, (jj % 4) * nq * two_f:(jj % 4 + 1) * nq * two_f],
                                       accs[0:nq * two_f, jj * ROWS:(jj + 1) * ROWS],
                                       ident[0:nq * two_f, 0:nq * two_f])
                mm.then_inc(s_at, 1)

            def gathers(base, tabs, per_bank):
                f = tabs[0].shape[3]
                views = [t[:, :, :, :].rearrange("p k (h c) f -> p k c h f", c=2) for t in tabs]

                def gather_group(g, b):
                    for k in range(4):
                        slot = k // 2 if len(tabs) == 2 else 0
                        if k % 2 == 0:
                            eng.wait_ge(s_oh[slot], base + g + 1)
                        if isinstance(g, int) and g == 0:
                            if k == 0 and isinstance(base, int):
                                eng.wait_ge(s_red, base * 4)
                        else:
                            eng.wait_ge(s_red, (base + g) * 4 + (k - 3))
                        for t in range(per_bank):
                            tile = (k * per_bank + t) % GT
                            for c in range(2):
                                for p in range(2):
                                    mm = eng.matmul(bank[k][:, t * HI * f:(t + 1) * HI * f],
                                                    oh[slot][b][:, c, tile * 128:(tile + 1) * 128],
                                                    views[slot][:, p, c, :, :],
                                                    start=(c == 0 and p == 0), stop=(c == 1 and p == 1))
                        mm.then_inc(s_gat, 1)
                return gather_group

            def scatters(base, m, span):
                def scatter_group(g, b):
                    eng.wait_ge(s_om, base + g + 1)
                    eng.wait_ge(s_sp, base + g + 1)
                    first = isinstance(g, int) and g == 0
                    last = isinstance(g, int) and g == NG - 1
                    for t in range(GT):
                        for a in range(-(-span // SPAN7)):
                            lo, hi = a * SPAN7, min(span, (a + 1) * SPAN7)
                            mm = eng.matmul(acc[a][0:m, 0:hi - lo], spread[b][:, t, 0:m], ohm[b][:, t, lo:hi],
                                            start=first and t == 0, stop=last and t == GT - 1)
                    mm.then_inc(s_sc, 1)
                return scatter_group

            def turns(base, cols, src, ready, per, bank_free):
                def turn_group(g, b):
                    eng.wait_ge(ready, (base + g + 1) * per)
                    bank_free(g)
                    eng.transpose(ybank[b][0:cols, 384:512], src(b), ident[:, :]).then_inc(s_tr, 1)
                return turn_group

            def z_read(base):
                return lambda g: wait_reuse(eng, s_hi, base, g, 1)

            def y_read(ybase, n):
                def free(g):
                    if ybase or not (isinstance(g, int) and g == 0):
                        eng.wait_ge(s_yr, g * n + ybase)
                return free

            def z_of(base):
                def z_group(g, b):
                    eng.wait_ge(s_tc, base + g + 1)
                    wait_reuse(eng, s_hi, base, g, 1)
                    k = GT * HID
                    eng.matmul(ybank[b][:, 0:k], tT[b][0:k + 1, :],
                               bd_e[0:k + 1, :, :].rearrange("p t o -> p (t o)"),
                               start=True, stop=True).then_inc(s_z, 1)
                return z_group

            def y_of(base, ybase, w, k, per):
                def y_group(g, b):
                    eng.wait_ge(s_tc, base + g + 1)
                    n = GT // per
                    for c in range(n):
                        at = g * n + c
                        if c >= 2:
                            eng.wait_ge(s_yr, at + (ybase - 1))
                        eng.matmul(ybank[c % 2][:, 0:per * k * F], tT[b][:, :],
                                   w[:, c * per:(c + 1) * per, :].rearrange("p t o -> p (t o)"),
                                   start=True, stop=True).then_inc(s_y, 1)
                return y_group

            def edge_pass(base, tabs, per_bank, m, span, middle):
                stages = [(0, gathers(base, tabs, per_bank))]
                if middle:
                    stages.append((1, middle[0]))
                stages.append((3, scatters(base, m, span)))
                if middle:
                    stages.append((1, middle[1]))
                skewed(eng, stages)

            eng.wait_ge(s_w, s_w_all[0])
            with eng.Fori(0, ROUNDS) as r:
                d = r * DENSE_PER_ROUND
                dense(d, Hn, bd_ab)
                eng.wait_ge(s_rx, r * 2 + 1)
                eng.transpose(bank[2][0:1, 0:128], amax[:, 0:1], ident[:, :]).then_inc(s_rt, 1)
                eng.wait_ge(s_rx, r * 2 + 2)
                eng.matmul(bank[2][:, 128:129], ones[0:1, :], top1[:, :], start=True, stop=True).then_inc(s_rt, 1)
                eng.wait_ge(s_tab, r + 1)
                edge_pass(r * NG, (tabA, tabB), 4, Q7 * 2 * HID, SPAN7,
                          (turns(r * NG, GT * HID + 1, lambda b: h1[b][:, :], s_in, 1, z_read(r * NG)), z_of(r * NG)))
                sums(r, Q7, 2 * HID, BLOCKS // Q7)
                dense(d + 1, S, bd_m)
                dense(d + 2, Hn, bd_x1)
                dense(d + 3, U, bd_m1)
                dense(d + 4, V, bd_2)
                dense(d + 5, U, bd_3)
            nd = ROUNDS * DENSE_PER_ROUND
            turn16 = lambda b: gx[b][:, :, :].rearrange("p t f -> p (t f)")
            eng.wait_ge(s_tab, ROUNDS + 1)
            edge_pass(L1_BASE, (tabH,), 2, Q4 * 2 * F, SPAN4,
                      (turns(L1_BASE, 128, turn16, s_red, 4, y_read(0, 2)), y_of(L1_BASE, 0, bd_y1, K1, 4)))
            sums(ROUNDS, Q4, 2 * F, BLOCKS // Q4)
            dense(nd, Hn, bd_root, 1)
            for k in range(2):
                eng.wait_ge(s_bn, k + 1)
                eng.matmul(bank[1][0:ROWS, 0:F], ones[0:ROWS, 0:ROWS], cs[:, :], start=True, stop=True).then_inc(s_bm, 1)
            eng.wait_ge(s_tab, ROUNDS + 2)
            edge_pass(L2_BASE, (tabH,), 2, Q4 * 2 * F, SPAN4,
                      (turns(L2_BASE, 128, turn16, s_red, 4, y_read(Y2_BASE, 4)), y_of(L2_BASE, Y2_BASE, bd_y2, K2, 2)))
            sums(ROUNDS + 1, Q4, 2 * F, BLOCKS // Q4)
            eng.wait_ge(s_tab, ROUNDS + 3)
            edge_pass(L3_BASE, (tabH,), 2, Q4 * 2 * F, SPAN4, None)
            sums(ROUNDS + 2, Q4, 2 * F, BLOCKS // Q4)
            eng.wait_ge(s_uo, 1)
            of = outer.rearrange("p j u v -> p j (u v)")
            for k in range(HI + 1):
                if k < HI:
                    if k >= 2:
                        eng.wait_ge(s_oc, k - 1)
                    for c in range(4):
                        mm = eng.transpose(bank[k % 2][:, c * ROWS:(c + 1) * ROWS],
                                           of[:, 2 * k + c // 2, (c % 2) * 128:(c % 2 + 1) * 128],
                                           ident[0:ROWS, 0:ROWS])
                    mm.then_inc(s_ot, 1)
                if k >= 1:
                    eng.wait_ge(s_oc, k)
                    for c in range(2):
                        j = 2 * (k - 1) + c
                        for half in range(2):
                            at = (2 * c + half) * ROWS
                            mm = eng.matmul(bank[4][0:ROWS, j * F:(j + 1) * F], (dT, accs)[(k - 1) % 2][:, at:at + ROWS],
                                            wt[:, half, :], start=half == 0, stop=half == 1)
                    mm.then_inc(s_om2, 1)
            dense(nd + 1, U, bd_out, 1)

        @block.scalar
        def _(eng):
            for a in range(4):
                for h in range(2):
                    eng.wait_ge(s_loht, 2 * a + h + 1)
                    if a >= 2 and h == 0:
                        eng.wait_ge(s_scr, 32 * (a - 1))
                    w, rows = ((512, 128), (256, 128))[h]
                    copied = eng.activation(stage[0:rows, a % 2, 512 * h:512 * h + w],
                                            bank[2 * (a % 2) + h][0:rows, 0:w], ACT.Copy)
                    if h:
                        copied = eng.activation(stage[0:T - 768, a % 2, 768:896],
                                                bank[2 * (a % 2) + h][0:T - 768, 256:384], ACT.Copy)
                    copied.then_inc(s_stage, 1)

            def dense(n):
                eng.wait_ge(s_dt, n + 1)
                eng.activation(dT[0:112, 0:4 * ROWS], bank[0][0:112, 0:4 * ROWS], ACT.Copy).then_inc(s_dc, 1)

            def sums(n, done, m, span):
                eng.wait_ge(s_sc, done)
                if span == SPAN7:
                    eng.activation(accs[0:m, 0:span], acc[0][0:m, 0:span], ACT.Copy).then_inc(s_ae, 1)
                else:
                    eng.activation(accs[0:m, 0:SPAN7], acc[0][0:m, 0:SPAN7], ACT.Copy)
                    eng.activation(accs[0:m, SPAN7:span], acc[1][0:m, 0:span - SPAN7], ACT.Copy).then_inc(s_ae, 1)

            def root_of(n, view):
                eng.wait_ge(s_var, n + 1)
                eng.activation(view, view, ACT.Sqrt, bias=eps_t[0:ROWS, :], scale=1.0).then_inc(s_std, 1)

            def turned(base, cols, reader, rbase, per):
                def copy_group(g, b):
                    eng.wait_ge(s_tr, base + g + 1)
                    wait_reuse(eng, reader, rbase, g, per)
                    eng.activation(tT[b][0:cols, :], ybank[b][0:cols, 384:512], ACT.Copy).then_inc(s_tc, 1)
                return copy_group

            def z_parts(base):
                def parts_group(g, b):
                    eng.wait_ge(s_z, base + g + 1)
                    wait_reuse(eng, s_sp, base, g, 1)
                    z = ybank[b][:, 0:GT * HID].rearrange("p (t f) -> p t f", f=HID)
                    eng.activation(zr[b][:, :, :], z, ACT.Relu, scale=sc[:, 2:3])
                    eng.activation(parts[b][:, :, 0:HID], z, ACT.Relu, scale=sc[:, 2:3]).then_inc(s_hi, 1)
                return parts_group

            def y_bias(ybase, k, per):
                def bias_group(g, b):
                    n = GT // per
                    for c in range(n):
                        at = g * n + c
                        eng.wait_ge(s_y, at + (ybase + 1))
                        if not (isinstance(g, int) and g == 0):
                            eng.wait_ge(s_msg, g + (ybase // 2))
                        elif ybase:
                            eng.wait_ge(s_msg, ybase // 2)
                        y = ybank[c % 2][:, 0:per * k * F].rearrange("p (t k o) -> p t k o", k=k, o=F)
                        eng.activation(yw[:, c * per:(c + 1) * per, k - 1, :], y[:, :, k - 1, :],
                                       ACT.Copy).then_inc(s_yb, 1)
                return bias_group

            def hi_parts(base, src, ready, rbase, per, scale):
                def hi_group(g, b):
                    eng.wait_ge(ready, (rbase + g + 1) * per)
                    wait_reuse(eng, s_sp, base, g, 1)
                    eng.activation(parts[b][:, :, 0:F], src[b][:, :, :], ACT.Copy, scale=scale).then_inc(s_hi, 1)
                return hi_group

            root_of(0, st2[:, :])
            with eng.Fori(0, ROUNDS) as r:
                dense(r * DENSE_PER_ROUND)
                skewed(eng, [(0, turned(r * NG, GT * HID + 1, s_z, r * NG, 1)), (0, z_parts(r * NG))])
                sums(r, (r + 1) * NG, Q7 * 2 * HID, SPAN7)
                for c in range(1, DENSE_PER_ROUND):
                    dense(r * DENSE_PER_ROUND + c)
            nd = ROUNDS * DENSE_PER_ROUND
            root_of(1, st2[:, :])
            skewed(eng, [(0, turned(L1_BASE, 128, s_y, 0, 2)), (0, y_bias(0, K1, 4)),
                         (0, hi_parts(L1_BASE, msg, s_msg, 0, 1, sc[:, 4:5]))])
            sums(ROUNDS, L1_BASE + NG, 128, SPAN4)
            dense(nd)
            root_of(2, cm[:, :])
            root_of(3, st2[:, :])
            skewed(eng, [(0, turned(L2_BASE, 128, s_y, Y2_BASE // 4, 4)), (0, y_bias(Y2_BASE, K2, 2)),
                         (0, hi_parts(L2_BASE, msg, s_msg, NG, 1, sc[:, 6:7]))])
            sums(ROUNDS + 1, L2_BASE + NG, 128, SPAN4)
            root_of(4, st2[:, :])
            skewed(eng, [(0, hi_parts(L3_BASE, gx, s_red, L3_BASE, 4, 1.0))])
            sums(ROUNDS + 2, L3_BASE + NG, 128, SPAN4)
            for k in range(HI):
                eng.wait_ge(s_ot, k + 1)
                if k >= 2:
                    eng.wait_ge(s_om2, k - 1)
                eng.activation((dT, accs)[k % 2][:, 0:4 * ROWS], bank[k % 2][:, 0:4 * ROWS], ACT.Copy).then_inc(s_oc, 1)
            dense(nd + 1)

        @block.vector
        def _(eng):
            chained = [0]
            chain_base = [0]

            def link(ins):
                chained[0] += 1
                ins.then_inc(s_v, 1)
                eng.wait_ge(s_v, chain_base[0] + chained[0])

            def bcj(v):
                return v[:, :].unsqueeze(2).broadcast_to([ROWS, BLOCKS, F])

            def bcf(v, f=F):
                return v[:, 0:f].unsqueeze(1).broadcast_to([ROWS, BLOCKS, f])

            for t in (bd_ab, bd_m, bd_x1, bd_m1, bd_2, bd_3, bd_root, bd_out, bd_e, bd_y1, bd_y2, X, U, V, S):
                eng.memset(t[:, :, :], 0.0)
            for t in (ea4, ea8):
                eng.memset(t[96:128, :, :], 0.0)
            for b in range(2):
                eng.memset(h1[b][:, GT * HID:GT * HID + 1], 1.0)
            eng.memset(ones[:, :], 1.0)
            eng.memset(eps_t[:, :], EPS)
            eng.memset(amax[:, :], 0.0).then_inc(s_w0, 1)

            eng.wait_ge(s_iota, 3)
            eng.tensor_copy(iota_m[:, :], iota_i[:, :])
            eng.tensor_copy(iota_f[:, :], iota_i[:, 0:128])
            eng.tensor_scalar(nmask[:, :], nmask_i[:, :], float(N), None, ALU.is_lt)
            link(eng.tensor_copy(part_f[:, :], part_i[:, :]))
            link(eng.tensor_scalar(past[:, :], part_f[:, :], float(ROWS), None, ALU.is_ge))
            link(eng.scalar_tensor_tensor(pv[:, 0:1], past[:, :], -float(ROWS), part_f[:, :], ALU.mult, ALU.add))
            link(eng.tensor_scalar(past[:, :], past[:, :], -float(ROWS), float(ROWS), ALU.mult, ALU.add))
            link(eng.tensor_tensor(pv[:, 1:2], past[:, :], pv[:, 0:1], ALU.add))

            ROUND = 1.5 * 2.0 ** 23

            def split(n, width, q, m):
                link(eng.tensor_scalar(q, n, 1.0 / width, 0.5 / width - 0.5, ALU.mult, ALU.add))
                link(eng.tensor_scalar(q, q, ROUND, -ROUND, ALU.add, ALU.add))
                return eng.scalar_tensor_tensor(m, q, -float(width), n, ALU.mult, ALU.add)

            def mask_of(out_ap, q, n):
                return eng.tensor_tensor(out_ap, q.unsqueeze(2).broadcast_to([128, T, n]),
                                         iota_f[:, 0:n].unsqueeze(1).broadcast_to([128, T, n]), ALU.is_equal)

            eng.wait_ge(s_idx, 64)
            for side in range(2):
                link(eng.tensor_copy(idx_f[side], idx_i[side]))
                if side:
                    eng.wait_ge(s_loht, 4)
                split(idx_f[side], 2 * ROWS, hi_f, lo_f).then_inc(s_lohi, 2)
                if side == 0:
                    link(split(idx_f[0], SPAN7, qf, m7d[:, :]))
                    link(mask_of(q7d[:, :, :], qf, Q7))
                    split(idx_f[0], ROWS, jd[:, :], rd[:, :])
                link(split(idx_f[side], SPAN4, qf, (m4d, m4s)[side][:, :]))
                link(mask_of((q4d, q4s)[side][:, :, :], qf, Q4))

            def count_group(g, b):
                wait_reuse(eng, s_cmm, 0, g, 1)
                for t in range(GT):
                    eng.tensor_scalar(ohm[b][:, t, 0:128], iota_m[:, 0:128], rd[:, bass.ds(g * GT + t, 1)], None,
                                      ALU.is_equal)
                eng.tensor_tensor(ohm[b][:, :, 128:128 + BLOCKS],
                                  jd[:, bass.ds(g * GT, GT)].unsqueeze(2).broadcast_to([128, GT, BLOCKS]),
                                  iota_f[:, 0:BLOCKS].unsqueeze(1).broadcast_to([128, GT, BLOCKS]),
                                  ALU.is_equal).then_inc(s_coh, 1)
            skewed(eng, [(0, count_group)])
            eng.wait_ge(s_cmm, NG)
            link(eng.tensor_copy(cnt[:, :], acc[1][0:ROWS, 0:BLOCKS]))
            link(eng.tensor_scalar(rcnt[:, :], cnt[:, :], 1.0, None, ALU.max))
            link(eng.reciprocal(rcnt[:, :], rcnt[:, :]))

            eng.wait_ge(s_w, s_w_all[0])
            for c, t in ((0, bd_e), (1, bd_y1), (2, bd_y2), (3, ea4), (4, ea8)):
                ins = eng.tensor_reduce(amax[:, c:c + 1], t[:, :, :], AX.XY, ALU.max, apply_absolute_value=True)
            ins.then_inc(s_mx, 1)
            eng.wait_ge(s_ma, 1)
            link(eng.tensor_copy(wmax[:, :], aall[:, :]))
            link(eng.memset(amax[:, :], 0.0))

            def power(at, src, top, more=1.0):
                s, inv = sc[:, at:at + 1], sc[:, at + 1:at + 2]
                link(eng.tensor_scalar(inv, src, 2.0 ** -60, None, ALU.max))
                link(eng.tensor_scalar(inv.bitcast(i32), inv.bitcast(i32), 0x7F800000, None, ALU.bitwise_and))
                link(eng.reciprocal(s, inv))
                link(eng.tensor_scalar(s, s, top, None, ALU.mult))
                link(eng.tensor_scalar(inv, inv, more / top, None, ALU.mult))

            for at, w, e, k in ((4, 1, 3, K1), (6, 2, 4, K2)):
                link(eng.tensor_scalar(wmax[:, e:e + 1], wmax[:, e:e + 1], 1.0, F * 4.0 * k * H_SCALE, ALU.max,
                                       ALU.mult))
                link(eng.tensor_tensor(wmax[:, e:e + 1], wmax[:, e:e + 1], wmax[:, w:w + 1], ALU.mult))
                power(at, wmax[:, e:e + 1], PART_TOP, 1.0 / H_SCALE)

            norms = [0]

            def norm():
                link(eng.tensor_reduce(st1[:, :], X[:, :, :], AX.X, ALU.add))
                link(eng.tensor_scalar(st1[:, :], st1[:, :], 1.0 / F, None, ALU.mult))
                link(eng.tensor_tensor(Hn[:, :, :], X[:, :, :], bcj(st1), ALU.subtract))
                link(eng.tensor_tensor(W[:, :, :], Hn[:, :, :], Hn[:, :, :], ALU.mult))
                link(eng.tensor_reduce(st2[:, :], W[:, :, :], AX.X, ALU.add))
                eng.tensor_scalar(st2[:, :], st2[:, :], 1.0 / F, None, ALU.mult).then_inc(s_var, 1)
                norms[0] += 1
                eng.wait_ge(s_std, norms[0])
                link(eng.reciprocal(st2[:, :], st2[:, :]))
                link(eng.tensor_tensor(Hn[:, :, :], Hn[:, :, :], bcj(st2), ALU.mult))
                return eng.tensor_scalar(Hn[:, :, :], Hn[:, :, :], 0.0, None, ALU.max)

            def table(tab, src, scale):
                link(eng.tensor_scalar(tab[0:ROWS, 0, :, :], src, scale, None, ALU.mult))
                return eng.scalar_tensor_tensor(tab[0:ROWS, 1, :, :], src, scale, tab[0:ROWS, 0, :, :],
                                                ALU.mult, ALU.subtract)

            def onehots(base, sides):
                def onehot_group(g, b):
                    for slot in range(len(sides)):
                        eng.wait_ge(s_bc[slot][b], (base + g + (2 - b)) * 16)
                        if slot == 0:
                            wait_reuse(eng, s_gat, base, g, 4)
                        for c in range(2):
                            ins = eng.tensor_scalar(oh[slot][b][:, c, :], bc[slot][b][:, :], pv[:, c:c + 1], None,
                                                    ALU.is_equal)
                        ins.then_inc(s_oh[slot], 1)
                return onehot_group

            def select(k, dst, per, f, base, g):
                eng.wait_ge(s_gat, (base + g) * 4 + (k + 1))
                view = bank[k][:, 0:per * HI * f].rearrange("p (t h f) -> p t f h", h=HI, f=f)
                eng.tensor_reduce(dst, view, AX.X, ALU.max).then_inc(s_red, 1)

            def select9(base):
                def select_group(g, b):
                    for k in range(4):
                        select(k, (g0, g1)[k // 2][:, (k % 2) * 4:(k % 2) * 4 + 4, :], 4, HID, base, g)
                    eng.wait_ge(s_red, (base + g) * 4 + 4)
                    eng.tensor_tensor(gs[:, :, :], g0[:, :, :], g1[:, :, :], ALU.add).then_inc(s_gs, 1)
                    eng.wait_ge(s_gs, base + g + 1)
                    wait_reuse(eng, s_tr, base, g, 1)
                    eng.tensor_scalar(h1[b][:, 0:GT * HID], gs[:, :, :].rearrange("p t f -> p (t f)"), 0.0,
                                      sc[:, 1:2], ALU.max, ALU.mult).then_inc(s_in, 1)
                return select_group

            def select16(base, reader):
                def select_group(g, b):
                    wait_reuse(eng, reader, base, g, 1)
                    for k in range(4):
                        select(k, gx[b][:, 2 * k:2 * k + 2, :], 2, F, base, g)
                return select_group

            def message(base, ybase, mbase, ea, k, per):
                def message_group(g, b):
                    n = GT // per
                    wait_reuse(eng, s_hi, base, g, 1)
                    for c in range(n):
                        eng.wait_ge(s_yb, g * n + (c + ybase + 1))
                        y = ybank[c % 2][:, 0:per * k * F].rearrange("p (t k o) -> p t k o", k=k, o=F)
                        e = ea[:, bass.ds(g * GT + c * per, per), :].unsqueeze(3)
                        eng.tensor_tensor(yw[:, c * per:(c + 1) * per, 0:k - 1, :], y[:, :, 0:k - 1, :],
                                          e.broadcast_to([128, per, k - 1, F]), ALU.mult).then_inc(s_yr, 1)
                    eng.wait_ge(s_yr, g * n + (n + ybase))
                    eng.tensor_reduce(msg[b][:, :, :], yw[:, :, 0:k, :].rearrange("p t k o -> p t o k"), AX.X,
                                      ALU.add).then_inc(s_msg, 1)
                return message_group

            def low9(base):
                def low_group(g, b):
                    eng.wait_ge(s_hi, base + g + 1)
                    eng.tensor_tensor(parts[b][:, :, HID:2 * HID], zr[b][:, :, :], parts[b][:, :, 0:HID],
                                      ALU.subtract).then_inc(s_lo, 1)
                return low_group

            def low16(base, src, scale):
                def low_group(g, b):
                    eng.wait_ge(s_hi, base + g + 1)
                    eng.scalar_tensor_tensor(parts[b][:, :, F:2 * F], src[b][:, :, :], scale,
                                             parts[b][:, :, 0:F], ALU.mult, ALU.subtract).then_inc(s_lo, 1)
                return low_group

            def onehot_m(base, m, span):
                def onehot_group(g, b):
                    wait_reuse(eng, s_sc, base, g, 1)
                    for t in range(GT):
                        ins = eng.tensor_scalar(ohm[b][:, t, 0:span], iota_m[:, 0:span],
                                                m[:, bass.ds(g * GT + t, 1)], None, ALU.is_equal)
                    ins.then_inc(s_om, 1)
                return onehot_group

            def sums(nq, f, inv):
                blocks = BLOCKS // nq
                to = S[:, :, :].rearrange("p (q j) f -> p j q f", j=blocks)
                tmp = W[:, :, :].rearrange("p (q j) f -> p j q f", j=blocks)
                for k in range(0, blocks, 4):
                    n = min(4, blocks - k)
                    d = bank[2 + k // 4][0:ROWS, 0:n * nq * 2 * f].rearrange("p (j q s f) -> p j q s f", q=nq,
                                                                             s=2, f=f)
                    for j in range(n):
                        ins = eng.tensor_scalar(tmp[:, k + j, :, 0:f], d[:, j, :, 0, :], inv, None, ALU.mult)
                    link(ins)
                    for j in range(n):
                        ins = eng.scalar_tensor_tensor(to[:, k + j, :, 0:f], d[:, j, :, 1, :], inv,
                                                       tmp[:, k + j, :, 0:f], ALU.mult, ALU.add)
                return ins

            def made(f):
                return bank[1][0:ROWS, 0:BLOCKS * f].rearrange("p (j f) -> p j f", f=f)

            norm().then_inc(s_di, 1)
            before = chained[0]
            LINKS = 19
            with eng.Fori(0, ROUNDS) as r:
                chained[0] = 0
                chain_base[0] = r * LINKS + before
                d = r * DENSE_PER_ROUND
                eng.wait_ge(s_dm, d + 1)
                eng.tensor_tensor(AB[:, :, 0:HID], made(2 * HID)[:, :, 0:HID], bcf(bias["e1"], HID), ALU.add)
                link(eng.tensor_copy(AB[:, :, HID:2 * HID], made(2 * HID)[:, :, HID:2 * HID]))
                eng.tensor_reduce(amax[0:ROWS, 0:1], AB[:, :, :], AX.XY, ALU.max,
                                  apply_absolute_value=True).then_inc(s_rx, 1)
                eng.wait_ge(s_rt, r * 2 + 1)
                eng.tensor_reduce(top1[:, :], bank[2][0:1, 0:128], AX.X, ALU.max).then_inc(s_rx, 1)
                eng.wait_ge(s_rt, r * 2 + 2)
                power(0, bank[2][:, 128:129], TABLE_TOP)
                link(eng.tensor_scalar(sc[:, 8:9], sc[:, 1:2], 4.0 * HID * TABLE_TOP, 1.0, ALU.mult, ALU.add))
                link(eng.tensor_tensor(sc[:, 8:9], sc[:, 8:9], wmax[:, 0:1], ALU.mult))
                power(2, sc[:, 8:9], PART_TOP)
                table(tabA, AB[:, :, 0:HID], sc[0:ROWS, 0:1])
                table(tabB, AB[:, :, HID:2 * HID], sc[0:ROWS, 0:1]).then_inc(s_tab, 1)
                skewed(eng, [(0, onehots(r * NG, (0, 1))), (1, select9(r * NG)), (2, low9(r * NG)),
                             (2, onehot_m(r * NG, m7d, SPAN7))])
                eng.wait_ge(s_at, r + 1)
                sums(Q7, HID, sc[0:ROWS, 3:4]).then_inc(s_di, 1)
                link(eng.tensor_tensor(AB[:, :, 0:HID], cnt[:, :].unsqueeze(2).broadcast_to([ROWS, BLOCKS, HID]),
                                       bcf(bias["e3"], HID), ALU.mult))
                eng.wait_ge(s_dm, d + 2)
                eng.tensor_tensor(U[:, :, 0:HID], made(HID), AB[:, :, 0:HID], ALU.add).then_inc(s_di, 1)
                eng.wait_ge(s_dm, d + 3)
                eng.tensor_tensor(V[:, :, 0:HID], made(HID), bcf(bias["x1"], HID), ALU.add).then_inc(s_di, 1)
                eng.wait_ge(s_dm, d + 4)
                eng.wait_ge(s_di, d + 4)
                link(eng.tensor_tensor(V[:, :, 0:HID], made(HID), V[:, :, 0:HID], ALU.add))
                eng.tensor_scalar(V[:, :, 0:HID], V[:, :, 0:HID], 0.0, None, ALU.max).then_inc(s_di, 1)
                eng.wait_ge(s_dm, d + 5)
                link(eng.tensor_tensor(U[:, :, 0:HID], made(HID), bcf(bias["x2"], HID), ALU.add))
                eng.tensor_scalar(U[:, :, 0:HID], U[:, :, 0:HID], 0.0, None, ALU.max).then_inc(s_di, 1)
                eng.wait_ge(s_dm, d + 6)
                eng.tensor_tensor(Hn[:, :, :], made(F), bcf(bias["x3"]), ALU.add).then_inc(s_di, 1)
                assert chained[0] == LINKS, chained
            chained[0] = before + ROUNDS * LINKS
            chain_base[0] = 0
            nd = ROUNDS * DENSE_PER_ROUND

            eng.wait_ge(s_di, nd + 1)
            link(eng.tensor_tensor(X[:, :, :], X[:, :, :], Hn[:, :, :], ALU.add))
            link(norm())
            table(tabH, Hn[:, :, :], H_SCALE).then_inc(s_tab, 1)
            skewed(eng, [(0, onehots(L1_BASE, (1,))), (2, message(L1_BASE, 0, 0, ea4, K1, 4)),
                         (1, select16(L1_BASE, s_tr)), (2, low16(L1_BASE, msg, sc[:, 4:5])),
                         (2, onehot_m(L1_BASE, m4d, SPAN4))])
            eng.wait_ge(s_at, ROUNDS + 1)
            link(sums(Q4, F, sc[0:ROWS, 5:6]))
            link(eng.tensor_tensor(W[:, :, :], S[:, :, :], bcj(rcnt), ALU.mult))
            link(eng.tensor_tensor(W[:, :, :], W[:, :, :], bcf(bias["c"]), ALU.add))
            eng.tensor_copy(U[:, :, :], W[:, :, :]).then_inc(s_di, 1)
            eng.wait_ge(s_dm, nd + 1)
            link(eng.tensor_tensor(W[:, :, :], made(F), W[:, :, :], ALU.add))
            for k in range(2):
                if k:
                    link(eng.tensor_tensor(U[:, :, :], W[:, :, :], W[:, :, :], ALU.mult))
                link(eng.tensor_tensor(U[:, :, :], (W, U)[k][:, :, :], bcj(nmask), ALU.mult))
                eng.tensor_reduce(cs[:, :], U[:, :, :].rearrange("p j f -> p f j"), AX.X, ALU.add).then_inc(s_bn, 1)
                eng.wait_ge(s_bm, k + 1)
                ins = eng.tensor_scalar(cm[:, :], bank[1][0:ROWS, 0:F], 1.0 / N, None, ALU.mult)
                if k == 0:
                    link(ins)
                    link(eng.tensor_tensor(W[:, :, :], W[:, :, :], bcf(cm), ALU.subtract))
                else:
                    ins.then_inc(s_var, 1)
            norms[0] += 1
            eng.wait_ge(s_std, norms[0])
            link(eng.reciprocal(cm[:, :], cm[:, :]))
            link(eng.tensor_tensor(cm[:, :], cm[:, :], bias["g"][:, :], ALU.mult))
            link(eng.tensor_tensor(W[:, :, :], W[:, :, :], bcf(cm), ALU.mult))
            link(eng.tensor_tensor(W[:, :, :], W[:, :, :], bcf(bias["be"]), ALU.add))
            link(eng.scalar_tensor_tensor(W[:, :, :], W[:, :, :], 0.01, W[:, :, :], ALU.mult, ALU.max))
            link(eng.tensor_tensor(X[:, :, :], X[:, :, :], W[:, :, :], ALU.add))

            link(norm())
            table(tabH, Hn[:, :, :], H_SCALE).then_inc(s_tab, 1)
            skewed(eng, [(0, onehots(L2_BASE, (0,))), (2, message(L2_BASE, Y2_BASE, NG, ea8, K2, 2)),
                         (1, select16(L2_BASE, s_tr)), (2, low16(L2_BASE, msg, sc[:, 6:7])),
                         (2, onehot_m(L2_BASE, m4s, SPAN4))])
            eng.wait_ge(s_at, ROUNDS + 2)
            link(sums(Q4, F, sc[0:ROWS, 7:8]))
            link(eng.tensor_tensor(X[:, :, :], X[:, :, :], S[:, :, :], ALU.add))

            link(norm())
            table(tabH, Hn[:, :, :], H_SCALE).then_inc(s_tab, 1)
            skewed(eng, [(0, onehots(L3_BASE, (0,))), (1, select16(L3_BASE, s_lo)),
                         (2, low16(L3_BASE, gx, 1.0)), (2, onehot_m(L3_BASE, m4s, SPAN4))])
            eng.wait_ge(s_at, ROUNDS + 3)
            link(sums(Q4, F, 1.0 / H_SCALE))
            for j in range(BLOCKS):
                ins = eng.tensor_tensor(outer[:, j, :, :], Hn[:, j, :].unsqueeze(2).broadcast_to([ROWS, F, F]),
                                        S[:, j, :].unsqueeze(1).broadcast_to([ROWS, F, F]), ALU.mult)
            ins.then_inc(s_uo, 1)
            eng.wait_ge(s_om2, HI)
            eng.tensor_copy(U[:, :, :], bank[4][0:ROWS, 0:BLOCKS * F].rearrange("p (j f) -> p j f", f=F)) \
               .then_inc(s_di, 1)
            eng.wait_ge(s_dm, nd + 2)
            link(eng.tensor_tensor(X[:, :, :], made(F), X[:, :, :], ALU.add))
            eng.tensor_tensor(X[:, :, :], X[:, :, :], bcf(bias["o"]), ALU.add).then_inc(s_x, 1)


def kernel(**a):
    import numpy as np
    import concourse.bacc as bacc
    from concourse import mybir as mb
    from concourse.bass_utils import run_bass_kernel_spmd as run

    g = lambda name: np.asarray(a[name])
    f = a["x"].shape[1]
    k1, k2 = a["edge_attr_4"].shape[1], a["edge_attr_8"].shape[1]
    arrays = [g("x"), g("src"), g("dst"), g("edge_attr_4"), g("edge_attr_8")]
    arrays += [g("L0_gnn_" + n) for n in ("fe_W1", "fe_b1", "fe_W2", "fe_b2", "fe_W3", "fe_b3",
                                          "fx_W1", "fx_b1", "fx_W2", "fx_b2", "fx_W3", "fx_b3")]
    arrays += [g("L1_gnn_enet_w").reshape(f, f, k1).transpose(0, 2, 1).reshape(f, k1 * f),
               g("L1_gnn_enet_b").reshape(f, f), g("L1_gnn_root"), g("L1_gnn_bias"), g("L1_gnn_gamma"),
               g("L1_gnn_beta"),
               g("L2_gnn_kernel").reshape(k2, f, f).transpose(2, 0, 1).reshape(f, k2 * f),
               g("L2_gnn_bias").reshape(f, f).T,
               g("L3_gnn_W_tp").reshape(f * f, f), g("L3_gnn_weight").T, g("L3_gnn_bias")]
    nc = bacc.Bacc("TRN2", target_bir_lowering=False, num_devices=1)
    feed, args = {}, []
    for i, v in enumerate(arrays):
        v = np.ascontiguousarray(v)
        feed[f"in_{i}"] = v
        args.append(nc.dram_tensor(f"in_{i}", v.shape, mb.dt.from_np(v.dtype), kind="ExternalInput").ap())
    o = nc.dram_tensor("out_x", a["x"].shape, mb.dt.float32, kind="ExternalOutput").ap()
    gnn_program(nc, *args, o)
    r = run(nc, [feed], core_ids=[0])
    return r.results[0]["out_x"]
```

```python
import concourse.bass as bass
from concourse import mybir
from contextlib import ExitStack


def gnn_program(
    nc: bass.Bass,
    x_in, src_in, dst_in, ea4_in, ea8_in,
    fe_W1, fe_b1, fe_W2, fe_b2, fe_W3, fe_b3,
    fx_W1, fx_b1, fx_W2, fx_b2, fx_W3, fx_b3,
    enet_w, enet_b, root, c_bias, gamma, beta,
    k2_w, k2_b, w_tp, w_out, b_out,
    out,
):
    fp32, fp16, i32 = mybir.dt.float32, mybir.dt.float16, mybir.dt.int32
    ALU = mybir.AluOpType
    ACT = mybir.ActivationFunctionType
    AX = mybir.AxisListType

    N, F = x_in.shape
    E = src_in.shape[0]
    HID = fe_W2.shape[0]
    ROWS, BLOCKS = 114, 28
    LAST = N - ROWS * (BLOCKS - 1)
    HI = BLOCKS // 2
    GT = 8
    ND = 4
    NP = GT - ND
    T = 816
    NG = T // GT
    EC = GT * 128
    FULL = E // EC
    REST_P = (E - FULL * EC) // GT
    REST_T = (E - FULL * EC) % GT
    WIN = 128
    WIDTH = ROWS * BLOCKS
    PAD_NODE = 4000
    BIG = 32768.0
    TABLE_TOP = 4096.0
    H_SCALE = 2048.0
    PART_TOP = 16384.0
    EPS = 1e-5
    Q7, Q4 = 7, 4
    SPAN7, SPAN4 = ROWS * BLOCKS // Q7, ROWS * BLOCKS // Q4
    K1, K2 = ea4_in.shape[1] + 1, ea8_in.shape[1] + 1
    ROUNDS = 3
    DENSE_PER_ROUND = 6
    assert N <= WIDTH < PAD_NODE - WIN and E <= 128 * T and REST_T and NG % 2 == 0

    def dram(name, shape, dt):
        return nc.dram_tensor(name, shape, dt, kind="Internal").ap()

    lo_dram = [dram("lo_dst", [T, 128], fp16), dram("lo_src", [T, 128], fp16)]
    hi_dram = [dram("hi_dst", [T, 128], fp16), dram("hi_src", [T, 128], fp16)]
    rel_dram = dram("rel_dst", [T, 128], fp16)
    scratch = [rel_dram, lo_dram[1], hi_dram[1], lo_dram[0], hi_dram[0]]
    COMMON_ARRAYS, ARRAYS = 3, 5
    tabB_dram = dram("table_b", [WIDTH, HID], fp32)
    tabH_dram = dram("table_h", [WIDTH, F], fp32)

    ctx = ExitStack()
    with ctx:
        def sb(name, shape, dt=fp32):
            return ctx.enter_context(nc.sbuf_tensor(name, shape, dt))

        def sem(name):
            return ctx.enter_context(nc.semaphore(name))

        m7d = sb("m7d", [128, T])
        rel = m7d
        m4d = sb("m4d", [128, T])
        m4s = sb("m4s", [128, T])
        q7d = sb("q7d", [128, T, Q7], fp16)
        q4d = sb("q4d", [128, T, Q4], fp16)
        q4s = sb("q4s", [128, T, Q4], fp16)
        ea4 = sb("ea4", [128, T, K1 - 1])
        ea8 = sb("ea8", [128, T, K2 - 1])
        work = sb("work", [128, BLOCKS * F * F])
        idx_i = [work[:, i * T:(i + 1) * T].bitcast(i32) for i in (0, 1)]
        idx_f = [work[:, i * T:(i + 1) * T] for i in (2, 3)]
        qf = work[:, 4 * T:5 * T]
        lo_f = work[:, 5 * T:6 * T]
        hi_f = work[:, 6 * T:7 * T]
        jd = work[:, 7 * T:8 * T]
        src_i = work[:, 7 * T:8 * T].bitcast(i32)
        rd = work[:, 0:T]
        sums_w = work[0:2 * F, 0:WIDTH]
        tab_w = work[0:2 * F, WIDTH:WIDTH + WIDTH // 2].bitcast(fp16)
        outer = work[0:ROWS, :].rearrange("p (j u v) -> p j u v", u=F, v=F)
        stage = sb("stage", [128, 2, 7 * 128], fp16)

        iota_m = sb("iota_m", [128, SPAN4], fp16)
        iota_f = sb("iota_f", [128, 128])
        part_i = sb("part_i", [128, 1], i32)
        first_f = sb("first_f", [1, NG])
        first_i = sb("first_i", [1, NG], i32)
        first_b = sb("first_b", [128, NG])
        bad = sb("bad", [128, 2])
        bad1 = sb("bad1", [1, 1])
        flag = sb("flag", [1, 1], i32)
        part_f = sb("part_f", [128, 1])
        past = sb("past", [128, 1])
        pv = sb("pv", [128, 2])
        ident16b = sb("ident16b", [128, 128], fp16)
        ident = sb("ident", [128, 128])
        ones = sb("ones", [128, 128])
        top1 = sb("top1", [1, 1])
        nmask_i = sb("nmask_i", [ROWS, BLOCKS], i32)
        nmask = sb("nmask", [ROWS, BLOCKS])
        eps_t = sb("eps_t", [128, 1])

        bd_ab = sb("bd_ab", [112, 7, 2 * HID])
        bd_m = sb("bd_m", [112, 7, HID])
        bd_x1 = sb("bd_x1", [112, 7, HID])
        bd_m1 = sb("bd_m1", [112, 7, HID])
        bd_2 = sb("bd_2", [112, 7, HID])
        bd_3 = sb("bd_3", [112, 7, F])
        bd_root = sb("bd_root", [112, 7, F])
        bd_out = sb("bd_out", [112, 7, F])
        bd_e = sb("bd_e", [128, GT, HID])
        bd_y1 = sb("bd_y1", [128, GT, K1 * F])
        bd_y2 = sb("bd_y2", [128, GT, K2 * F])
        wt = sb("wt", [128, 2, F])
        bias = {n: sb("b_" + n, [ROWS, a.shape[0]]) for n, a in
                dict(e1=fe_b1, e3=fe_b3, x1=fx_b1, x2=fx_b2, x3=fx_b3, c=c_bias, g=gamma, be=beta,
                     o=b_out).items()}

        X = sb("X", [ROWS, BLOCKS, F])
        Hn = sb("Hn", [ROWS, BLOCKS, F])
        U = sb("U", [ROWS, BLOCKS, F])
        V = sb("V", [ROWS, BLOCKS, F])
        S = sb("S", [ROWS, BLOCKS, F])
        W = sb("W", [ROWS, BLOCKS, F])
        AB = sb("AB", [ROWS, BLOCKS, 2 * HID])
        st1 = sb("st1", [ROWS, BLOCKS])
        st2 = sb("st2", [ROWS, BLOCKS])
        cnt = sb("cnt", [ROWS, BLOCKS])
        rcnt = sb("rcnt", [ROWS, BLOCKS])
        cs = sb("cs", [ROWS, F])
        cm = sb("cm", [ROWS, F])
        amax = sb("amax", [128, 8])
        aall = sb("aall", [128, 8])
        wmax = sb("wmax", [128, 8])
        sc = sb("sc", [128, 16])
        tabA = sb("tabA", [128, 2, BLOCKS, HID], fp16)
        tabB = sb("tabB", [128, 2, BLOCKS, HID], fp16)
        tabH = sb("tabH", [128, 2, BLOCKS, F], fp16)
        dT = sb("dT", [128, 4 * 128])
        accs = sb("accs", [128, SPAN4])

        bc = [[sb(f"bc{s}{b}", [128, EC], fp16) for b in range(2)] for s in "XY"]
        oh = [[sb(f"oh{s}{b}", [128, 2, EC], fp16) for b in range(2)] for s in "XY"]
        gx = [sb(f"gx{b}", [128, GT, F]) for b in range(2)]
        g0 = sb("g0", [128, GT, HID])
        g1 = [sb(f"g1{b}", [128, GT, HID]) for b in range(2)]
        rows = [sb(f"rows{b}", [128, ND], i32) for b in range(2)]
        spare = [sb(f"spare{b}", [1, 1]) for b in range(2)]
        ones_i = sb("ones_i", [128, ND], i32)
        gs = sb("gs", [128, GT, HID])
        h1 = [sb(f"h1{b}", [128, GT * HID + 1]) for b in range(2)]
        tT = [sb(f"tT{b}", [128, 128]) for b in range(2)]
        zr = [sb(f"zr{b}", [128, GT, HID]) for b in range(2)]
        yw = sb("yw", [128, GT, K2, F])
        iota_i = yw[:, :, :, :].rearrange("p t k o -> p (t k o)")[:, 0:SPAN4].bitcast(i32)
        msg = [sb(f"msg{b}", [128, GT, F]) for b in range(2)]
        parts = [sb(f"parts{b}", [128, GT, 2 * F + 1], fp16) for b in range(2)]
        spread = [sb(f"spread{b}", [128, GT, 128], fp16) for b in range(2)]
        win = [sb(f"win{b}", [128, 2 * F], fp16) for b in range(2)]
        P9 = 2 * F - 2 * HID
        ohm = [sb(f"ohm{b}", [128, GT, SPAN4], fp16) for b in range(2)]

        bank = [ctx.enter_context(nc.psum_tensor(f"bank{i}", [128, 512], fp32)) for i in range(8)]
        acc = bank[4:6]
        ybank = bank[6:8]

        s_idx = sem("idx_loaded")
        s_idx0 = sem("idx_padded")
        s_w0 = sem("weights_cleared")
        s_w = sem("weights_loaded")
        s_iota = sem("iota_made")
        s_const = sem("constants_made")
        s_tab0 = sem("tables_cleared")
        s_lohi = sem("lo_hi_made")
        s_loht = sem("lo_hi_transposed")
        s_stage = sem("lo_hi_staged")
        s_scr = sem("scratch_written")
        s_v = sem("vector_chain")
        s_g = sem("gpsimd_chain")
        s_coh = sem("count_onehots_made")
        s_cmm = sem("count_group_added")
        s_bc = [[sem(f"bc{s}{b}_loaded") for b in range(2)] for s in "XY"]
        s_oh = [sem("ohX_made"), sem("ohY_made")]
        s_gs = sem("sides_added")
        s_first = sem("window_starts_made")
        s_fb = sem("window_starts_spread")
        s_flag = sem("flag_made")
        s_bad = sem("bad_made")
        s_wt = sem("window_transposed")
        s_wc = sem("window_copied")
        s_xg = sem("window_gathered")
        s_xr = sem("window_gather_read")
        s_ac = sem("window_sums_added")
        s_tt = sem("table_blocks_transposed")
        s_td = sem("table_blocks_copied")
        s_srci = sem("gather_rows_made")
        s_rows = sem("gather_rows_copied")
        s_tf = sem("table_scaled")
        s_tw = sem("table_stored")
        s_gd = [sem(f"gathered_by_dma{b}") for b in range(2)]
        s_gat = sem("gather_banks_full")
        s_red = sem("gather_banks_read")
        s_in = sem("edge_input_made")
        s_tr = sem("edge_input_transposed")
        s_tc = sem("transposed_copied")
        s_z = sem("z_made")
        s_y = sem("y_banks_full")
        s_yr = sem("y_banks_read")
        s_yb = sem("y_bias_copied")
        s_msg = sem("message_made")
        s_hi = sem("part_hi_made")
        s_lo = sem("part_lo_made")
        s_sp = sem("parts_spread")
        s_om = sem("onehot_m_made")
        s_sc = sem("group_scattered")
        s_tab = sem("table_written")
        s_mx = sem("maxima_made")
        s_ma = sem("maxima_reduced")
        s_rx = sem("round_maximum_made")
        s_rt = sem("round_maximum_moved")
        s_di = sem("dense_input_made")
        s_dt = sem("dense_transposed")
        s_dc = sem("dense_copied")
        s_dm = sem("dense_made")
        s_ae = sem("sums_copied")
        s_at = sem("sums_transposed")
        s_var = sem("variance_made")
        s_std = sem("deviation_made")
        s_bn = sem("batch_input_made")
        s_bm = sem("batch_sums_made")
        s_uo = sem("outer_made")
        s_ot = sem("outer_transposed")
        s_oc = sem("outer_copied")
        s_om2 = sem("outer_multiplied")
        s_x = sem("x_made")
        s_out = sem("out_written")

        block = ctx.enter_context(nc.Block())

        PRO = 6

        def skewed(eng, stages):
            top = max(lag for lag, _ in stages)
            for s in range(PRO):
                for lag, stage_of in stages:
                    if s - lag >= 0:
                        stage_of(s - lag, (s - lag) % 2)
            with eng.Fori(0, (NG - PRO) // 2) as i:
                for h in range(2):
                    for lag, stage_of in stages:
                        stage_of(i * 2 + (PRO + h - lag), (h - lag) % 2)
            for s in range(NG, NG + top):
                for lag, stage_of in stages:
                    if s - lag < NG:
                        stage_of(s - lag, (s - lag) % 2)

        def wait_reuse(eng, sm, base, g, per, back=2):
            if isinstance(g, int) and g < back:
                if isinstance(base, int) and base > 0:
                    eng.wait_ge(sm, base * per)
            else:
                eng.wait_ge(sm, (base + g - back + 1) * per)

        def by_block(tab):
            return tab[:, :, :, :].rearrange("p k j f -> p (k j f)").rearrange("p (j k f) -> p j k f", k=2,
                                                                               f=tab.shape[3])

        def flag_of(eng):
            eng.wait_ge(s_flag, 1)
            return eng.value_load(flag[0:1, 0:1], min_val=0, max_val=1)

        def start_of(eng, g):
            return eng.value_load(first_i[0:1, bass.ds(g, 1)], min_val=0, max_val=WIDTH - WIN)

        L1_BASE, L2_BASE, L3_BASE = ROUNDS * NG, (ROUNDS + 1) * NG, (ROUNDS + 2) * NG
        Y2_BASE = 2 * NG

        s_w_all = [0]

        @block.sync
        def _(eng):
            eng.wait_ge(s_idx0, 2)

            def load_edges(t, src, sm):
                at, rest = FULL * EC, FULL * EC + REST_P * GT
                k = "k" if len(src.shape) == 2 else ""
                eng.dma_start(t[:, 0:FULL * GT].rearrange("p (g t) -> p g t", t=GT) if not k else
                              t[:, 0:FULL * GT, :].rearrange("p (g t) k -> p g (t k)", t=GT),
                              src[0:at].rearrange("(g p t) -> p g t", p=128, t=GT) if not k else
                              src[0:at, :].rearrange("(g p t) k -> p g (t k)", p=128, t=GT)).then_inc(sm, 16)
                if k:
                    eng.dma_start(t[0:REST_P, FULL * GT:FULL * GT + GT, :],
                                  src[at:rest, :].rearrange("(p t) k -> p t k", t=GT)).then_inc(sm, 16)
                    eng.dma_start(t[REST_P:REST_P + 1, FULL * GT:FULL * GT + REST_T, :],
                                  src[rest:E, :].rearrange("(p t) k -> p t k", p=1)).then_inc(sm, 16)
                else:
                    eng.dma_start(t[0:REST_P, FULL * GT:FULL * GT + GT],
                                  src[at:rest].rearrange("(p t) -> p t", t=GT)).then_inc(sm, 16)
                    eng.dma_start(t[REST_P:REST_P + 1, FULL * GT:FULL * GT + REST_T],
                                  src[rest:E].rearrange("(p t) -> p t", p=1)).then_inc(sm, 16)

            for t, src in zip(idx_i, (dst_in, src_in)):
                load_edges(t, src, s_idx)
            eng.wait_ge(s_w0, 1)

            def load(dst, src):
                eng.dma_start(dst, src).then_inc(s_w, 16)
                s_w_all[0] += 16

            load(X[:, 0:BLOCKS - 1, :], x_in[0:ROWS * (BLOCKS - 1), :].rearrange("(j r) f -> r j f", r=ROWS))
            load(X[0:LAST, BLOCKS - 1, :], x_in[ROWS * (BLOCKS - 1):N, :])
            for name, a in dict(e1=fe_b1, e3=fe_b3, x1=fx_b1, x2=fx_b2, x3=fx_b3, c=c_bias, g=gamma,
                                be=beta, o=b_out).items():
                load(bias[name][:, :], a.rearrange("(z n) -> z n", z=1).broadcast_to([ROWS, a.shape[0]]))
            for j in range(7):
                at = slice(16 * j, 16 * j + F)
                hid = slice(16 * j, 16 * j + HID)
                load(bd_ab[at, j, 0:HID], fe_W1[0:F, :])
                load(bd_ab[at, j, HID:2 * HID], fe_W1[F:2 * F, :])
                load(bd_m[hid, j, :], fe_W3)
                load(bd_x1[at, j, :], fx_W1[0:F, :])
                load(bd_m1[hid, j, :], fx_W1[F:F + HID, :])
                load(bd_2[hid, j, :], fx_W2)
                load(bd_3[hid, j, :], fx_W3)
                load(bd_root[at, j, :], root)
                load(bd_out[at, j, :], w_out)
            for t in range(GT):
                load(bd_e[HID * t:HID * (t + 1), t, :], fe_W2)
                load(bd_e[GT * HID:GT * HID + 1, t, :], fe_b2.rearrange("(z n) -> z n", z=1))
                at = slice(16 * t, 16 * t + F)
                load(bd_y1[at, t, 0:(K1 - 1) * F], enet_w)
                load(bd_y1[at, t, (K1 - 1) * F:K1 * F], enet_b)
                load(bd_y2[at, t, 0:(K2 - 1) * F], k2_w)
                load(bd_y2[at, t, (K2 - 1) * F:K2 * F], k2_b)
            load(wt[:, :, :], w_tp.rearrange("(h p) w -> p h w", p=128))
            for t, src in ((ea4, ea4_in), (ea8, ea8_in)):
                load_edges(t, src, s_w)
                s_w_all[0] += 48

            def store_array(a):
                if a >= 1:
                    eng.wait_ge(s_scr, 32 * a)
                eng.wait_ge(s_stage, 2 * (a + 1))
                st = stage[:, a % 2, :].rearrange("t (c p) -> t c p", p=128)
                eng.dma_start(scratch[a][0:768, :].rearrange("(c t) p -> t c p", t=128),
                              st[:, 0:6, :]).then_inc(s_scr, 16)
                eng.dma_start(scratch[a][768:T, :], st[0:T - 768, 6, :]).then_inc(s_scr, 16)

            for a in range(COMMON_ARRAYS):
                store_array(a)
            eng.wait_ge(s_scr, 32 * COMMON_ARRAYS)

            def wide(base, slot, side, skip=0):
                n, w = GT - skip, (GT - skip) * 128

                def load_group(g, b):
                    wait_reuse(eng, s_oh[slot], base, g, 1)
                    lo = lo_dram[side][bass.ds(g * GT + skip, n), :].rearrange("(z a) p -> z (a p)", z=1)
                    hi = hi_dram[side][bass.ds(g * GT + skip, n), :].rearrange("(z a) p -> z (a p)", z=1)
                    eng.dma_start(bc[slot][b][0:ROWS, 0:w], lo.broadcast_to([ROWS, w])).then_inc(s_bc[slot][b], 16)
                    eng.dma_start(bc[slot][b][ROWS:128, 0:w],
                                  hi.broadcast_to([128 - ROWS, w])).then_inc(s_bc[slot][b], 16)
                return load_group

            def windowed(base):
                def load_group(g, b):
                    wait_reuse(eng, s_oh[0], base, g, 1)
                    at = rel_dram[bass.ds(g * GT, GT), :].rearrange("(z a) p -> z (a p)", z=1)
                    eng.dma_start(bc[0][b][:, :], at.broadcast_to([128, EC])).then_inc(s_bc[0][b], 16)
                return load_group

            def main(windows):
                if not windows:
                    for a in range(COMMON_ARRAYS, ARRAYS):
                        store_array(a)
                    eng.wait_ge(s_scr, 32 * ARRAYS)
                with eng.Fori(0, ROUNDS) as r:
                    eng.wait_ge(s_di, r * DENSE_PER_ROUND + 1)
                    dst_side = windowed(r * NG) if windows else wide(r * NG, 0, 0)
                    skewed(eng, [(0, dst_side), (0, wide(r * NG, 1, 1, ND if windows else 0))])
                if windows:
                    skewed(eng, [(0, wide(L1_BASE, 1, 1, ND))])
                    skewed(eng, [(0, windowed(L1_BASE))])
                    skewed(eng, [(0, windowed(L2_BASE))])
                else:
                    skewed(eng, [(0, wide(L1_BASE, 0, 1))])
                    skewed(eng, [(0, wide(L2_BASE, 0, 0))])
                    skewed(eng, [(0, wide(L3_BASE, 0, 0))])

            near = flag_of(eng)
            with eng.If(near != 0):
                main(True)
            with eng.Else():
                main(False)

            eng.wait_ge(s_x, 1)
            eng.dma_start(out[0:ROWS * (BLOCKS - 1), :].rearrange("(j r) f -> r j f", r=ROWS),
                          X[:, 0:BLOCKS - 1, :]).then_inc(s_out, 16)
            eng.dma_start(out[ROWS * (BLOCKS - 1):N, :], X[0:LAST, BLOCKS - 1, :]).then_inc(s_out, 16)
            eng.wait_ge(s_out, 32)

        @block.gpsimd
        def _(eng):
            eng.memset(idx_i[0], PAD_NODE).then_inc(s_idx0, 1)
            eng.memset(idx_i[1], PAD_NODE).then_inc(s_idx0, 1)
            eng.iota(iota_i, pattern=[[1, SPAN4]], base=0, channel_multiplier=0).then_inc(s_iota, 1)
            eng.iota(part_i[:, :], pattern=[[0, 1]], base=0, channel_multiplier=1).then_inc(s_iota, 1)
            eng.iota(nmask_i[:, :], pattern=[[ROWS, BLOCKS]], base=0, channel_multiplier=1).then_inc(s_iota, 1)
            eng.memset(ident[:, :], 0.0).then_inc(s_g, 1)
            eng.wait_ge(s_g, 1)
            eng.affine_select(out=ident[:, :], in_=ident[:, :], compare_op=ALU.not_equal, fill=1.0, base=0,
                              pattern=[[-1, 128]], channel_multiplier=1).then_inc(s_const, 1)
            eng.memset(ident16b[:, :], 0.0).then_inc(s_g, 1)
            eng.wait_ge(s_g, 2)
            eng.affine_select(out=ident16b[:, :], in_=ident16b[:, :], compare_op=ALU.not_equal, fill=1.0, base=0,
                              pattern=[[-1, 128]], channel_multiplier=1).then_inc(s_const, 1)
            eng.memset(ones_i[:, :], 1)
            for b in range(2):
                eng.memset(parts[b][:, :, :], 1.0)
            tabs = (tabA, tabB, tabH)
            for t in tabs:
                eng.memset(t[:, :, :, :], 0.0).then_inc(s_g, 1)
            eng.wait_ge(s_g, 5)
            for n, t in enumerate(tabs):
                pen = t[:, 0, :, :].rearrange("p (h c) f -> p c h f", c=2)[:, 0, :, :]
                eng.memset(pen, -BIG).then_inc(s_g, 1)
                eng.wait_ge(s_g, 6 + n)
                eng.affine_select(out=pen, in_=pen, compare_op=ALU.not_equal, fill=0.0, base=ROWS,
                                  pattern=[[1, HI], [0, t.shape[3]]], channel_multiplier=-1).then_inc(s_tab0, 1)

            def spreads(base, sbase, mask, nq, two_f):
                def spread_group(g, b):
                    eng.wait_ge(s_lo, base + g + 1)
                    wait_reuse(eng, s_sc, base, g, 1)
                    p0 = 2 * F - two_f
                    out_ap = spread[b][:, :, 0:nq * two_f].rearrange("p t (q c) -> p t q c", c=two_f)
                    eng.tensor_tensor(
                        out_ap,
                        parts[b][:, :, p0:2 * F].unsqueeze(2).broadcast_to([128, GT, nq, two_f]),
                        mask[:, bass.ds(g * GT, GT), :].unsqueeze(3).broadcast_to([128, GT, nq, two_f]),
                        ALU.mult).then_inc(s_sp, 1)
                skewed(eng, [(0, spread_group)])

            eng.wait_ge(s_mx, 1)
            eng.partition_all_reduce(aall[:, :], amax[:, :], 128, bass.bass_isa.ReduceOp.absmax).then_inc(s_ma, 1)

            def fetches(base, tab, dst, used):
                def fetch_group(g, b):
                    wait_reuse(eng, used, base, g, 1)
                    eng.tensor_tensor(rows[b][:, :], src_i[:, bass.ds(g * GT, ND)], ones_i[:, :],
                                      ALU.mult).then_inc(s_rows, 1)
                    eng.wait_ge(s_rows, base + g + 1)
                    eng.tensor_tensor(spare[b][:, :], ones[0:1, 0:1], ones[0:1, 0:1], ALU.mult)
                    for t in range(ND):
                        eng.indirect_dma_start(dst[b][:, t, :], None, tab[:, :],
                                               bass.IndirectOffsetOnAxis(rows[b][:, t:t + 1], 0)) \
                           .then_inc(s_gd[b], 16)
                skewed(eng, [(0, fetch_group)])

            def main(windows):
                if windows:
                    eng.wait_ge(s_srci, 1)
                    with eng.Fori(0, ROUNDS) as r:
                        eng.wait_ge(s_tw, r * 16 + 16)
                        fetches(r * NG, tabB_dram, g1, s_xr)
                    eng.wait_ge(s_tw, (ROUNDS + 1) * 16)
                    fetches(L1_BASE, tabH_dram, gx, s_tr)
                else:
                    with eng.Fori(0, ROUNDS) as r:
                        spreads(r * NG, r * NG, q7d, Q7, 2 * HID)
                    spreads(L1_BASE, L1_BASE, q4d, Q4, 2 * F)
                base = 0 if windows else L2_BASE
                spreads(L2_BASE, base, q4s, Q4, 2 * F)
                spreads(L3_BASE, base + NG, q4s, Q4, 2 * F)

            near = flag_of(eng)
            with eng.If(near != 0):
                main(True)
            with eng.Else():
                main(False)

        @block.tensor
        def _(eng):
            eng.wait_ge(s_const, 2)
            eng.wait_ge(s_first, 1)
            eng.matmul(bank[4][:, 0:NG], ones[0:1, :], first_f[:, :], start=True, stop=True).then_inc(s_fb, 1)

            def turn_array(a, src):
                eng.wait_ge(s_lohi, a + 1)
                if a >= 2:
                    eng.wait_ge(s_stage, 2 * (a - 1))
                for c in range(7):
                    w = min(128, T - 128 * c)
                    dst = bank[2 * (a % 2) + c // 4][0:w, (c % 4) * 128:(c % 4 + 1) * 128]
                    mm = eng.transpose(dst, src[:, 128 * c:128 * c + w], ident[:, :])
                    if c in (3, 6):
                        mm.then_inc(s_loht, 1)

            turn_array(0, rel)
            eng.wait_ge(s_bad, 1)
            eng.matmul(bank[5][0:1, 0:1], bad[:, 1:2], ones[:, 0:1], start=True, stop=True).then_inc(s_fb, 1)
            turn_array(1, lo_f)
            turn_array(2, hi_f)

            def count_group(g, b):
                eng.wait_ge(s_coh, g + 1)
                for t in range(GT):
                    mm = eng.matmul(acc[1][:, 0:BLOCKS], ohm[b][:, t, 0:128], ohm[b][:, t, 128:128 + BLOCKS],
                                    start=isinstance(g, int) and g == 0 and t == 0,
                                    stop=isinstance(g, int) and g == NG - 1 and t == GT - 1)
                mm.then_inc(s_cmm, 1)
            count = [(1, count_group)]

            def dense(n, dense_in, w, spare=0):
                eng.wait_ge(s_di, n + (1 + spare))
                for k in range(4):
                    mm = eng.transpose(bank[0][0:112, k * ROWS:(k + 1) * ROWS],
                                       dense_in[:, 7 * k:7 * k + 7, :].rearrange("p j f -> p (j f)"),
                                       ident[0:ROWS, 0:ROWS])
                mm.then_inc(s_dt, 1)
                eng.wait_ge(s_dc, n + 1)
                o = 7 * w.shape[2]
                for k in range(4):
                    mm = eng.matmul(bank[1][0:ROWS, k * o:(k + 1) * o], dT[0:112, k * ROWS:(k + 1) * ROWS],
                                    w[:, :, :].rearrange("p j o -> p (j o)"), start=True, stop=True)
                mm.then_inc(s_dm, 1)

            def sums(n, nq, two_f, blocks):
                eng.wait_ge(s_ae, n + 1)
                for jj in range(blocks):
                    mm = eng.transpose(bank[2 + jj // 4][0:ROWS, (jj % 4) * nq * two_f:(jj % 4 + 1) * nq * two_f],
                                       accs[0:nq * two_f, jj * ROWS:(jj + 1) * ROWS],
                                       ident[0:nq * two_f, 0:nq * two_f])
                mm.then_inc(s_at, 1)

            def gathers(base, tabs, per_bank, slots, sbase, banks=(0, 1, 2, 3)):
                f = tabs[0].shape[3]
                inc = 4 // len(banks)
                views = [t[:, :, :, :].rearrange("p k (h c) f -> p k c h f", c=2) for t in tabs]

                def gather_group(g, b):
                    for n, k in enumerate(banks):
                        at = n // 2 if len(tabs) == 2 else 0
                        slot = slots[at]
                        if n % 2 == 0:
                            eng.wait_ge(s_oh[slot], sbase + g + 1)
                        if isinstance(g, int) and g == 0:
                            if k == 0 and isinstance(base, int):
                                eng.wait_ge(s_red, base * 4)
                        else:
                            eng.wait_ge(s_red, (base + g) * 4 + (inc * (n + 1) - 4))
                        for t in range(per_bank):
                            tile = (n * per_bank + t) % GT
                            for c in range(2):
                                for p in range(2):
                                    mm = eng.matmul(bank[k][:, t * HI * f:(t + 1) * HI * f],
                                                    oh[slot][b][:, c, tile * 128:(tile + 1) * 128],
                                                    views[at][:, p, c, :, :],
                                                    start=(c == 0 and p == 0), stop=(c == 1 and p == 1))
                        mm.then_inc(s_gat, inc)
                return gather_group

            def rest_gathers(base, tab, per_bank, banks_of):
                f = tab.shape[3]
                view = tab[:, :, :, :].rearrange("p k (h c) f -> p k c h f", c=2)

                def gather_group(g, b):
                    eng.wait_ge(s_oh[1], base + g + 1)
                    wait_reuse(eng, s_red, base, g, 4)
                    for n, k in enumerate(banks_of(b)):
                        for t in range(per_bank):
                            at = n * per_bank + t
                            for c in range(2):
                                for p in range(2):
                                    mm = eng.matmul(bank[k][:, t * HI * f:(t + 1) * HI * f],
                                                    oh[1][b][:, c, at * 128:(at + 1) * 128], view[:, p, c, :, :],
                                                    start=(c == 0 and p == 0), stop=(c == 1 and p == 1))
                        mm.then_inc(s_gat, 4 * per_bank // NP)
                return gather_group

            def window_turns(table_done, free, fbase, per, two_f):
                def window_group(g, b):
                    start = start_of(eng, g)
                    if isinstance(g, int) and g == 0:
                        eng.wait_ge(s_td, table_done * 4)
                    wait_reuse(eng, free, fbase, g, per)
                    eng.matmul(bank[b][:, 0:two_f], tab_w[0:two_f, bass.ds(start, WIN)],
                               ident16b[0:two_f, 0:two_f], start=True, stop=True).then_inc(s_wt, 1)
                return window_group

            def window_gathers(xbase, f):
                def gather_group(g, b):
                    eng.wait_ge(s_wc, xbase + g + 1)
                    eng.wait_ge(s_oh[0], xbase + g + 1)
                    for t in range(GT):
                        for p in range(2):
                            mm = eng.matmul(bank[b][:, t * f:(t + 1) * f], oh[0][b][:, 0, t * 128:(t + 1) * 128],
                                            win[b][:, p * f:(p + 1) * f], start=p == 0, stop=p == 1)
                    mm.then_inc(s_xg, 1)
                return gather_group

            def window_scatters(base, p0, m):
                def scatter_group(g, b):
                    eng.wait_ge(s_om, base + g + 1)
                    eng.wait_ge(s_lo, base + g + 1)
                    wait_reuse(eng, s_ac, base, g, 1)
                    for t in range(GT):
                        mm = eng.matmul(acc[b][0:m, 0:WIN], parts[b][:, t, p0:p0 + m], ohm[b][:, t, 0:WIN],
                                        start=t == 0, stop=t == GT - 1)
                    mm.then_inc(s_sc, 1)
                return scatter_group

            def window_table(k, tab, f):
                for c in range(4):
                    for jj in range(7):
                        src = by_block(tab)[0:ROWS, 7 * c + jj, :, :].rearrange("p k f -> p (k f)")
                        mm = eng.transpose(bank[c][0:2 * f, jj * 57:(jj + 1) * 57].bitcast(fp16), src,
                                           ident16b[0:ROWS, 0:ROWS])
                    mm.then_inc(s_tt, 1)

            def window_sums(done, m):
                eng.wait_ge(s_ac, done)
                per = 512 // m
                for j in range(BLOCKS):
                    mm = eng.matmul(bank[2 + j // per][0:ROWS, (j % per) * m:(j % per + 1) * m],
                                    sums_w[0:m, j * ROWS:(j + 1) * ROWS], ident[0:m, 0:m], start=True, stop=True)
                mm.then_inc(s_at, 1)

            def scatters(base, sbase, m, span):
                def scatter_group(g, b):
                    eng.wait_ge(s_om, base + g + 1)
                    eng.wait_ge(s_sp, sbase + g + 1)
                    first = isinstance(g, int) and g == 0
                    last = isinstance(g, int) and g == NG - 1
                    for t in range(GT):
                        for a in range(-(-span // SPAN7)):
                            lo, hi = a * SPAN7, min(span, (a + 1) * SPAN7)
                            mm = eng.matmul(acc[a][0:m, 0:hi - lo], spread[b][:, t, 0:m], ohm[b][:, t, lo:hi],
                                            start=first and t == 0, stop=last and t == GT - 1)
                    mm.then_inc(s_sc, 1)
                return scatter_group

            def turns(base, cols, src, ready, per, bank_free, fetched=False):
                def turn_group(g, b):
                    eng.wait_ge(ready, (base + g + 1) * per)
                    if fetched:
                        eng.wait_ge(s_gd[b], (base + g + (2 - b)) * (8 * ND))
                    bank_free(g)
                    eng.transpose(ybank[b][0:cols, 384:512], src(b), ident[:, :]).then_inc(s_tr, 1)
                return turn_group

            def z_read(base):
                return lambda g: wait_reuse(eng, s_hi, base, g, 1)

            def y_read(ybase, n):
                def free(g):
                    if ybase or not (isinstance(g, int) and g == 0):
                        eng.wait_ge(s_yr, g * n + ybase)
                return free

            def z_of(base):
                def z_group(g, b):
                    eng.wait_ge(s_tc, base + g + 1)
                    wait_reuse(eng, s_hi, base, g, 1)
                    k = GT * HID
                    eng.matmul(ybank[b][:, 0:k], tT[b][0:k + 1, :],
                               bd_e[0:k + 1, :, :].rearrange("p t o -> p (t o)"),
                               start=True, stop=True).then_inc(s_z, 1)
                return z_group

            def y_of(base, ybase, w, k, per):
                def y_group(g, b):
                    eng.wait_ge(s_tc, base + g + 1)
                    n = GT // per
                    for c in range(n):
                        at = g * n + c
                        if c >= 2:
                            eng.wait_ge(s_yr, at + (ybase - 1))
                        eng.matmul(ybank[c % 2][:, 0:per * k * F], tT[b][:, :],
                                   w[:, c * per:(c + 1) * per, :].rearrange("p t o -> p (t o)"),
                                   start=True, stop=True).then_inc(s_y, 1)
                return y_group

            nd = ROUNDS * DENSE_PER_ROUND
            turn16 = lambda b: gx[b][:, :, :].rearrange("p t f -> p (t f)")

            def main(windows):
                if not windows:
                    turn_array(3, lo_f)
                    turn_array(4, hi_f)
                    skewed(eng, count)
                eng.wait_ge(s_w, s_w_all[0])
                with eng.Fori(0, ROUNDS) as r:
                    d = r * DENSE_PER_ROUND
                    base = r * NG
                    dense(d, Hn, bd_ab)
                    eng.wait_ge(s_rx, r * 2 + 1)
                    eng.transpose(bank[2][0:1, 0:128], amax[:, 0:1], ident[:, :]).then_inc(s_rt, 1)
                    eng.wait_ge(s_rx, r * 2 + 2)
                    eng.matmul(bank[2][:, 128:129], ones[0:1, :], top1[:, :], start=True,
                               stop=True).then_inc(s_rt, 1)
                    eng.wait_ge(s_tab, r + 1)
                    middle = (turns(base, GT * HID + 1, lambda b: h1[b][:, :], s_in, 1, z_read(base)), z_of(base))
                    if windows:
                        window_table(r, tabA, HID)
                        skewed(eng, [(0, window_turns(r + 1, s_xr, base, 1, 2 * HID)),
                                     (0, rest_gathers(base, tabB, 4, lambda b: (2 + b,))),
                                     (0, window_gathers(base, HID)), (1, middle[0]),
                                     (3, window_scatters(base, P9, 2 * HID + 1)), (1, middle[1])])
                        window_sums((r + 1) * NG, 2 * HID + 1)
                    else:
                        skewed(eng, [(0, gathers(base, (tabA, tabB), 4, (0, 1), base)), (1, middle[0]),
                                     (3, scatters(base, base, Q7 * 2 * HID, SPAN7)), (1, middle[1])])
                        sums(r, Q7, 2 * HID, BLOCKS // Q7)
                    dense(d + 1, S, bd_m)
                    dense(d + 2, Hn, bd_x1)
                    dense(d + 3, U, bd_m1)
                    dense(d + 4, V, bd_2)
                    dense(d + 5, U, bd_3)
                eng.wait_ge(s_tab, ROUNDS + 1)
                skewed(eng, [(0, rest_gathers(L1_BASE, tabH, 2, lambda b: (2 * b, 2 * b + 1)) if windows else
                              gathers(L1_BASE, (tabH,), 2, (0,), L1_BASE)),
                             (1, turns(L1_BASE, 128, turn16, s_red, 4, y_read(0, 2), windows)),
                             (3, window_scatters(L1_BASE, 0, 2 * F) if windows else
                              scatters(L1_BASE, L1_BASE, Q4 * 2 * F, SPAN4)),
                             (1, y_of(L1_BASE, 0, bd_y1, K1, 4))])
                if windows:
                    window_sums(L1_BASE + NG, 2 * F)
                else:
                    sums(ROUNDS, Q4, 2 * F, BLOCKS // Q4)
                dense(nd, Hn, bd_root, 1)
                for k in range(2):
                    eng.wait_ge(s_bn, k + 1)
                    eng.matmul(bank[1][0:ROWS, 0:F], ones[0:ROWS, 0:ROWS], cs[:, :], start=True,
                               stop=True).then_inc(s_bm, 1)
                eng.wait_ge(s_tab, ROUNDS + 2)
                middle = (turns(L2_BASE, 128, turn16, s_red, 4, y_read(Y2_BASE, 4)),
                          y_of(L2_BASE, Y2_BASE, bd_y2, K2, 2))
                if windows:
                    window_table(ROUNDS, tabH, F)
                    skewed(eng, [(0, window_turns(ROUNDS + 1, s_red, L2_BASE, 4, 2 * F)),
                                 (1, window_gathers(L1_BASE, F)), (2, middle[0]),
                                 (4, scatters(L2_BASE, 0, Q4 * 2 * F, SPAN4)), (2, middle[1])])
                else:
                    skewed(eng, [(0, gathers(L2_BASE, (tabH,), 2, (0,), L2_BASE)), (1, middle[0]),
                                 (3, scatters(L2_BASE, L2_BASE, Q4 * 2 * F, SPAN4)), (1, middle[1])])
                copied = 0 if windows else ROUNDS + 1
                sums(copied, Q4, 2 * F, BLOCKS // Q4)
                eng.wait_ge(s_tab, ROUNDS + 3)
                if windows:
                    window_table(ROUNDS + 1, tabH, F)
                    skewed(eng, [(0, window_turns(ROUNDS + 2, s_red, L3_BASE, 4, 2 * F)),
                                 (1, window_gathers(L2_BASE, F)),
                                 (3, scatters(L3_BASE, NG, Q4 * 2 * F, SPAN4))])
                else:
                    skewed(eng, [(0, gathers(L3_BASE, (tabH,), 2, (0,), L3_BASE)),
                                 (3, scatters(L3_BASE, L3_BASE, Q4 * 2 * F, SPAN4))])
                sums(copied + 1, Q4, 2 * F, BLOCKS // Q4)

            near = flag_of(eng)
            with eng.If(near != 0):
                main(True)
            with eng.Else():
                main(False)

            eng.wait_ge(s_uo, 1)
            of = outer.rearrange("p j u v -> p j (u v)")
            for k in range(HI + 1):
                if k < HI:
                    if k >= 2:
                        eng.wait_ge(s_oc, k - 1)
                    for c in range(4):
                        mm = eng.transpose(bank[k % 2][:, c * ROWS:(c + 1) * ROWS],
                                           of[:, 2 * k + c // 2, (c % 2) * 128:(c % 2 + 1) * 128],
                                           ident[0:ROWS, 0:ROWS])
                    mm.then_inc(s_ot, 1)
                if k >= 1:
                    eng.wait_ge(s_oc, k)
                    for c in range(2):
                        j = 2 * (k - 1) + c
                        for half in range(2):
                            at = (2 * c + half) * ROWS
                            mm = eng.matmul(bank[4][0:ROWS, j * F:(j + 1) * F], (dT, accs)[(k - 1) % 2][:, at:at + ROWS],
                                            wt[:, half, :], start=half == 0, stop=half == 1)
                    mm.then_inc(s_om2, 1)
            dense(nd + 1, U, bd_out, 1)

        @block.scalar
        def _(eng):
            def stage_array(a):
                for h in range(2):
                    eng.wait_ge(s_loht, 2 * a + h + 1)
                    if a >= 2 and h == 0:
                        eng.wait_ge(s_scr, 32 * (a - 1))
                    w, rows = ((512, 128), (256, 128))[h]
                    copied = eng.activation(stage[0:rows, a % 2, 512 * h:512 * h + w],
                                            bank[2 * (a % 2) + h][0:rows, 0:w], ACT.Copy)
                    if h:
                        copied = eng.activation(stage[0:T - 768, a % 2, 768:896],
                                                bank[2 * (a % 2) + h][0:T - 768, 256:384], ACT.Copy)
                    copied.then_inc(s_stage, 1)

            for a in range(COMMON_ARRAYS):
                stage_array(a)

            def dense(n):
                eng.wait_ge(s_dt, n + 1)
                eng.activation(dT[0:112, 0:4 * ROWS], bank[0][0:112, 0:4 * ROWS], ACT.Copy).then_inc(s_dc, 1)

            def sums(n, done, m, span):
                eng.wait_ge(s_sc, done)
                if span == SPAN7:
                    eng.activation(accs[0:m, 0:span], acc[0][0:m, 0:span], ACT.Copy).then_inc(s_ae, 1)
                else:
                    eng.activation(accs[0:m, 0:SPAN7], acc[0][0:m, 0:SPAN7], ACT.Copy)
                    eng.activation(accs[0:m, SPAN7:span], acc[1][0:m, 0:span - SPAN7], ACT.Copy).then_inc(s_ae, 1)

            def root_of(n, view):
                eng.wait_ge(s_var, n + 1)
                eng.activation(view, view, ACT.Sqrt, bias=eps_t[0:ROWS, :], scale=1.0).then_inc(s_std, 1)

            def turned(base, cols, reader, rbase, per):
                def copy_group(g, b):
                    eng.wait_ge(s_tr, base + g + 1)
                    wait_reuse(eng, reader, rbase, g, per)
                    eng.activation(tT[b][0:cols, :], ybank[b][0:cols, 384:512], ACT.Copy).then_inc(s_tc, 1)
                return copy_group

            def z_parts(base, used):
                def parts_group(g, b):
                    eng.wait_ge(s_z, base + g + 1)
                    used(g)
                    z = ybank[b][:, 0:GT * HID].rearrange("p (t f) -> p t f", f=HID)
                    eng.activation(zr[b][:, :, :], z, ACT.Relu, scale=sc[:, 2:3])
                    eng.activation(parts[b][:, :, P9:P9 + HID], z, ACT.Relu, scale=sc[:, 2:3]).then_inc(s_hi, 1)
                return parts_group

            def y_bias(ybase, k, per):
                def bias_group(g, b):
                    n = GT // per
                    for c in range(n):
                        at = g * n + c
                        eng.wait_ge(s_y, at + (ybase + 1))
                        if not (isinstance(g, int) and g == 0):
                            eng.wait_ge(s_msg, g + (ybase // 2))
                        elif ybase:
                            eng.wait_ge(s_msg, ybase // 2)
                        y = ybank[c % 2][:, 0:per * k * F].rearrange("p (t k o) -> p t k o", k=k, o=F)
                        eng.activation(yw[:, c * per:(c + 1) * per, k - 1, :], y[:, :, k - 1, :],
                                       ACT.Copy).then_inc(s_yb, 1)
                return bias_group

            def hi_parts(src, ready, rbase, per, scale, used):
                def hi_group(g, b):
                    eng.wait_ge(ready, (rbase + g + 1) * per)
                    used(g)
                    eng.activation(parts[b][:, :, 0:F], src[b][:, :, :], ACT.Copy, scale=scale).then_inc(s_hi, 1)
                return hi_group

            def window_copies(xbase, two_f):
                def copy_group(g, b):
                    eng.wait_ge(s_wt, xbase + g + 1)
                    wait_reuse(eng, s_xg, xbase, g, 1)
                    eng.activation(win[b][:, 0:two_f], bank[b][:, 0:two_f], ACT.Copy).then_inc(s_wc, 1)
                return copy_group

            def gathered_copies(xbase, base, reader):
                def copy_group(g, b):
                    eng.wait_ge(s_xg, xbase + g + 1)
                    wait_reuse(eng, reader, base, g, 1)
                    eng.activation(gx[b][:, :, :], bank[b][:, 0:GT * F].rearrange("p (t f) -> p t f", f=F),
                                   ACT.Copy).then_inc(s_red, 4)
                return copy_group

            def window_table(k, two_f):
                for c in range(4):
                    eng.wait_ge(s_tt, 4 * k + (c + 1))
                    eng.activation(tab_w[0:two_f, 7 * c * ROWS:7 * (c + 1) * ROWS],
                                   bank[c][0:two_f, 0:7 * ROWS // 2].bitcast(fp16), ACT.Copy).then_inc(s_td, 1)

            def store_table(k, tab, src):
                eng.wait_ge(s_tf, k + 1)
                view = tab.rearrange("(j r) f -> r j f", r=ROWS)
                eng.dma_start(view, src).then_inc(s_tw, 16)

            def used_by(sm, base):
                return lambda g: wait_reuse(eng, sm, base, g, 1)

            nd = ROUNDS * DENSE_PER_ROUND

            def main(windows):
                if not windows:
                    for a in range(COMMON_ARRAYS, ARRAYS):
                        stage_array(a)
                root_of(0, st2[:, :])
                with eng.Fori(0, ROUNDS) as r:
                    base = r * NG
                    dense(r * DENSE_PER_ROUND)
                    turn = turned(base, GT * HID + 1, s_z, base, 1)
                    if windows:
                        store_table(r, tabB_dram, AB[:, :, HID:2 * HID])
                        window_table(r, 2 * HID)
                        skewed(eng, [(0, window_copies(base, 2 * HID)), (1, turn),
                                     (1, z_parts(base, used_by(s_sc, base)))])
                    else:
                        skewed(eng, [(0, turn), (0, z_parts(base, used_by(s_sp, base)))])
                        sums(r, (r + 1) * NG, Q7 * 2 * HID, SPAN7)
                    for c in range(1, DENSE_PER_ROUND):
                        dense(r * DENSE_PER_ROUND + c)
                root_of(1, st2[:, :])
                if windows:
                    store_table(ROUNDS, tabH_dram, V[:, :, :])
                skewed(eng, [(0, turned(L1_BASE, 128, s_y, 0, 2)), (0, y_bias(0, K1, 4)),
                             (0, hi_parts(msg, s_msg, 0, 1, sc[:, 4:5],
                                          used_by(s_sc if windows else s_sp, L1_BASE)))])
                if not windows:
                    sums(ROUNDS, L1_BASE + NG, 128, SPAN4)
                dense(nd)
                root_of(2, cm[:, :])
                root_of(3, st2[:, :])
                sbase = 0 if windows else L2_BASE
                turn = turned(L2_BASE, 128, s_y, Y2_BASE // 4, 4)
                hi = hi_parts(msg, s_msg, NG, 1, sc[:, 6:7], used_by(s_sp, sbase))
                if windows:
                    window_table(ROUNDS, 2 * F)
                    skewed(eng, [(0, window_copies(L1_BASE, 2 * F)), (1, gathered_copies(L1_BASE, L2_BASE, s_tr)),
                                 (2, turn), (2, y_bias(Y2_BASE, K2, 2)), (2, hi)])
                else:
                    skewed(eng, [(0, turn), (0, y_bias(Y2_BASE, K2, 2)), (0, hi)])
                sums(ROUNDS + 1, L2_BASE + NG, 128, SPAN4)
                root_of(4, st2[:, :])
                hi = hi_parts(gx, s_red, L3_BASE, 4, 1.0, used_by(s_sp, sbase + NG))
                if windows:
                    window_table(ROUNDS + 1, 2 * F)
                    skewed(eng, [(0, window_copies(L2_BASE, 2 * F)), (1, gathered_copies(L2_BASE, L3_BASE, s_lo)),
                                 (1, hi)])
                else:
                    skewed(eng, [(0, hi)])
                sums(ROUNDS + 2, L3_BASE + NG, 128, SPAN4)

            near = flag_of(eng)
            with eng.If(near != 0):
                main(True)
            with eng.Else():
                main(False)

            for k in range(HI):
                eng.wait_ge(s_ot, k + 1)
                if k >= 2:
                    eng.wait_ge(s_om2, k - 1)
                eng.activation((dT, accs)[k % 2][:, 0:4 * ROWS], bank[k % 2][:, 0:4 * ROWS], ACT.Copy).then_inc(s_oc, 1)
            dense(nd + 1)

        @block.vector
        def _(eng):
            chained = [0]
            chain_base = [0]

            def link(ins):
                chained[0] += 1
                ins.then_inc(s_v, 1)
                eng.wait_ge(s_v, chain_base[0] + chained[0])

            def bcj(v):
                return v[:, :].unsqueeze(2).broadcast_to([ROWS, BLOCKS, F])

            def bcf(v, f=F):
                return v[:, 0:f].unsqueeze(1).broadcast_to([ROWS, BLOCKS, f])

            for t in (bd_ab, bd_m, bd_x1, bd_m1, bd_2, bd_3, bd_root, bd_out, bd_e, bd_y1, bd_y2, X, U, V, S):
                eng.memset(t[:, :, :], 0.0)
            for t in (ea4, ea8):
                eng.memset(t[:, FULL * GT:T, :], 0.0)
            for b in range(2):
                eng.memset(h1[b][:, GT * HID:GT * HID + 1], 1.0)
            eng.memset(ones[:, :], 1.0)
            eng.memset(eps_t[:, :], EPS)
            eng.memset(amax[:, :], 0.0).then_inc(s_w0, 1)

            eng.wait_ge(s_iota, 3)
            eng.tensor_copy(iota_m[:, :], iota_i[:, :])
            eng.tensor_copy(iota_f[:, :], iota_i[:, 0:128])
            eng.tensor_scalar(nmask[:, :], nmask_i[:, :], float(N), None, ALU.is_lt)
            link(eng.tensor_copy(part_f[:, :], part_i[:, :]))
            link(eng.tensor_scalar(past[:, :], part_f[:, :], float(ROWS), None, ALU.is_ge))
            link(eng.scalar_tensor_tensor(pv[:, 0:1], past[:, :], -float(ROWS), part_f[:, :], ALU.mult, ALU.add))
            link(eng.tensor_scalar(past[:, :], past[:, :], -float(ROWS), float(ROWS), ALU.mult, ALU.add))
            link(eng.tensor_tensor(pv[:, 1:2], past[:, :], pv[:, 0:1], ALU.add))

            ROUND = 1.5 * 2.0 ** 23

            def split(n, width, q, m):
                link(eng.tensor_scalar(q, n, 1.0 / width, 0.5 / width - 0.5, ALU.mult, ALU.add))
                link(eng.tensor_scalar(q, q, ROUND, -ROUND, ALU.add, ALU.add))
                return eng.scalar_tensor_tensor(m, q, -float(width), n, ALU.mult, ALU.add)

            def mask_of(out_ap, q, n):
                return eng.tensor_tensor(out_ap, q.unsqueeze(2).broadcast_to([128, T, n]),
                                         iota_f[:, 0:n].unsqueeze(1).broadcast_to([128, T, n]), ALU.is_equal)

            eng.wait_ge(s_idx, 96)
            link(eng.tensor_copy(idx_f[0], idx_i[0]))
            eng.tensor_copy(idx_f[1], idx_i[1])
            link(eng.tensor_scalar(first_f[:, :], idx_f[0][0:1, :].rearrange("p (g t) -> p g t", t=GT)[:, :, 0],
                                   float(WIDTH - WIN), None, ALU.min))
            eng.tensor_copy(first_i[:, :], first_f[:, :]).then_inc(s_first, 1)
            eng.wait_ge(s_fb, 1)
            link(eng.tensor_copy(first_b[:, :], bank[4][:, 0:NG]))
            grouped = lambda v: v.rearrange("p (g t) -> p g t", t=GT)
            eng.tensor_tensor(grouped(rel[:, :]), grouped(idx_f[0]),
                              first_b[:, :].unsqueeze(2).broadcast_to([128, NG, GT]),
                              ALU.subtract).then_inc(s_lohi, 1)
            eng.wait_ge(s_lohi, 1)
            link(eng.tensor_scalar(qf, idx_f[0], float(N), None, ALU.is_lt))
            link(eng.scalar_tensor_tensor(lo_f, rel[:, :], float(WIN), qf, ALU.is_ge, ALU.mult))
            link(eng.scalar_tensor_tensor(lo_f, rel[:, :], 0.0, lo_f, ALU.is_lt, ALU.add))
            eng.tensor_reduce(bad[:, 1:2], lo_f, AX.X, ALU.add).then_inc(s_bad, 1)
            eng.wait_ge(s_fb, 2)
            link(eng.tensor_scalar(bad1[:, :], bank[5][0:1, 0:1], 0.5, None, ALU.is_lt))
            eng.tensor_copy(flag[:, :], bad1[:, :]).then_inc(s_flag, 1)
            split(idx_f[1], 2 * ROWS, hi_f, lo_f).then_inc(s_lohi, 2)
            link(split(idx_f[1], SPAN4, qf, m4s[:, :]))
            link(mask_of(q4s[:, :, :], qf, Q4))

            def count_group(g, b):
                wait_reuse(eng, s_cmm, 0, g, 1)
                for t in range(GT):
                    eng.tensor_scalar(ohm[b][:, t, 0:128], iota_m[:, 0:128], rd[:, bass.ds(g * GT + t, 1)], None,
                                      ALU.is_equal)
                eng.tensor_tensor(ohm[b][:, :, 128:128 + BLOCKS],
                                  jd[:, bass.ds(g * GT, GT)].unsqueeze(2).broadcast_to([128, GT, BLOCKS]),
                                  iota_f[:, 0:BLOCKS].unsqueeze(1).broadcast_to([128, GT, BLOCKS]),
                                  ALU.is_equal).then_inc(s_coh, 1)

            def destinations():
                eng.wait_ge(s_loht, 2 * COMMON_ARRAYS)
                split(idx_f[0], 2 * ROWS, hi_f, lo_f).then_inc(s_lohi, 2)
                link(split(idx_f[0], SPAN7, qf, m7d[:, :]))
                link(mask_of(q7d[:, :, :], qf, Q7))
                link(split(idx_f[0], ROWS, jd[:, :], rd[:, :]))
                link(split(idx_f[0], SPAN4, qf, m4d[:, :]))
                link(mask_of(q4d[:, :, :], qf, Q4))
                skewed(eng, [(0, count_group)])
                eng.wait_ge(s_cmm, NG)
                link(eng.tensor_copy(cnt[:, :], acc[1][0:ROWS, 0:BLOCKS]))

            def reciprocal_count():
                link(eng.tensor_scalar(rcnt[:, :], cnt[:, :], 1.0, None, ALU.max))
                link(eng.reciprocal(rcnt[:, :], rcnt[:, :]))

            eng.wait_ge(s_w, s_w_all[0])
            for c, t in ((0, bd_e), (1, bd_y1), (2, bd_y2), (3, ea4), (4, ea8)):
                ins = eng.tensor_reduce(amax[:, c:c + 1], t[:, :, :], AX.XY, ALU.max, apply_absolute_value=True)
            ins.then_inc(s_mx, 1)
            eng.wait_ge(s_ma, 1)
            link(eng.tensor_copy(wmax[:, :], aall[:, :]))
            link(eng.memset(amax[:, :], 0.0))

            def power(at, src, top, more=1.0):
                s, inv = sc[:, at:at + 1], sc[:, at + 1:at + 2]
                link(eng.tensor_scalar(inv, src, 2.0 ** -60, None, ALU.max))
                link(eng.tensor_scalar(inv.bitcast(i32), inv.bitcast(i32), 0x7F800000, None, ALU.bitwise_and))
                link(eng.reciprocal(s, inv))
                link(eng.tensor_scalar(s, s, top, None, ALU.mult))
                link(eng.tensor_scalar(inv, inv, more / top, None, ALU.mult))

            for at, w, e, k in ((4, 1, 3, K1), (6, 2, 4, K2)):
                link(eng.tensor_scalar(wmax[:, e:e + 1], wmax[:, e:e + 1], 1.0, F * 4.0 * k * H_SCALE, ALU.max,
                                       ALU.mult))
                link(eng.tensor_tensor(wmax[:, e:e + 1], wmax[:, e:e + 1], wmax[:, w:w + 1], ALU.mult))
                power(at, wmax[:, e:e + 1], PART_TOP, 1.0 / H_SCALE)

            norms = [0]

            def norm():
                link(eng.tensor_reduce(st1[:, :], X[:, :, :], AX.X, ALU.add))
                link(eng.tensor_scalar(st1[:, :], st1[:, :], 1.0 / F, None, ALU.mult))
                link(eng.tensor_tensor(Hn[:, :, :], X[:, :, :], bcj(st1), ALU.subtract))
                link(eng.tensor_tensor(W[:, :, :], Hn[:, :, :], Hn[:, :, :], ALU.mult))
                link(eng.tensor_reduce(st2[:, :], W[:, :, :], AX.X, ALU.add))
                eng.tensor_scalar(st2[:, :], st2[:, :], 1.0 / F, None, ALU.mult).then_inc(s_var, 1)
                norms[0] += 1
                eng.wait_ge(s_std, norms[0])
                link(eng.reciprocal(st2[:, :], st2[:, :]))
                link(eng.tensor_tensor(Hn[:, :, :], Hn[:, :, :], bcj(st2), ALU.mult))
                return eng.tensor_scalar(Hn[:, :, :], Hn[:, :, :], 0.0, None, ALU.max)

            def table(tab, src, scale, to_turn=False):
                hi, lo = [by_block(tab)[0:ROWS, :, k, :] if to_turn else tab[0:ROWS, k, :, :] for k in range(2)]
                link(eng.tensor_scalar(hi, src, scale, None, ALU.mult))
                return eng.scalar_tensor_tensor(lo, src, scale, hi, ALU.mult, ALU.subtract)

            def onehots(base, slot, reader, rbase, per, w=EC):
                def onehot_group(g, b):
                    eng.wait_ge(s_bc[slot][b], (base + g + (2 - b)) * 16)
                    wait_reuse(eng, reader, rbase, g, per)
                    for c in range(2):
                        ins = eng.tensor_scalar(oh[slot][b][:, c, 0:w], bc[slot][b][:, 0:w], pv[:, c:c + 1], None,
                                                ALU.is_equal)
                    ins.then_inc(s_oh[slot], 1)
                return onehot_group

            def window_onehots(xbase):
                def onehot_group(g, b):
                    eng.wait_ge(s_bc[0][b], (xbase + g + (2 - b)) * 8)
                    wait_reuse(eng, s_xg, xbase, g, 1)
                    eng.tensor_scalar(oh[0][b][:, 0, :], bc[0][b][:, :], part_f[:, 0:1], None,
                                      ALU.is_equal).then_inc(s_oh[0], 1)
                return onehot_group

            def select(k, dst, per, f):
                view = bank[k][:, 0:per * HI * f].rearrange("p (t h f) -> p t f h", h=HI, f=f)
                return eng.tensor_reduce(dst, view, AX.X, ALU.max)

            def select9(base, windows):
                def select_group(g, b):
                    if windows:
                        eng.wait_ge(s_gat, (base + g + 1) * 4)
                        select(2 + b, g1[b][:, ND:GT, :], NP, HID).then_inc(s_red, 4)
                        eng.wait_ge(s_red, (base + g + 1) * 4)
                        eng.wait_ge(s_gd[b], (base + g + (2 - b)) * (8 * ND))
                        eng.wait_ge(s_xg, base + g + 1)
                        eng.tensor_tensor(gs[:, :, :], bank[b][:, 0:GT * HID].rearrange("p (t f) -> p t f", f=HID),
                                          g1[b][:, :, :], ALU.add).then_inc(s_xr, 1)
                        eng.wait_ge(s_xr, base + g + 1)
                    else:
                        for k in range(4):
                            eng.wait_ge(s_gat, (base + g) * 4 + (k + 1))
                            select(k, (g0, g1[0])[k // 2][:, (k % 2) * 4:(k % 2) * 4 + 4, :], 4, HID).then_inc(s_red, 1)
                        eng.wait_ge(s_red, (base + g) * 4 + 4)
                        eng.tensor_tensor(gs[:, :, :], g0[:, :, :], g1[0][:, :, :], ALU.add).then_inc(s_gs, 1)
                        eng.wait_ge(s_gs, base + g + 1)
                    wait_reuse(eng, s_tr, base, g, 1)
                    eng.tensor_scalar(h1[b][:, 0:GT * HID], gs[:, :, :].rearrange("p t f -> p (t f)"), 0.0,
                                      sc[:, 1:2], ALU.max, ALU.mult).then_inc(s_in, 1)
                return select_group

            def select16(base, reader, windows=False):
                def select_group(g, b):
                    wait_reuse(eng, reader, base, g, 1)
                    for k in range(2 if windows else 4):
                        n = 2 if windows else 1
                        eng.wait_ge(s_gat, (base + g) * 4 + n * (k + 1))
                        at = (ND if windows else 0) + 2 * k
                        select((2 * b if windows else 0) + k, gx[b][:, at:at + 2, :], 2, F).then_inc(s_red, n)
                return select_group

            def message(base, ybase, mbase, ea, k, per):
                def message_group(g, b):
                    n = GT // per
                    wait_reuse(eng, s_hi, base, g, 1)
                    for c in range(n):
                        eng.wait_ge(s_yb, g * n + (c + ybase + 1))
                        y = ybank[c % 2][:, 0:per * k * F].rearrange("p (t k o) -> p t k o", k=k, o=F)
                        e = ea[:, bass.ds(g * GT + c * per, per), :].unsqueeze(3)
                        eng.tensor_tensor(yw[:, c * per:(c + 1) * per, 0:k - 1, :], y[:, :, 0:k - 1, :],
                                          e.broadcast_to([128, per, k - 1, F]), ALU.mult).then_inc(s_yr, 1)
                    eng.wait_ge(s_yr, g * n + (n + ybase))
                    eng.tensor_reduce(msg[b][:, :, :], yw[:, :, 0:k, :].rearrange("p t k o -> p t o k"), AX.X,
                                      ALU.add).then_inc(s_msg, 1)
                return message_group

            def low9(base):
                def low_group(g, b):
                    eng.wait_ge(s_hi, base + g + 1)
                    eng.tensor_tensor(parts[b][:, :, P9 + HID:2 * F], zr[b][:, :, :], parts[b][:, :, P9:P9 + HID],
                                      ALU.subtract).then_inc(s_lo, 1)
                return low_group

            def low16(base, src, scale):
                def low_group(g, b):
                    eng.wait_ge(s_hi, base + g + 1)
                    eng.scalar_tensor_tensor(parts[b][:, :, F:2 * F], src[b][:, :, :], scale,
                                             parts[b][:, :, 0:F], ALU.mult, ALU.subtract).then_inc(s_lo, 1)
                return low_group

            def onehot_m(base, m, span):
                def onehot_group(g, b):
                    wait_reuse(eng, s_sc, base, g, 1)
                    for t in range(GT):
                        ins = eng.tensor_scalar(ohm[b][:, t, 0:span], iota_m[:, 0:span],
                                                m[:, bass.ds(g * GT + t, 1)], None, ALU.is_equal)
                    ins.then_inc(s_om, 1)
                return onehot_group

            def window_sum(base, m):
                def sum_group(g, b):
                    start = start_of(eng, g)
                    if not (isinstance(g, int) and g == 0):
                        eng.wait_ge(s_ac, base + g)
                    eng.wait_ge(s_sc, base + g + 1)
                    to = sums_w[0:m, bass.ds(start, WIN)]
                    eng.tensor_tensor(to, acc[b][0:m, 0:WIN], to, ALU.add).then_inc(s_ac, 1)
                return sum_group

            def window_sums(m, f, p0, inv):
                per = 512 // m
                for k in range(0, BLOCKS, per):
                    n = min(per, BLOCKS - k)
                    d = bank[2 + k // per][0:ROWS, 0:n * m].rearrange("p (j f) -> p j f", f=m)
                    link(eng.tensor_scalar(W[:, k:k + n, 0:f], d[:, :, 0:f], inv, None, ALU.mult))
                    ins = eng.scalar_tensor_tensor(S[:, k:k + n, 0:f], d[:, :, f:2 * f], inv, W[:, k:k + n, 0:f],
                                                   ALU.mult, ALU.add)
                    if m > 2 * f:
                        link(ins)
                        ins = eng.tensor_copy(cnt[:, k:k + n], d[:, :, 2 * f])
                return ins

            def sums(nq, f, inv):
                blocks = BLOCKS // nq
                to = S[:, :, :].rearrange("p (q j) f -> p j q f", j=blocks)
                tmp = W[:, :, :].rearrange("p (q j) f -> p j q f", j=blocks)
                for k in range(0, blocks, 4):
                    n = min(4, blocks - k)
                    d = bank[2 + k // 4][0:ROWS, 0:n * nq * 2 * f].rearrange("p (j q s f) -> p j q s f", q=nq,
                                                                             s=2, f=f)
                    for j in range(n):
                        ins = eng.tensor_scalar(tmp[:, k + j, :, 0:f], d[:, j, :, 0, :], inv, None, ALU.mult)
                    link(ins)
                    for j in range(n):
                        ins = eng.scalar_tensor_tensor(to[:, k + j, :, 0:f], d[:, j, :, 1, :], inv,
                                                       tmp[:, k + j, :, 0:f], ALU.mult, ALU.add)
                return ins

            def made(f):
                return bank[1][0:ROWS, 0:BLOCKS * f].rearrange("p (j f) -> p j f", f=f)

            prologue = chained[0]

            def main(windows):
                chained[0], norms[0] = prologue, 0
                if windows:
                    eng.wait_ge(s_loht, 2 * COMMON_ARRAYS)
                    link(eng.tensor_scalar(qf, idx_f[1], float(WIDTH - 1), None, ALU.min))
                    eng.tensor_copy(src_i, qf).then_inc(s_srci, 1)
                else:
                    destinations()
                norm().then_inc(s_di, 1)
                before = chained[0]
                LINKS = 23 if windows else 19
                with eng.Fori(0, ROUNDS) as r:
                    chained[0] = 0
                    chain_base[0] = r * LINKS + before
                    d = r * DENSE_PER_ROUND
                    eng.wait_ge(s_dm, d + 1)
                    eng.tensor_tensor(AB[:, :, 0:HID], made(2 * HID)[:, :, 0:HID], bcf(bias["e1"], HID), ALU.add)
                    link(eng.tensor_copy(AB[:, :, HID:2 * HID], made(2 * HID)[:, :, HID:2 * HID]))
                    eng.tensor_reduce(amax[0:ROWS, 0:1], AB[:, :, :], AX.XY, ALU.max,
                                      apply_absolute_value=True).then_inc(s_rx, 1)
                    eng.wait_ge(s_rt, r * 2 + 1)
                    eng.tensor_reduce(top1[:, :], bank[2][0:1, 0:128], AX.X, ALU.max).then_inc(s_rx, 1)
                    eng.wait_ge(s_rt, r * 2 + 2)
                    power(0, bank[2][:, 128:129], TABLE_TOP)
                    link(eng.tensor_scalar(sc[:, 8:9], sc[:, 1:2], 4.0 * HID * TABLE_TOP, 1.0, ALU.mult, ALU.add))
                    link(eng.tensor_tensor(sc[:, 8:9], sc[:, 8:9], wmax[:, 0:1], ALU.mult))
                    power(2, sc[:, 8:9], PART_TOP)
                    scaled = AB[:, :, HID:2 * HID]
                    if windows:
                        eng.tensor_scalar(scaled, scaled, sc[0:ROWS, 0:1], None, ALU.mult).then_inc(s_tf, 1)
                        eng.wait_ge(s_tf, r + 1)
                    table(tabA, AB[:, :, 0:HID], sc[0:ROWS, 0:1], windows)
                    table(tabB, scaled, 1.0 if windows else sc[0:ROWS, 0:1]).then_inc(s_tab, 1)
                    base = r * NG
                    src_side = onehots(base, 1, s_gat, base, 4, NP * 128 if windows else EC)
                    if windows:
                        link(eng.memset(sums_w, 0.0))
                        skewed(eng, [(0, window_onehots(base)), (0, src_side), (1, select9(base, True)),
                                     (2, low9(base)), (2, onehot_m(base, rel, WIN)),
                                     (4, window_sum(base, 2 * HID + 1))])
                        eng.wait_ge(s_at, r + 1)
                        window_sums(2 * HID + 1, HID, P9, sc[0:ROWS, 3:4]).then_inc(s_di, 1)
                        eng.wait_ge(s_di, d + 2)
                    else:
                        skewed(eng, [(0, onehots(base, 0, s_gat, base, 4)), (0, src_side),
                                     (1, select9(base, False)), (2, low9(base)), (2, onehot_m(base, m7d, SPAN7))])
                        eng.wait_ge(s_at, r + 1)
                        sums(Q7, HID, sc[0:ROWS, 3:4]).then_inc(s_di, 1)
                    link(eng.tensor_tensor(AB[:, :, 0:HID], cnt[:, :].unsqueeze(2).broadcast_to([ROWS, BLOCKS, HID]),
                                           bcf(bias["e3"], HID), ALU.mult))
                    eng.wait_ge(s_dm, d + 2)
                    eng.tensor_tensor(U[:, :, 0:HID], made(HID), AB[:, :, 0:HID], ALU.add).then_inc(s_di, 1)
                    eng.wait_ge(s_dm, d + 3)
                    eng.tensor_tensor(V[:, :, 0:HID], made(HID), bcf(bias["x1"], HID), ALU.add).then_inc(s_di, 1)
                    eng.wait_ge(s_dm, d + 4)
                    eng.wait_ge(s_di, d + 4)
                    link(eng.tensor_tensor(V[:, :, 0:HID], made(HID), V[:, :, 0:HID], ALU.add))
                    eng.tensor_scalar(V[:, :, 0:HID], V[:, :, 0:HID], 0.0, None, ALU.max).then_inc(s_di, 1)
                    eng.wait_ge(s_dm, d + 5)
                    link(eng.tensor_tensor(U[:, :, 0:HID], made(HID), bcf(bias["x2"], HID), ALU.add))
                    eng.tensor_scalar(U[:, :, 0:HID], U[:, :, 0:HID], 0.0, None, ALU.max).then_inc(s_di, 1)
                    eng.wait_ge(s_dm, d + 6)
                    eng.tensor_tensor(Hn[:, :, :], made(F), bcf(bias["x3"]), ALU.add).then_inc(s_di, 1)
                    assert chained[0] == LINKS, chained
                chained[0] = before + ROUNDS * LINKS
                chain_base[0] = 0
                nd = ROUNDS * DENSE_PER_ROUND

                eng.wait_ge(s_di, nd + 1)
                link(eng.tensor_tensor(X[:, :, :], X[:, :, :], Hn[:, :, :], ALU.add))
                link(norm())
                if windows:
                    eng.tensor_scalar(V[:, :, :], Hn[:, :, :], H_SCALE, None, ALU.mult).then_inc(s_tf, 1)
                table(tabH, Hn[:, :, :], H_SCALE).then_inc(s_tab, 1)
                reciprocal_count()
                stages = [(0, onehots(L1_BASE, 1 if windows else 0, s_gat, L1_BASE, 4, NP * 128 if windows else EC)),
                          (2, message(L1_BASE, 0, 0, ea4, K1, 4)), (1, select16(L1_BASE, s_tr, windows)),
                          (2, low16(L1_BASE, msg, sc[:, 4:5]))]
                if windows:
                    link(eng.memset(sums_w, 0.0))
                    skewed(eng, stages + [(2, onehot_m(L1_BASE, rel, WIN)), (4, window_sum(L1_BASE, 2 * F))])
                    eng.wait_ge(s_at, ROUNDS + 1)
                    link(window_sums(2 * F, F, 0, sc[0:ROWS, 5:6]))
                else:
                    skewed(eng, stages + [(2, onehot_m(L1_BASE, m4d, SPAN4))])
                    eng.wait_ge(s_at, ROUNDS + 1)
                    link(sums(Q4, F, sc[0:ROWS, 5:6]))
                link(eng.tensor_tensor(W[:, :, :], S[:, :, :], bcj(rcnt), ALU.mult))
                link(eng.tensor_tensor(W[:, :, :], W[:, :, :], bcf(bias["c"]), ALU.add))
                eng.tensor_copy(U[:, :, :], W[:, :, :]).then_inc(s_di, 1)
                eng.wait_ge(s_dm, nd + 1)
                link(eng.tensor_tensor(W[:, :, :], made(F), W[:, :, :], ALU.add))
                for k in range(2):
                    if k:
                        link(eng.tensor_tensor(U[:, :, :], W[:, :, :], W[:, :, :], ALU.mult))
                    link(eng.tensor_tensor(U[:, :, :], (W, U)[k][:, :, :], bcj(nmask), ALU.mult))
                    eng.tensor_reduce(cs[:, :], U[:, :, :].rearrange("p j f -> p f j"), AX.X, ALU.add).then_inc(s_bn, 1)
                    eng.wait_ge(s_bm, k + 1)
                    ins = eng.tensor_scalar(cm[:, :], bank[1][0:ROWS, 0:F], 1.0 / N, None, ALU.mult)
                    if k == 0:
                        link(ins)
                        link(eng.tensor_tensor(W[:, :, :], W[:, :, :], bcf(cm), ALU.subtract))
                    else:
                        ins.then_inc(s_var, 1)
                norms[0] += 1
                eng.wait_ge(s_std, norms[0])
                link(eng.reciprocal(cm[:, :], cm[:, :]))
                link(eng.tensor_tensor(cm[:, :], cm[:, :], bias["g"][:, :], ALU.mult))
                link(eng.tensor_tensor(W[:, :, :], W[:, :, :], bcf(cm), ALU.mult))
                link(eng.tensor_tensor(W[:, :, :], W[:, :, :], bcf(bias["be"]), ALU.add))
                link(eng.scalar_tensor_tensor(W[:, :, :], W[:, :, :], 0.01, W[:, :, :], ALU.mult, ALU.max))
                link(eng.tensor_tensor(X[:, :, :], X[:, :, :], W[:, :, :], ALU.add))

                link(norm())
                table(tabH, Hn[:, :, :], H_SCALE, windows).then_inc(s_tab, 1)
                if windows:
                    skewed(eng, [(0, window_onehots(L1_BASE)), (3, message(L2_BASE, Y2_BASE, NG, ea8, K2, 2)),
                                 (3, onehot_m(L2_BASE, m4s, SPAN4)), (3, low16(L2_BASE, msg, sc[:, 6:7]))])
                else:
                    skewed(eng, [(0, onehots(L2_BASE, 0, s_gat, L2_BASE, 4)),
                                 (2, message(L2_BASE, Y2_BASE, NG, ea8, K2, 2)),
                                 (1, select16(L2_BASE, s_tr)), (2, low16(L2_BASE, msg, sc[:, 6:7])),
                                 (2, onehot_m(L2_BASE, m4s, SPAN4))])
                eng.wait_ge(s_at, ROUNDS + 2)
                link(sums(Q4, F, sc[0:ROWS, 7:8]))
                link(eng.tensor_tensor(X[:, :, :], X[:, :, :], S[:, :, :], ALU.add))

                link(norm())
                table(tabH, Hn[:, :, :], H_SCALE, windows).then_inc(s_tab, 1)
                if windows:
                    skewed(eng, [(0, window_onehots(L2_BASE)), (2, onehot_m(L3_BASE, m4s, SPAN4)),
                                 (2, low16(L3_BASE, gx, 1.0))])
                else:
                    skewed(eng, [(0, onehots(L3_BASE, 0, s_gat, L3_BASE, 4)), (1, select16(L3_BASE, s_lo)),
                                 (2, low16(L3_BASE, gx, 1.0)), (2, onehot_m(L3_BASE, m4s, SPAN4))])
                eng.wait_ge(s_at, ROUNDS + 3)
                link(sums(Q4, F, 1.0 / H_SCALE))
                for j in range(BLOCKS):
                    ins = eng.tensor_tensor(outer[:, j, :, :], Hn[:, j, :].unsqueeze(2).broadcast_to([ROWS, F, F]),
                                            S[:, j, :].unsqueeze(1).broadcast_to([ROWS, F, F]), ALU.mult)
                ins.then_inc(s_uo, 1)
                eng.wait_ge(s_om2, HI)
                eng.tensor_copy(U[:, :, :], bank[4][0:ROWS, 0:BLOCKS * F].rearrange("p (j f) -> p j f", f=F)) \
                   .then_inc(s_di, 1)
                eng.wait_ge(s_dm, nd + 2)
                link(eng.tensor_tensor(X[:, :, :], made(F), X[:, :, :], ALU.add))
                eng.tensor_tensor(X[:, :, :], X[:, :, :], bcf(bias["o"]), ALU.add).then_inc(s_x, 1)

            near = flag_of(eng)
            with eng.If(near != 0):
                main(True)
            with eng.Else():
                main(False)


def kernel(**a):
    import numpy as np
    import concourse.bacc as bacc
    from concourse import mybir as mb
    from concourse.bass_utils import run_bass_kernel_spmd as run

    g = lambda name: np.asarray(a[name])
    f = a["x"].shape[1]
    k1, k2 = a["edge_attr_4"].shape[1], a["edge_attr_8"].shape[1]
    arrays = [g("x"), g("src"), g("dst"), g("edge_attr_4"), g("edge_attr_8")]
    arrays += [g("L0_gnn_" + n) for n in ("fe_W1", "fe_b1", "fe_W2", "fe_b2", "fe_W3", "fe_b3",
                                          "fx_W1", "fx_b1", "fx_W2", "fx_b2", "fx_W3", "fx_b3")]
    arrays += [g("L1_gnn_enet_w").reshape(f, f, k1).transpose(0, 2, 1).reshape(f, k1 * f),
               g("L1_gnn_enet_b").reshape(f, f), g("L1_gnn_root"), g("L1_gnn_bias"), g("L1_gnn_gamma"),
               g("L1_gnn_beta"),
               g("L2_gnn_kernel").reshape(k2, f, f).transpose(2, 0, 1).reshape(f, k2 * f),
               g("L2_gnn_bias").reshape(f, f).T,
               g("L3_gnn_W_tp").reshape(f * f, f), g("L3_gnn_weight").T, g("L3_gnn_bias")]
    nc = bacc.Bacc("TRN2", target_bir_lowering=False, num_devices=1)
    feed, args = {}, []
    for i, v in enumerate(arrays):
        v = np.ascontiguousarray(v)
        feed[f"in_{i}"] = v
        args.append(nc.dram_tensor(f"in_{i}", v.shape, mb.dt.from_np(v.dtype), kind="ExternalInput").ap())
    o = nc.dram_tensor("out_x", a["x"].shape, mb.dt.float32, kind="ExternalOutput").ap()
    gnn_program(nc, *args, o)
    r = run(nc, [feed], core_ids=[0])
    return r.results[0]["out_x"]
```

```python
import concourse.bass as bass
from concourse import mybir
from contextlib import ExitStack


def gnn_program(
    nc: bass.Bass,
    x_in, src_in, dst_in, ea4_in, ea8_in,
    fe_W1, fe_b1, fe_W2, fe_b2, fe_W3, fe_b3,
    fx_W1, fx_b1, fx_W2, fx_b2, fx_W3, fx_b3,
    enet_w, enet_b, root, c_bias, gamma, beta,
    k2_w, k2_b, w_tp, w_out, b_out,
    out,
):
    fp32, fp16, i32 = mybir.dt.float32, mybir.dt.float16, mybir.dt.int32
    ALU = mybir.AluOpType
    ACT = mybir.ActivationFunctionType
    AX = mybir.AxisListType

    N, F = x_in.shape
    E = src_in.shape[0]
    HID = fe_W2.shape[0]
    ROWS, BLOCKS = 114, 28
    LAST = N - ROWS * (BLOCKS - 1)
    HI = BLOCKS // 2
    GT = 8
    ND = 4
    NP = GT - ND
    ND0 = (ND, ND - 1)
    T = 816
    NG = T // GT
    EC = GT * 128
    FULL = E // EC
    REST_P = (E - FULL * EC) // GT
    REST_T = (E - FULL * EC) % GT
    WIN = 128
    WIDTH = ROWS * BLOCKS
    PAD_NODE = 4000
    MORE_AT = 384
    BIG = 32768.0
    TABLE_TOP = 4096.0
    H_SCALE = 2048.0
    PART_TOP = 16384.0
    EPS = 1e-5
    Q7, Q4 = 7, 4
    SPAN7, SPAN4 = ROWS * BLOCKS // Q7, ROWS * BLOCKS // Q4
    K1, K2 = ea4_in.shape[1] + 1, ea8_in.shape[1] + 1
    ROUNDS = 3
    DENSE_PER_ROUND = 5
    assert N <= WIDTH < PAD_NODE - WIN and E <= 128 * T and REST_T and NG % 2 == 0

    def dram(name, shape, dt):
        return nc.dram_tensor(name, shape, dt, kind="Internal").ap()

    lo_dram = [dram("lo_dst", [T, 128], fp16), dram("lo_src", [T, 128], fp16)]
    hi_dram = [dram("hi_dst", [T, 128], fp16), dram("hi_src", [T, 128], fp16)]
    rel_dram = dram("rel_dst", [T, 128], fp16)
    scratch = [rel_dram, lo_dram[1], hi_dram[1], lo_dram[0], hi_dram[0]]
    COMMON_ARRAYS, ARRAYS = 3, 5
    tabB_dram = dram("table_b", [WIDTH, HID], fp32)
    tabH_dram = dram("table_h", [WIDTH, F], fp32)

    ctx = ExitStack()
    with ctx:
        def sb(name, shape, dt=fp32):
            return ctx.enter_context(nc.sbuf_tensor(name, shape, dt))

        def sem(name):
            return ctx.enter_context(nc.semaphore(name))

        m7d = sb("m7d", [128, T])
        rel = m7d
        m4d = sb("m4d", [128, T])
        m4s = sb("m4s", [128, T])
        q7d = sb("q7d", [128, T, Q7], fp16)
        ms, q7s = m4s, q7d
        q4d = sb("q4d", [128, T, Q4], fp16)
        q4s = sb("q4s", [128, T, Q4], fp16)
        ea4 = sb("ea4", [128, T, K1 - 1])
        ea8 = sb("ea8", [128, T, K2 - 1])
        work = sb("work", [128, BLOCKS * F * F])
        idx_i = [work[:, i * T:(i + 1) * T].bitcast(i32) for i in (0, 1)]
        idx_f = [work[:, i * T:(i + 1) * T] for i in (2, 3)]
        qf = work[:, 4 * T:5 * T]
        lo_f = work[:, 5 * T:6 * T]
        hi_f = work[:, 6 * T:7 * T]
        jd = work[:, 7 * T:8 * T]
        src_i = work[:, 7 * T:8 * T].bitcast(i32)
        rd = work[:, 0:T]
        sums_w = work[0:2 * F, 0:WIDTH]
        tab_w = work[0:2 * F, WIDTH:WIDTH + WIDTH // 2].bitcast(fp16)
        outer = work[0:ROWS, :].rearrange("p (j u v) -> p j u v", u=F, v=F)
        stage = sb("stage", [128, 2, 7 * 128], fp16)

        iota_m = sb("iota_m", [128, SPAN4], fp16)
        iota_f = sb("iota_f", [128, 128])
        part_i = sb("part_i", [128, 1], i32)
        first_f = sb("first_f", [1, NG // 2])
        first_i = sb("first_i", [1, NG // 2], i32)
        first_b = sb("first_b", [128, NG // 2])
        bad = sb("bad", [128, 2])
        bad1 = sb("bad1", [1, 1])
        flag = sb("flag", [1, 1], i32)
        part_f = sb("part_f", [128, 1])
        past = sb("past", [128, 1])
        pv = sb("pv", [128, 2])
        ident16b = sb("ident16b", [128, 128], fp16)
        ident = sb("ident", [128, 128])
        ones = sb("ones", [128, 128])
        top1 = sb("top1", [1, 1])
        nmask_i = sb("nmask_i", [ROWS, BLOCKS], i32)
        nmask = sb("nmask", [ROWS, BLOCKS])
        eps_t = sb("eps_t", [128, 1])

        bd_ab = sb("bd_ab", [112, 7, 2 * HID])
        bd_m = sb("bd_m", [112, 7, HID])
        bd_x1 = sb("bd_x1", [112, 7, HID])
        bd_m1 = sb("bd_m1", [112, 7, HID])
        bd_2 = sb("bd_2", [112, 7, HID])
        bd_3 = sb("bd_3", [112, 7, F])
        bd_root = sb("bd_root", [112, 7, F])
        bd_out = sb("bd_out", [112, 7, F])
        bd_e = sb("bd_e", [128, GT, HID])
        bd_y1 = sb("bd_y1", [128, GT, K1 * F])
        bd_y2 = sb("bd_y2", [128, GT, K2 * F])
        wt = sb("wt", [128, 2, F])
        bias = {n: sb("b_" + n, [ROWS, a.shape[0]]) for n, a in
                dict(e1=fe_b1, e3=fe_b3, x1=fx_b1, x2=fx_b2, x3=fx_b3, c=c_bias, g=gamma, be=beta,
                     o=b_out).items()}

        X = sb("X", [ROWS, BLOCKS, F])
        Hn = sb("Hn", [ROWS, BLOCKS, F])
        U = sb("U", [ROWS, BLOCKS, F])
        V = sb("V", [ROWS, BLOCKS, F])
        S = sb("S", [ROWS, BLOCKS, F])
        W = sb("W", [ROWS, BLOCKS, F])
        AB = sb("AB", [ROWS, BLOCKS, 2 * HID])
        st1 = sb("st1", [ROWS, BLOCKS])
        st2 = sb("st2", [ROWS, BLOCKS])
        cnt = sb("cnt", [ROWS, BLOCKS])
        rcnt = sb("rcnt", [ROWS, BLOCKS])
        cs = sb("cs", [ROWS, F])
        cm = sb("cm", [ROWS, F])
        amax = sb("amax", [128, 8])
        aall = sb("aall", [128, 8])
        wmax = sb("wmax", [128, 8])
        sc = sb("sc", [128, 16])
        tabA = sb("tabA", [128, 2, BLOCKS, HID], fp16)
        tabB = sb("tabB", [128, 2, BLOCKS, HID], fp16)
        tabH = sb("tabH", [128, 2, BLOCKS, F], fp16)
        dT = sb("dT", [128, 4 * 128])
        accs = sb("accs", [128, 2 * SPAN7])

        bc = [[sb(f"bc{s}{b}", [128, EC], fp16) for b in range(2)] for s in "XY"]
        oh = [[sb(f"oh{s}{b}", [128, 2, EC], fp16) for b in range(2)] for s in "XY"]
        gx = [sb(f"gx{b}", [128, GT, F]) for b in range(2)]
        g0 = sb("g0", [128, GT, HID])
        g1 = [sb(f"g1{b}", [128, GT, HID]) for b in range(2)]
        rows = [sb(f"rows{b}", [128, 2, ND], i32) for b in range(2)]
        spare = [sb(f"spare{b}", [1, 1]) for b in range(2)]
        ones_i = sb("ones_i", [128, 2, ND], i32)
        gs = sb("gs", [128, GT, HID])
        h1 = [sb(f"h1{b}", [128, GT * HID + 1]) for b in range(2)]
        tT = [sb(f"tT{b}", [128, 128]) for b in range(2)]
        zr = [sb(f"zr{b}", [128, GT, HID]) for b in range(2)]
        yw = sb("yw", [128, GT, K2, F])
        iota_i = yw[:, :, :, :].rearrange("p t k o -> p (t k o)")[:, 0:SPAN4].bitcast(i32)
        msg = [sb(f"msg{b}", [128, GT, F]) for b in range(2)]
        parts = [sb(f"parts{b}", [128, GT, 2 * F + 1], fp16) for b in range(2)]
        spread = [sb(f"spread{b}", [128, GT, 128], fp16) for b in range(2)]
        spread7 = [oh[1][b][:, :, :].rearrange("p c e -> p (c e)")[:, 0:GT * 2 * Q7 * F]
                   .rearrange("p (t s q f) -> p t s q f", t=GT, s=2, f=F) for b in range(2)]
        win = [sb(f"win{b}", [128, 2 * F], fp16) for b in range(2)]
        P9 = 2 * F - 2 * HID
        ohm = [sb(f"ohm{b}", [128, GT, SPAN4], fp16) for b in range(2)]

        bank = [ctx.enter_context(nc.psum_tensor(f"bank{i}", [128, 512], fp32)) for i in range(8)]
        acc = bank[4:6]
        ybank = bank[6:8]
        ybank4 = bank[2:4] + bank[6:8]

        s_idx = sem("idx_loaded")
        s_idx0 = sem("idx_padded")
        s_w0 = sem("weights_cleared")
        s_w = sem("weights_loaded")
        s_wy = sem("edge_weights_loaded")
        s_iota = sem("iota_made")
        s_const = sem("constants_made")
        s_tab0 = sem("tables_cleared")
        s_lohi = sem("lo_hi_made")
        s_loht = sem("lo_hi_transposed")
        s_stage = sem("lo_hi_staged")
        s_scr = sem("scratch_written")
        s_v = sem("vector_chain")
        s_g = sem("gpsimd_chain")
        s_coh = sem("count_onehots_made")
        s_cmm = sem("count_group_added")
        s_bc = [[sem(f"bc{s}{b}_loaded") for b in range(2)] for s in "XY"]
        s_oh = [sem("ohX_made"), sem("ohY_made")]
        s_gs = sem("sides_added")
        s_first = sem("window_starts_made")
        s_fb = sem("window_starts_spread")
        s_flag = sem("flag_made")
        s_bad = sem("bad_made")
        s_wt = sem("window_transposed")
        s_wc = sem("window_copied")
        s_xg = sem("window_gathered")
        s_xr = sem("window_gather_read")
        s_ac = sem("window_sums_added")
        s_tt = sem("table_blocks_transposed")
        s_td = sem("table_blocks_copied")
        s_srci = sem("gather_rows_made")
        s_rows = sem("gather_rows_copied")
        s_tf = sem("table_scaled")
        s_tw = sem("table_stored")
        s_gd = [sem(f"gathered_by_dma{b}") for b in range(2)]
        s_gat = sem("gather_banks_full")
        s_red = sem("gather_banks_read")
        s_in = sem("edge_input_made")
        s_tr = sem("edge_input_transposed")
        s_tc = sem("transposed_copied")
        s_z = sem("z_made")
        s_y = sem("y_banks_full")
        s_yr = sem("y_banks_read")
        s_yb = sem("y_bias_copied")
        s_msg = sem("message_made")
        s_hi = sem("part_hi_made")
        s_lo = sem("part_lo_made")
        s_sp = sem("parts_spread")
        s_om = sem("onehot_m_made")
        s_sc = sem("group_scattered")
        s_tab = sem("table_written")
        s_mx = sem("maxima_made")
        s_ma = sem("maxima_reduced")
        s_rx = sem("round_maximum_made")
        s_rt = sem("round_maximum_moved")
        s_di = sem("dense_input_made")
        s_dt = sem("dense_transposed")
        s_dc = sem("dense_copied")
        s_dm = sem("dense_made")
        s_ae = sem("sums_copied")
        s_at = sem("sums_transposed")
        s_var = sem("variance_made")
        s_std = sem("deviation_made")
        s_bn = sem("batch_input_made")
        s_bm = sem("batch_sums_made")
        s_uo = sem("outer_made")
        s_ot = sem("outer_transposed")
        s_oc = [sem("outer_copied_by_scalar"), sem("outer_copied_by_vector")]
        s_om2 = sem("outer_multiplied")
        s_x = sem("x_made")
        s_out = sem("out_written")

        block = ctx.enter_context(nc.Block())

        PRO = 6

        def skewed(eng, stages):
            top = max(lag for lag, _ in stages)
            for s in range(PRO):
                for lag, stage_of in stages:
                    if s - lag >= 0:
                        stage_of(s - lag, (s - lag) % 2, ((s - lag) // 2, (s - lag) // 2 % 2))
            with eng.Fori(0, (NG - PRO) // 4) as i:
                for h in range(4):
                    for lag, stage_of in stages:
                        at = PRO + h - lag
                        stage_of(i * 4 + at, at % 2, (i * 2 + at // 2, at // 2 % 2))
            for s in range(NG, NG + top):
                for lag, stage_of in stages:
                    if s - lag < NG:
                        stage_of(s - lag, (s - lag) % 2, ((s - lag) // 2, (s - lag) // 2 % 2))

        def wait_reuse(eng, sm, base, g, per, back=2):
            if isinstance(g, int) and g < back:
                if isinstance(base, int) and base > 0:
                    eng.wait_ge(sm, base * per)
            else:
                eng.wait_ge(sm, (base + g - back + 1) * per)

        def by_block(tab):
            return tab[:, :, :, :].rearrange("p k j f -> p (k j f)").rearrange("p (j k f) -> p j k f", k=2,
                                                                               f=tab.shape[3])

        def flag_of(eng):
            eng.wait_ge(s_flag, 1)
            return eng.value_load(flag[0:1, 0:1], min_val=0, max_val=1)

        def start_of(eng, pair):
            return eng.value_load(first_i[0:1, bass.ds(pair[0], 1)], min_val=0, max_val=WIDTH - WIN)

        def fetched_by(base, g, b):
            if base is L1_BASE:
                return L1_BASE * 8 * ND0[b] + (g + (2 - b)) * (8 * ND)
            return (base + g + (2 - b)) * (8 * ND0[b])

        def gather_read(eng, free, fbase, g, per, turned):
            wait_reuse(eng, free, fbase, g, per)
            if turned:
                wait_reuse(eng, s_tc, fbase, g, 1)

        L1_BASE, L2_BASE, L3_BASE = ROUNDS * NG, (ROUNDS + 1) * NG, (ROUNDS + 2) * NG
        Y2_BASE = 2 * NG

        s_w_all = [0]

        @block.sync
        def _(eng):
            eng.wait_ge(s_idx0, 2)

            def load_edges(t, src, sm):
                at, rest = FULL * EC, FULL * EC + REST_P * GT
                k = "k" if len(src.shape) == 2 else ""
                eng.dma_start(t[:, 0:FULL * GT].rearrange("p (g t) -> p g t", t=GT) if not k else
                              t[:, 0:FULL * GT, :].rearrange("p (g t) k -> p g (t k)", t=GT),
                              src[0:at].rearrange("(g p t) -> p g t", p=128, t=GT) if not k else
                              src[0:at, :].rearrange("(g p t) k -> p g (t k)", p=128, t=GT)).then_inc(sm, 16)
                if k:
                    eng.dma_start(t[0:REST_P, FULL * GT:FULL * GT + GT, :],
                                  src[at:rest, :].rearrange("(p t) k -> p t k", t=GT)).then_inc(sm, 16)
                    eng.dma_start(t[REST_P:REST_P + 1, FULL * GT:FULL * GT + REST_T, :],
                                  src[rest:E, :].rearrange("(p t) k -> p t k", p=1)).then_inc(sm, 16)
                else:
                    eng.dma_start(t[0:REST_P, FULL * GT:FULL * GT + GT],
                                  src[at:rest].rearrange("(p t) -> p t", t=GT)).then_inc(sm, 16)
                    eng.dma_start(t[REST_P:REST_P + 1, FULL * GT:FULL * GT + REST_T],
                                  src[rest:E].rearrange("(p t) -> p t", p=1)).then_inc(sm, 16)

            for t, src in zip(idx_i, (dst_in, src_in)):
                load_edges(t, src, s_idx)
            eng.wait_ge(s_w0, 1)

            def load(dst, src):
                eng.dma_start(dst, src).then_inc(s_w, 16)
                s_w_all[0] += 16

            for t, src in ((ea4, ea4_in), (ea8, ea8_in)):
                load_edges(t, src, s_w)
                s_w_all[0] += 48
            load(X[:, 0:BLOCKS - 1, :], x_in[0:ROWS * (BLOCKS - 1), :].rearrange("(j r) f -> r j f", r=ROWS))
            load(X[0:LAST, BLOCKS - 1, :], x_in[ROWS * (BLOCKS - 1):N, :])
            for name, a in dict(e1=fe_b1, e3=fe_b3, x1=fx_b1, x2=fx_b2, x3=fx_b3, c=c_bias, g=gamma,
                                be=beta, o=b_out).items():
                load(bias[name][:, :], a.rearrange("(z n) -> z n", z=1).broadcast_to([ROWS, a.shape[0]]))
            for j in range(7):
                at = slice(16 * j, 16 * j + F)
                hid = slice(16 * j, 16 * j + HID)
                load(bd_ab[at, j, 0:HID], fe_W1[0:F, :])
                load(bd_ab[at, j, HID:2 * HID], fe_W1[F:2 * F, :])
                load(bd_m[hid, j, :], fe_W3)
                load(bd_x1[at, j, :], fx_W1[0:F, :])
                load(bd_m1[hid, j, :], fx_W1[F:F + HID, :])
                load(bd_2[hid, j, :], fx_W2)
                load(bd_3[hid, j, :], fx_W3)
                load(bd_root[at, j, :], root)
                load(bd_out[at, j, :], w_out)
            for t in range(GT):
                load(bd_e[HID * t:HID * (t + 1), t, :], fe_W2)
                load(bd_e[GT * HID:GT * HID + 1, t, :], fe_b2.rearrange("(z n) -> z n", z=1))
            load(wt[:, :, :], w_tp.rearrange("(h p) w -> p h w", p=128))

            def store_array(a):
                if a >= 1:
                    eng.wait_ge(s_scr, 32 * a)
                eng.wait_ge(s_stage, 2 * (a + 1))
                st = stage[:, a % 2, :].rearrange("t (c p) -> t c p", p=128)
                eng.dma_start(scratch[a][0:768, :].rearrange("(c t) p -> t c p", t=128),
                              st[:, 0:6, :]).then_inc(s_scr, 16)
                eng.dma_start(scratch[a][768:T, :], st[0:T - 768, 6, :]).then_inc(s_scr, 16)

            for a in range(COMMON_ARRAYS):
                store_array(a)
            eng.wait_ge(s_scr, 32 * COMMON_ARRAYS)

            def wide(base, slot, side, skips=(0, 0)):
                def load_group(g, b, pair):
                    skip = skips[b]
                    n, w = GT - skip, (GT - skip) * 128
                    wait_reuse(eng, s_oh[slot], base, g, 1)
                    lo = lo_dram[side][bass.ds(g * GT + skip, n), :].rearrange("(z a) p -> z (a p)", z=1)
                    hi = hi_dram[side][bass.ds(g * GT + skip, n), :].rearrange("(z a) p -> z (a p)", z=1)
                    eng.dma_start(bc[slot][b][0:ROWS, 0:w], lo.broadcast_to([ROWS, w])).then_inc(s_bc[slot][b], 16)
                    eng.dma_start(bc[slot][b][ROWS:128, 0:w],
                                  hi.broadcast_to([128 - ROWS, w])).then_inc(s_bc[slot][b], 16)
                return load_group

            def windowed(base):
                def load_group(g, b, pair):
                    wait_reuse(eng, s_oh[0], base, g, 1)
                    at = rel_dram[bass.ds(g * GT, GT), :].rearrange("(z a) p -> z (a p)", z=1)
                    eng.dma_start(bc[0][b][:, :], at.broadcast_to([128, EC])).then_inc(s_bc[0][b], 16)
                return load_group

            def main(windows):
                if not windows:
                    for a in range(COMMON_ARRAYS, ARRAYS):
                        store_array(a)
                    eng.wait_ge(s_scr, 32 * ARRAYS)
                with eng.Fori(0, ROUNDS) as r:
                    eng.wait_ge(s_di, r * DENSE_PER_ROUND + 1)
                    dst_side = windowed(r * NG) if windows else wide(r * NG, 0, 0)
                    skewed(eng, [(0, dst_side), (0, wide(r * NG, 1, 1, ND0 if windows else (0, 0)))])
                if windows:
                    skewed(eng, [(0, wide(L1_BASE, 1, 1, (ND, ND)))])
                    skewed(eng, [(0, windowed(L1_BASE))])
                    skewed(eng, [(0, windowed(L2_BASE))])
                else:
                    skewed(eng, [(0, wide(L1_BASE, 0, 1))])
                    skewed(eng, [(0, wide(L2_BASE, 0, 0))])
                    skewed(eng, [(0, wide(L3_BASE, 0, 0))])

            near = flag_of(eng)
            with eng.If(near != 0):
                main(True)
            with eng.Else():
                main(False)

            eng.wait_ge(s_x, 1)
            eng.dma_start(out[0:ROWS * (BLOCKS - 1), :].rearrange("(j r) f -> r j f", r=ROWS),
                          X[:, 0:BLOCKS - 1, :]).then_inc(s_out, 16)
            eng.dma_start(out[ROWS * (BLOCKS - 1):N, :], X[0:LAST, BLOCKS - 1, :]).then_inc(s_out, 16)
            eng.wait_ge(s_out, 32)

        @block.gpsimd
        def _(eng):
            eng.memset(idx_i[0], PAD_NODE).then_inc(s_idx0, 1)
            eng.memset(idx_i[1], PAD_NODE).then_inc(s_idx0, 1)
            eng.iota(iota_i, pattern=[[1, SPAN4]], base=0, channel_multiplier=0).then_inc(s_iota, 1)
            eng.iota(part_i[:, :], pattern=[[0, 1]], base=0, channel_multiplier=1).then_inc(s_iota, 1)
            eng.iota(nmask_i[:, :], pattern=[[ROWS, BLOCKS]], base=0, channel_multiplier=1).then_inc(s_iota, 1)
            eng.memset(ident[:, :], 0.0).then_inc(s_g, 1)
            eng.wait_ge(s_g, 1)
            eng.affine_select(out=ident[:, :], in_=ident[:, :], compare_op=ALU.not_equal, fill=1.0, base=0,
                              pattern=[[-1, 128]], channel_multiplier=1).then_inc(s_const, 1)
            eng.memset(ident16b[:, :], 0.0).then_inc(s_g, 1)
            eng.wait_ge(s_g, 2)
            eng.affine_select(out=ident16b[:, :], in_=ident16b[:, :], compare_op=ALU.not_equal, fill=1.0, base=0,
                              pattern=[[-1, 128]], channel_multiplier=1).then_inc(s_const, 1)
            eng.memset(ones_i[:, :, :], 1)
            for b in range(2):
                eng.memset(parts[b][:, :, :], 1.0)
            tabs = (tabA, tabB, tabH)
            for t in tabs:
                eng.memset(t[:, :, :, :], 0.0).then_inc(s_g, 1)
            eng.wait_ge(s_g, 5)
            for n, t in enumerate(tabs):
                pen = t[:, 0, :, :].rearrange("p (h c) f -> p c h f", c=2)[:, 0, :, :]
                eng.memset(pen, -BIG).then_inc(s_g, 1)
                eng.wait_ge(s_g, 6 + n)
                eng.affine_select(out=pen, in_=pen, compare_op=ALU.not_equal, fill=0.0, base=ROWS,
                                  pattern=[[1, HI], [0, t.shape[3]]], channel_multiplier=-1).then_inc(s_tab0, 1)

            def spreads(base, sbase, mask, nq, two_f):
                def spread_group(g, b, pair):
                    eng.wait_ge(s_lo, base + g + 1)
                    wait_reuse(eng, s_sc, base, g, 1)
                    p0 = 2 * F - two_f
                    out_ap = spread[b][:, :, 0:nq * two_f].rearrange("p t (q c) -> p t q c", c=two_f)
                    eng.tensor_tensor(
                        out_ap,
                        parts[b][:, :, p0:2 * F].unsqueeze(2).broadcast_to([128, GT, nq, two_f]),
                        mask[:, bass.ds(g * GT, GT), :].unsqueeze(3).broadcast_to([128, GT, nq, two_f]),
                        ALU.mult).then_inc(s_sp, 1)
                skewed(eng, [(0, spread_group)])

            eng.wait_ge(s_w0, 1)
            for t in range(GT):
                at = slice(16 * t, 16 * t + F)
                for dst, src in ((bd_y1[at, t, 0:(K1 - 1) * F], enet_w), (bd_y1[at, t, (K1 - 1) * F:K1 * F], enet_b),
                                 (bd_y2[at, t, 0:(K2 - 1) * F], k2_w), (bd_y2[at, t, (K2 - 1) * F:K2 * F], k2_b)):
                    eng.dma_start(dst, src).then_inc(s_wy, 16)
            eng.wait_ge(s_mx, 1)
            eng.partition_all_reduce(aall[:, :], amax[:, :], 128, bass.bass_isa.ReduceOp.absmax).then_inc(s_ma, 1)

            def spreads7(base):
                def spread_group(g, b, pair):
                    eng.wait_ge(s_lo, base + g + 1)
                    wait_reuse(eng, s_sc, base, g, 1)
                    for p in range(2):
                        ins = eng.tensor_tensor(
                            spread7[b][:, :, p, :, :],
                            parts[b][:, :, p * F:(p + 1) * F].unsqueeze(2).broadcast_to([128, GT, Q7, F]),
                            q7s[:, bass.ds(g * GT, GT), :].unsqueeze(3).broadcast_to([128, GT, Q7, F]),
                            ALU.mult)
                    ins.then_inc(s_sp, 1)
                skewed(eng, [(0, spread_group)])

            def fetches(base, tab, dst, used, nd):
                def fetch_group(g, b, pair):
                    wait_reuse(eng, used, base, g, 1)
                    at = rows[pair[1]]
                    if not b:
                        both = src_i[:, bass.ds(pair[0] * (2 * GT), 2 * GT)].rearrange("p (h t) -> p h t", t=GT)
                        eng.tensor_tensor(at[:, :, :], both[:, :, 0:ND], ones_i[:, :, :],
                                          ALU.mult).then_inc(s_rows, 2)
                        eng.wait_ge(s_rows, base + g + 2)
                    eng.tensor_tensor(spare[b][:, :], ones[0:1, 0:1], ones[0:1, 0:1], ALU.mult)
                    for t in range(nd[b]):
                        eng.indirect_dma_start(dst[b][:, t, :], None, tab[:, :],
                                               bass.IndirectOffsetOnAxis(at[:, b, t:t + 1], 0)) \
                           .then_inc(s_gd[b], 16)
                skewed(eng, [(0, fetch_group)])

            def main(windows):
                if windows:
                    eng.wait_ge(s_srci, 1)
                    with eng.Fori(0, ROUNDS) as r:
                        eng.wait_ge(s_tw, r * 16 + 16)
                        fetches(r * NG, tabB_dram, g1, s_xr, ND0)
                    eng.wait_ge(s_tw, (ROUNDS + 1) * 16)
                    fetches(L1_BASE, tabH_dram, gx, s_tr, (ND, ND))
                else:
                    with eng.Fori(0, ROUNDS) as r:
                        spreads(r * NG, r * NG, q7d, Q7, 2 * HID)
                    spreads(L1_BASE, L1_BASE, q4d, Q4, 2 * F)
                if windows:
                    spreads7(L2_BASE)
                    spreads7(L3_BASE)
                else:
                    spreads(L2_BASE, L2_BASE, q4s, Q4, 2 * F)
                    spreads(L3_BASE, L3_BASE, q4s, Q4, 2 * F)

            near = flag_of(eng)
            with eng.If(near != 0):
                main(True)
            with eng.Else():
                main(False)

        @block.tensor
        def _(eng):
            eng.wait_ge(s_const, 2)
            eng.wait_ge(s_first, 1)
            eng.matmul(bank[4][:, 0:NG // 2], ones[0:1, :], first_f[:, :], start=True, stop=True).then_inc(s_fb, 1)

            def turn_array(a, src):
                eng.wait_ge(s_lohi, a + 1)
                if a >= 2:
                    eng.wait_ge(s_stage, 2 * (a - 1))
                for c in range(7):
                    w = min(128, T - 128 * c)
                    dst = bank[2 * (a % 2) + c // 4][0:w, (c % 4) * 128:(c % 4 + 1) * 128]
                    mm = eng.transpose(dst, src[:, 128 * c:128 * c + w], ident[:, :])
                    if c in (3, 6):
                        mm.then_inc(s_loht, 1)

            turn_array(0, rel)
            eng.wait_ge(s_bad, 1)
            eng.matmul(bank[5][0:1, 0:1], bad[:, 1:2], ones[:, 0:1], start=True, stop=True).then_inc(s_fb, 1)
            turn_array(1, lo_f)
            turn_array(2, hi_f)

            def count_group(g, b, pair):
                eng.wait_ge(s_coh, g + 1)
                for t in range(GT):
                    mm = eng.matmul(acc[1][:, 0:BLOCKS], ohm[b][:, t, 0:128], ohm[b][:, t, 128:128 + BLOCKS],
                                    start=isinstance(g, int) and g == 0 and t == 0,
                                    stop=isinstance(g, int) and g == NG - 1 and t == GT - 1)
                mm.then_inc(s_cmm, 1)
            count = [(1, count_group)]

            def dense(n, dense_in, w, spare=0, also=None):
                eng.wait_ge(s_di, n + (1 + spare))
                for k in range(4):
                    mm = eng.transpose(bank[0][0:112, k * ROWS:(k + 1) * ROWS],
                                       dense_in[:, 7 * k:7 * k + 7, :].rearrange("p j f -> p (j f)"),
                                       ident[0:ROWS, 0:ROWS])
                mm.then_inc(s_dt, 1)
                eng.wait_ge(s_dc, n + 1)
                o = 7 * w.shape[2]
                for k in range(4):
                    mm = eng.matmul(bank[1][0:ROWS, k * o:(k + 1) * o], dT[0:112, k * ROWS:(k + 1) * ROWS],
                                    w[:, :, :].rearrange("p j o -> p (j o)"), start=True, stop=True)
                if also is not None:
                    o = 7 * also.shape[2]
                    for k in range(4):
                        mm = eng.matmul(bank[3][0:ROWS, k * o:(k + 1) * o], dT[0:112, k * ROWS:(k + 1) * ROWS],
                                        also[:, :, :].rearrange("p j o -> p (j o)"), start=True, stop=True)
                mm.then_inc(s_dm, 1)

            def sums(n, nq, two_f, blocks):
                eng.wait_ge(s_ae, n + 1)
                for jj in range(blocks):
                    mm = eng.transpose(bank[2 + jj // 4][0:ROWS, (jj % 4) * nq * two_f:(jj % 4 + 1) * nq * two_f],
                                       accs[0:nq * two_f, jj * ROWS:(jj + 1) * ROWS],
                                       ident[0:nq * two_f, 0:nq * two_f])
                mm.then_inc(s_at, 1)

            def gathers(base, tabs, per_bank, slots, sbase, banks=(0, 1, 2, 3)):
                f = tabs[0].shape[3]
                inc = 4 // len(banks)
                views = [t[:, :, :, :].rearrange("p k (h c) f -> p k c h f", c=2) for t in tabs]

                def gather_group(g, b, pair):
                    for n, k in enumerate(banks):
                        at = n // 2 if len(tabs) == 2 else 0
                        slot = slots[at]
                        if n % 2 == 0:
                            eng.wait_ge(s_oh[slot], sbase + g + 1)
                        if isinstance(g, int) and g == 0:
                            if k == 0 and isinstance(base, int):
                                eng.wait_ge(s_red, base * 4)
                        else:
                            eng.wait_ge(s_red, (base + g) * 4 + (inc * (n + 1) - 4))
                        for t in range(per_bank):
                            tile = (n * per_bank + t) % GT
                            for c in range(2):
                                for p in range(2):
                                    mm = eng.matmul(bank[k][:, t * HI * f:(t + 1) * HI * f],
                                                    oh[slot][b][:, c, tile * 128:(tile + 1) * 128],
                                                    views[at][:, p, c, :, :],
                                                    start=(c == 0 and p == 0), stop=(c == 1 and p == 1))
                        mm.then_inc(s_gat, inc)
                return gather_group

            def b_tile(b, at, bank_cols):
                view = tabB[:, :, :, :].rearrange("p k (h c) f -> p k c h f", c=2)
                for c in range(2):
                    for p in range(2):
                        mm = eng.matmul(bank_cols, oh[1][b][:, c, at * 128:(at + 1) * 128], view[:, p, c, :, :],
                                        start=(c == 0 and p == 0), stop=(c == 1 and p == 1))
                return mm

            def rest_gathers(base, tab, per_bank, banks_of, more=(0, 0)):
                f = tab.shape[3]
                view = tab[:, :, :, :].rearrange("p k (h c) f -> p k c h f", c=2)

                def gather_group(g, b, pair):
                    eng.wait_ge(s_oh[1], base + g + 1)
                    wait_reuse(eng, s_red, base, g, 4)
                    for n, k in enumerate(banks_of(b)):
                        for t in range(per_bank):
                            at = more[b] + n * per_bank + t
                            for c in range(2):
                                for p in range(2):
                                    mm = eng.matmul(bank[k][:, t * HI * f:(t + 1) * HI * f],
                                                    oh[1][b][:, c, at * 128:(at + 1) * 128], view[:, p, c, :, :],
                                                    start=(c == 0 and p == 0), stop=(c == 1 and p == 1))
                        mm.then_inc(s_gat, 4 * per_bank // NP)
                return gather_group

            def window_turns(table_done, free, fbase, per, two_f, turned=False):
                def window_group(g, b, pair):
                    if b:
                        return
                    start = start_of(eng, pair)
                    if isinstance(g, int) and g == 0:
                        eng.wait_ge(s_td, table_done * 4)
                    gather_read(eng, free, fbase, g, per, turned)
                    eng.matmul(bank[0][:, 0:two_f], tab_w[0:two_f, bass.ds(start, WIN)],
                               ident16b[0:two_f, 0:two_f], start=True, stop=True).then_inc(s_wt, 2)
                return window_group

            def window_gathers(xbase, f, free, fbase, per, turned=False, more=(0, 0)):
                def gather_group(g, b, pair):
                    eng.wait_ge(s_wc, xbase + g + (2 - b))
                    eng.wait_ge(s_oh[0], xbase + g + 1)
                    if b:
                        gather_read(eng, free, fbase, g, per, turned)
                    for t in range(GT):
                        for p in range(2):
                            mm = eng.matmul(bank[b][:, t * f:(t + 1) * f], oh[0][b][:, 0, t * 128:(t + 1) * 128],
                                            win[pair[1]][:, p * f:(p + 1) * f], start=p == 0, stop=p == 1)
                    if more[b]:
                        mm = b_tile(b, 0, bank[b][:, MORE_AT:MORE_AT + HI * HID])
                    mm.then_inc(s_xg, 1)
                return gather_group

            def window_scatters(base, p0, m):
                def scatter_group(g, b, pair):
                    eng.wait_ge(s_om, base + g + 1)
                    eng.wait_ge(s_lo, base + g + 1)
                    if not b:
                        wait_reuse(eng, s_ac, base, g, 1, 3)
                    for t in range(GT):
                        mm = eng.matmul(acc[pair[1]][0:m, 0:WIN], parts[b][:, t, p0:p0 + m], ohm[b][:, t, 0:WIN],
                                        start=b == 0 and t == 0, stop=b == 1 and t == GT - 1)
                    mm.then_inc(s_sc, 1)
                return scatter_group

            def window_table(k, tab, f):
                for c in range(4):
                    for jj in range(7):
                        src = by_block(tab)[0:ROWS, 7 * c + jj, :, :].rearrange("p k f -> p (k f)")
                        mm = eng.transpose(bank[c][0:2 * f, jj * 57:(jj + 1) * 57].bitcast(fp16), src,
                                           ident16b[0:ROWS, 0:ROWS])
                    mm.then_inc(s_tt, 1)

            def window_sums(done, m):
                eng.wait_ge(s_ac, done)
                per = 512 // m
                for j in range(BLOCKS):
                    to = bank[2 + j // per][0:ROWS, (j % per) * m:(j % per + 1) * m]
                    block = sums_w[0:m, j * ROWS:(j + 1) * ROWS]
                    mm = (eng.transpose(to, block, ident[0:m, 0:m]) if j else
                          eng.matmul(to, block, ident[0:m, 0:m], start=True, stop=True))
                mm.then_inc(s_at, 1)

            def scatters(base, sbase, m, span):
                def scatter_group(g, b, pair):
                    eng.wait_ge(s_om, base + g + 1)
                    eng.wait_ge(s_sp, sbase + g + 1)
                    first = isinstance(g, int) and g == 0
                    last = isinstance(g, int) and g == NG - 1
                    for t in range(GT):
                        for a in range(-(-span // SPAN7)):
                            lo, hi = a * SPAN7, min(span, (a + 1) * SPAN7)
                            mm = eng.matmul(acc[a][0:m, 0:hi - lo], spread[b][:, t, 0:m], ohm[b][:, t, lo:hi],
                                            start=first and t == 0, stop=last and t == GT - 1)
                    mm.then_inc(s_sc, 1)
                return scatter_group

            def scatters7(base, sbase):
                def scatter_group(g, b, pair):
                    eng.wait_ge(s_om, base + g + 1)
                    eng.wait_ge(s_sp, sbase + g + 1)
                    first = isinstance(g, int) and g == 0
                    last = isinstance(g, int) and g == NG - 1
                    for t in range(GT):
                        for p in range(2):
                            mm = eng.matmul(acc[p][0:Q7 * F, 0:SPAN7],
                                            spread7[b][:, t, p, :, :].rearrange("p q f -> p (q f)"),
                                            ohm[b][:, t, 0:SPAN7],
                                            start=first and t == 0, stop=last and t == GT - 1)
                    mm.then_inc(s_sc, 1)
                return scatter_group

            def sums7(n):
                eng.wait_ge(s_ae, n + 1)
                for p in range(2):
                    for j in range(BLOCKS // Q7):
                        mm = eng.transpose(bank[2 + p][0:ROWS, j * Q7 * F:(j + 1) * Q7 * F],
                                           accs[0:Q7 * F, p * SPAN7 + j * ROWS:p * SPAN7 + (j + 1) * ROWS],
                                           ident[0:Q7 * F, 0:Q7 * F])
                mm.then_inc(s_at, 1)

            def turns(base, cols, src, ready, per, bank_free, fetched=False, to=ybank):
                def turn_group(g, b, pair):
                    eng.wait_ge(ready, (base + g + 1) * per)
                    if fetched:
                        eng.wait_ge(s_gd[b], fetched_by(base, g, b))
                    bank_free(g)
                    eng.transpose(to[b][0:cols, 384:512], src(b), ident[:, :]).then_inc(s_tr, 1)
                return turn_group

            def z_read(base):
                return lambda g: wait_reuse(eng, s_hi, base, g, 1)

            def y_read(ybase, n):
                def free(g):
                    if ybase or not (isinstance(g, int) and g == 0):
                        eng.wait_ge(s_yr, g * n + ybase)
                return free

            def z_of(base):
                def z_group(g, b, pair):
                    eng.wait_ge(s_tc, base + g + 1)
                    wait_reuse(eng, s_hi, base, g, 1)
                    k = GT * HID
                    eng.matmul(ybank[b][:, 0:k], tT[b][0:k + 1, :],
                               bd_e[0:k + 1, :, :].rearrange("p t o -> p (t o)"),
                               start=True, stop=True).then_inc(s_z, 1)
                return z_group

            def y_of(base, ybase, w, k, per, to=ybank):
                def y_group(g, b, pair):
                    eng.wait_ge(s_tc, base + g + 1)
                    n = GT // per
                    for c in range(n):
                        at = g * n + c
                        if len(to) == 2:
                            if c >= 2:
                                eng.wait_ge(s_yr, at + (ybase - 1))
                        elif ybase or not (isinstance(g, int) and g == 0):
                            eng.wait_ge(s_yr, at + (ybase - 3))
                        eng.matmul(to[c % len(to)][:, 0:per * k * F], tT[b][:, :],
                                   w[:, c * per:(c + 1) * per, :].rearrange("p t o -> p (t o)"),
                                   start=True, stop=True).then_inc(s_y, 1)
                return y_group

            nd = ROUNDS * DENSE_PER_ROUND
            turn16 = lambda b: gx[b][:, :, :].rearrange("p t f -> p (t f)")

            def main(windows):
                if not windows:
                    turn_array(3, lo_f)
                    turn_array(4, hi_f)
                    skewed(eng, count)
                eng.wait_ge(s_w, s_w_all[0])
                eng.wait_ge(s_wy, 4 * GT * 16)
                with eng.Fori(0, ROUNDS) as r:
                    d = r * DENSE_PER_ROUND
                    base = r * NG
                    dense(d, Hn, bd_ab, 0, bd_x1)
                    eng.wait_ge(s_rx, r * 2 + 1)
                    eng.transpose(bank[2][0:1, 0:128], amax[:, 0:1], ident[:, :]).then_inc(s_rt, 1)
                    eng.wait_ge(s_rx, r * 2 + 2)
                    eng.matmul(bank[2][:, 128:129], ones[0:1, :], top1[:, :], start=True,
                               stop=True).then_inc(s_rt, 1)
                    eng.wait_ge(s_tab, r + 1)
                    middle = (turns(base, GT * HID + 1, lambda b: h1[b][:, :], s_in, 1, z_read(base)), z_of(base))
                    if windows:
                        window_table(r, tabA, HID)
                        skewed(eng, [(0, window_turns(r + 1, s_xr, base, 1, 2 * HID)),
                                     (0, rest_gathers(base, tabB, 4, lambda b: (2 + b,), (0, 1))),
                                     (0, window_gathers(base, HID, s_xr, base, 1, False, (0, 1))), (1, middle[0]),
                                     (3, window_scatters(base, P9, 2 * HID + 1)), (1, middle[1])])
                        window_sums((r + 1) * NG, 2 * HID + 1)
                    else:
                        skewed(eng, [(0, gathers(base, (tabA, tabB), 4, (0, 1), base)), (1, middle[0]),
                                     (3, scatters(base, base, Q7 * 2 * HID, SPAN7)), (1, middle[1])])
                        sums(r, Q7, 2 * HID, BLOCKS // Q7)
                    dense(d + 1, S, bd_m)
                    dense(d + 2, U, bd_m1)
                    dense(d + 3, V, bd_2)
                    dense(d + 4, U, bd_3)
                eng.wait_ge(s_tab, ROUNDS + 1)
                skewed(eng, [(0, rest_gathers(L1_BASE, tabH, 2, lambda b: (2 * b, 2 * b + 1)) if windows else
                              gathers(L1_BASE, (tabH,), 2, (0,), L1_BASE)),
                             (1, turns(L1_BASE, 128, turn16, s_red, 4, y_read(0, 2), windows)),
                             (3, window_scatters(L1_BASE, 0, 2 * F) if windows else
                              scatters(L1_BASE, L1_BASE, Q4 * 2 * F, SPAN4)),
                             (1, y_of(L1_BASE, 0, bd_y1, K1, 4))])
                if windows:
                    window_sums(L1_BASE + NG, 2 * F)
                else:
                    sums(ROUNDS, Q4, 2 * F, BLOCKS // Q4)
                dense(nd, Hn, bd_root, 1)
                for k in range(2):
                    eng.wait_ge(s_bn, k + 1)
                    eng.matmul(bank[1][0:ROWS, 0:F], ones[0:ROWS, 0:ROWS], cs[:, :], start=True,
                               stop=True).then_inc(s_bm, 1)
                eng.wait_ge(s_tab, ROUNDS + 2)
                if windows:
                    middle = (turns(L2_BASE, 128, turn16, s_red, 4, lambda g: None, False, bank[0:2]),
                              y_of(L2_BASE, Y2_BASE, bd_y2, K2, 2, ybank4))
                    window_table(ROUNDS, tabH, F)
                    skewed(eng, [(2, middle[0]), (1, window_gathers(L1_BASE, F, s_red, L2_BASE, 4, True)),
                                 (0, window_turns(ROUNDS + 1, s_red, L2_BASE, 4, 2 * F, True)), (2, middle[1]), (4, scatters7(L2_BASE, 0))])
                    sums7(0)
                else:
                    middle = (turns(L2_BASE, 128, turn16, s_red, 4, y_read(Y2_BASE, 4)),
                              y_of(L2_BASE, Y2_BASE, bd_y2, K2, 2))
                    skewed(eng, [(0, gathers(L2_BASE, (tabH,), 2, (0,), L2_BASE)), (1, middle[0]),
                                 (3, scatters(L2_BASE, L2_BASE, Q4 * 2 * F, SPAN4)), (1, middle[1])])
                    sums(ROUNDS + 1, Q4, 2 * F, BLOCKS // Q4)
                eng.wait_ge(s_tab, ROUNDS + 3)
                if windows:
                    window_table(ROUNDS + 1, tabH, F)
                    skewed(eng, [(0, window_turns(ROUNDS + 2, s_red, L3_BASE, 4, 2 * F)),
                                 (1, window_gathers(L2_BASE, F, s_red, L3_BASE, 4)),
                                 (3, scatters7(L3_BASE, NG))])
                    sums7(1)
                else:
                    skewed(eng, [(0, gathers(L3_BASE, (tabH,), 2, (0,), L3_BASE)),
                                 (3, scatters(L3_BASE, L3_BASE, Q4 * 2 * F, SPAN4))])
                    sums(ROUNDS + 2, Q4, 2 * F, BLOCKS // Q4)

            near = flag_of(eng)
            with eng.If(near != 0):
                main(True)
            with eng.Else():
                main(False)

            of = outer.rearrange("p j u v -> p j (u v)")
            for k in range(HI + 1):
                if k < HI:
                    eng.wait_ge(s_uo, k + 1)
                    if k >= 2:
                        eng.wait_ge(s_oc[k % 2], k // 2)
                    for c in range(4):
                        mm = eng.transpose(bank[k % 2][:, c * ROWS:(c + 1) * ROWS],
                                           of[:, 2 * k + c // 2, (c % 2) * 128:(c % 2 + 1) * 128],
                                           ident[0:ROWS, 0:ROWS])
                    mm.then_inc(s_ot, 1)
                if k >= 1:
                    eng.wait_ge(s_oc[(k - 1) % 2], (k + 1) // 2)
                    for c in range(2):
                        j = 2 * (k - 1) + c
                        for half in range(2):
                            at = (2 * c + half) * ROWS
                            mm = eng.matmul(bank[4][0:ROWS, j * F:(j + 1) * F], (dT, accs)[(k - 1) % 2][:, at:at + ROWS],
                                            wt[:, half, :], start=half == 0, stop=half == 1)
                    mm.then_inc(s_om2, 1)
            dense(nd + 1, U, bd_out, 1)

        @block.scalar
        def _(eng):
            def stage_array(a):
                for h in range(2):
                    eng.wait_ge(s_loht, 2 * a + h + 1)
                    if a >= 2 and h == 0:
                        eng.wait_ge(s_scr, 32 * (a - 1))
                    w, rows = ((512, 128), (256, 128))[h]
                    copied = eng.activation(stage[0:rows, a % 2, 512 * h:512 * h + w],
                                            bank[2 * (a % 2) + h][0:rows, 0:w], ACT.Copy)
                    if h:
                        copied = eng.activation(stage[0:T - 768, a % 2, 768:896],
                                                bank[2 * (a % 2) + h][0:T - 768, 256:384], ACT.Copy)
                    copied.then_inc(s_stage, 1)

            for a in range(COMMON_ARRAYS):
                stage_array(a)

            def dense(n):
                eng.wait_ge(s_dt, n + 1)
                eng.activation(dT[0:112, 0:4 * ROWS], bank[0][0:112, 0:4 * ROWS], ACT.Copy).then_inc(s_dc, 1)

            def sums(n, done, m, span):
                eng.wait_ge(s_sc, done)
                if span == SPAN7:
                    eng.activation(accs[0:m, 0:span], acc[0][0:m, 0:span], ACT.Copy).then_inc(s_ae, 1)
                else:
                    eng.activation(accs[0:m, 0:SPAN7], acc[0][0:m, 0:SPAN7], ACT.Copy)
                    eng.activation(accs[0:m, SPAN7:span], acc[1][0:m, 0:span - SPAN7], ACT.Copy).then_inc(s_ae, 1)

            def sums7(done):
                eng.wait_ge(s_sc, done)
                eng.activation(accs[0:Q7 * F, 0:SPAN7], acc[0][0:Q7 * F, 0:SPAN7], ACT.Copy)
                eng.activation(accs[0:Q7 * F, SPAN7:2 * SPAN7], acc[1][0:Q7 * F, 0:SPAN7],
                               ACT.Copy).then_inc(s_ae, 1)

            def root_of(n, view):
                eng.wait_ge(s_var, n + 1)
                eng.activation(view, view, ACT.Sqrt, bias=eps_t[0:ROWS, :], scale=1.0).then_inc(s_std, 1)

            def turned(base, cols, reader, rbase, per, src=ybank):
                def copy_group(g, b, pair):
                    eng.wait_ge(s_tr, base + g + 1)
                    wait_reuse(eng, reader, rbase, g, per)
                    eng.activation(tT[b][0:cols, :], src[b][0:cols, 384:512], ACT.Copy).then_inc(s_tc, 1)
                return copy_group

            def z_parts(base, used):
                def parts_group(g, b, pair):
                    eng.wait_ge(s_z, base + g + 1)
                    used(g)
                    z = ybank[b][:, 0:GT * HID].rearrange("p (t f) -> p t f", f=HID)
                    eng.activation(zr[b][:, :, :], z, ACT.Relu, scale=sc[:, 2:3])
                    eng.activation(parts[b][:, :, P9:P9 + HID], z, ACT.Relu, scale=sc[:, 2:3]).then_inc(s_hi, 1)
                return parts_group

            def y_bias(ybase, k, per, banks=ybank):
                def bias_group(g, b, pair):
                    n = GT // per
                    for c in range(n):
                        at = g * n + c
                        eng.wait_ge(s_y, at + (ybase + 1))
                        if not (isinstance(g, int) and g == 0):
                            eng.wait_ge(s_msg, g + (ybase // 2))
                        elif ybase:
                            eng.wait_ge(s_msg, ybase // 2)
                        y = banks[c % len(banks)][:, 0:per * k * F].rearrange("p (t k o) -> p t k o", k=k, o=F)
                        eng.activation(yw[:, c * per:(c + 1) * per, k - 1, :], y[:, :, k - 1, :],
                                       ACT.Copy).then_inc(s_yb, 1)
                return bias_group

            def hi_parts(src, ready, rbase, per, scale, used):
                def hi_group(g, b, pair):
                    eng.wait_ge(ready, (rbase + g + 1) * per)
                    used(g)
                    eng.activation(parts[b][:, :, 0:F], src[b][:, :, :], ACT.Copy, scale=scale).then_inc(s_hi, 1)
                return hi_group

            def window_copies(xbase, two_f):
                def copy_group(g, b, pair):
                    if b:
                        return
                    eng.wait_ge(s_wt, xbase + g + 2)
                    wait_reuse(eng, s_xg, xbase, g, 1, 3)
                    eng.activation(win[pair[1]][:, 0:two_f], bank[0][:, 0:two_f], ACT.Copy).then_inc(s_wc, 2)
                return copy_group

            def gathered_copies(xbase, base, reader):
                def copy_group(g, b, pair):
                    eng.wait_ge(s_xg, xbase + g + 1)
                    wait_reuse(eng, reader, base, g, 1)
                    eng.activation(gx[b][:, :, :], bank[b][:, 0:GT * F].rearrange("p (t f) -> p t f", f=F),
                                   ACT.Copy).then_inc(s_red, 4)
                return copy_group

            def window_table(k, two_f):
                for c in range(4):
                    eng.wait_ge(s_tt, 4 * k + (c + 1))
                    eng.activation(tab_w[0:two_f, 7 * c * ROWS:7 * (c + 1) * ROWS],
                                   bank[c][0:two_f, 0:7 * ROWS // 2].bitcast(fp16), ACT.Copy).then_inc(s_td, 1)

            def store_table(k, tab, src):
                eng.wait_ge(s_tf, k + 1)
                view = tab.rearrange("(j r) f -> r j f", r=ROWS)
                eng.dma_start(view, src).then_inc(s_tw, 16)

            def used_by(sm, base):
                return lambda g: wait_reuse(eng, sm, base, g, 1)

            nd = ROUNDS * DENSE_PER_ROUND

            def main(windows):
                if not windows:
                    for a in range(COMMON_ARRAYS, ARRAYS):
                        stage_array(a)
                root_of(0, st2[:, :])
                with eng.Fori(0, ROUNDS) as r:
                    base = r * NG
                    dense(r * DENSE_PER_ROUND)
                    turn = turned(base, GT * HID + 1, s_z, base, 1)
                    if windows:
                        store_table(r, tabB_dram, AB[:, :, HID:2 * HID])
                        window_table(r, 2 * HID)
                        skewed(eng, [(0, window_copies(base, 2 * HID)), (1, turn),
                                     (1, z_parts(base, used_by(s_sc, base)))])
                    else:
                        skewed(eng, [(0, turn), (0, z_parts(base, used_by(s_sp, base)))])
                        sums(r, (r + 1) * NG, Q7 * 2 * HID, SPAN7)
                    for c in range(1, DENSE_PER_ROUND):
                        dense(r * DENSE_PER_ROUND + c)
                root_of(1, st2[:, :])
                if windows:
                    store_table(ROUNDS, tabH_dram, V[:, :, :])
                skewed(eng, [(0, turned(L1_BASE, 128, s_y, 0, 2)), (0, y_bias(0, K1, 4)),
                             (0, hi_parts(msg, s_msg, 0, 1, sc[:, 4:5],
                                          used_by(s_sc if windows else s_sp, L1_BASE)))])
                if not windows:
                    sums(ROUNDS, L1_BASE + NG, 128, SPAN4)
                dense(nd)
                root_of(2, cm[:, :])
                root_of(3, st2[:, :])
                sbase = 0 if windows else L2_BASE
                turn = turned(L2_BASE, 128, s_y, Y2_BASE // 4, 4, bank[0:2] if windows else ybank)
                hi = hi_parts(msg, s_msg, NG, 1, sc[:, 6:7], used_by(s_sp, sbase))
                if windows:
                    window_table(ROUNDS, 2 * F)
                    skewed(eng, [(2, turn), (1, gathered_copies(L1_BASE, L2_BASE, s_tr)),
                                 (0, window_copies(L1_BASE, 2 * F)), (2, y_bias(Y2_BASE, K2, 2, ybank4)), (2, hi)])
                else:
                    skewed(eng, [(0, turn), (0, y_bias(Y2_BASE, K2, 2)), (0, hi)])
                if windows:
                    sums7(L2_BASE + NG)
                else:
                    sums(ROUNDS + 1, L2_BASE + NG, 128, SPAN4)
                root_of(4, st2[:, :])
                hi = hi_parts(gx, s_red, L3_BASE, 4, 1.0, used_by(s_sp, sbase + NG))
                if windows:
                    window_table(ROUNDS + 1, 2 * F)
                    skewed(eng, [(0, window_copies(L2_BASE, 2 * F)), (1, gathered_copies(L2_BASE, L3_BASE, s_lo)),
                                 (1, hi)])
                else:
                    skewed(eng, [(0, hi)])
                if windows:
                    sums7(L3_BASE + NG)
                else:
                    sums(ROUNDS + 2, L3_BASE + NG, 128, SPAN4)

            near = flag_of(eng)
            with eng.If(near != 0):
                main(True)
            with eng.Else():
                main(False)

            for k in range(0, HI, 2):
                eng.wait_ge(s_ot, k + 1)
                if k >= 2:
                    eng.wait_ge(s_om2, k - 1)
                eng.activation(dT[:, 0:4 * ROWS], bank[0][:, 0:4 * ROWS], ACT.Copy).then_inc(s_oc[0], 1)
            dense(nd + 1)

        @block.vector
        def _(eng):
            chained = [0]
            chain_base = [0]

            def link(ins):
                chained[0] += 1
                ins.then_inc(s_v, 1)
                eng.wait_ge(s_v, chain_base[0] + chained[0])

            def bcj(v):
                return v[:, :].unsqueeze(2).broadcast_to([ROWS, BLOCKS, F])

            def bcf(v, f=F):
                return v[:, 0:f].unsqueeze(1).broadcast_to([ROWS, BLOCKS, f])

            for t in (bd_ab, bd_m, bd_x1, bd_m1, bd_2, bd_3, bd_root, bd_out, bd_e, bd_y1, bd_y2, X, U, V, S):
                eng.memset(t[:, :, :], 0.0)
            for t in (ea4, ea8):
                eng.memset(t[:, FULL * GT:T, :], 0.0)
            for b in range(2):
                eng.memset(h1[b][:, GT * HID:GT * HID + 1], 1.0)
            eng.memset(ones[:, :], 1.0)
            eng.memset(eps_t[:, :], EPS)
            eng.memset(amax[:, :], 0.0).then_inc(s_w0, 1)

            eng.wait_ge(s_iota, 3)
            eng.tensor_copy(iota_m[:, :], iota_i[:, :])
            eng.tensor_copy(iota_f[:, :], iota_i[:, 0:128])
            eng.tensor_scalar(nmask[:, :], nmask_i[:, :], float(N), None, ALU.is_lt)
            link(eng.tensor_copy(part_f[:, :], part_i[:, :]))
            link(eng.tensor_scalar(past[:, :], part_f[:, :], float(ROWS), None, ALU.is_ge))
            link(eng.scalar_tensor_tensor(pv[:, 0:1], past[:, :], -float(ROWS), part_f[:, :], ALU.mult, ALU.add))
            link(eng.tensor_scalar(past[:, :], past[:, :], -float(ROWS), float(ROWS), ALU.mult, ALU.add))
            link(eng.tensor_tensor(pv[:, 1:2], past[:, :], pv[:, 0:1], ALU.add))

            ROUND = 1.5 * 2.0 ** 23

            def split(n, width, q, m):
                link(eng.tensor_scalar(q, n, 1.0 / width, 0.5 / width - 0.5, ALU.mult, ALU.add))
                link(eng.tensor_scalar(q, q, ROUND, -ROUND, ALU.add, ALU.add))
                return eng.scalar_tensor_tensor(m, q, -float(width), n, ALU.mult, ALU.add)

            def mask_of(out_ap, q, n):
                return eng.tensor_tensor(out_ap, q.unsqueeze(2).broadcast_to([128, T, n]),
                                         iota_f[:, 0:n].unsqueeze(1).broadcast_to([128, T, n]), ALU.is_equal)

            eng.wait_ge(s_idx, 96)
            link(eng.tensor_copy(idx_f[0], idx_i[0]))
            eng.tensor_copy(idx_f[1], idx_i[1])
            link(eng.tensor_scalar(first_f[:, :], idx_f[0][0:1, :].rearrange("p (g t) -> p g t", t=2 * GT)[:, :, 0],
                                   float(WIDTH - WIN), None, ALU.min))
            eng.tensor_copy(first_i[:, :], first_f[:, :]).then_inc(s_first, 1)
            eng.wait_ge(s_fb, 1)
            link(eng.tensor_copy(first_b[:, :], bank[4][:, 0:NG // 2]))
            grouped = lambda v: v.rearrange("p (g t) -> p g t", t=2 * GT)
            eng.tensor_tensor(grouped(rel[:, :]), grouped(idx_f[0]),
                              first_b[:, :].unsqueeze(2).broadcast_to([128, NG // 2, 2 * GT]),
                              ALU.subtract).then_inc(s_lohi, 1)
            eng.wait_ge(s_lohi, 1)
            link(eng.tensor_scalar(qf, idx_f[0], float(N), None, ALU.is_lt))
            link(eng.scalar_tensor_tensor(lo_f, rel[:, :], float(WIN), qf, ALU.is_ge, ALU.mult))
            link(eng.scalar_tensor_tensor(lo_f, rel[:, :], 0.0, lo_f, ALU.is_lt, ALU.add))
            eng.tensor_reduce(bad[:, 1:2], lo_f, AX.X, ALU.add).then_inc(s_bad, 1)
            eng.wait_ge(s_fb, 2)
            link(eng.tensor_scalar(bad1[:, :], bank[5][0:1, 0:1], 0.5, None, ALU.is_lt))
            eng.tensor_copy(flag[:, :], bad1[:, :]).then_inc(s_flag, 1)
            split(idx_f[1], 2 * ROWS, hi_f, lo_f).then_inc(s_lohi, 2)

            def count_group(g, b, pair):
                wait_reuse(eng, s_cmm, 0, g, 1)
                for t in range(GT):
                    eng.tensor_scalar(ohm[b][:, t, 0:128], iota_m[:, 0:128], rd[:, bass.ds(g * GT + t, 1)], None,
                                      ALU.is_equal)
                eng.tensor_tensor(ohm[b][:, :, 128:128 + BLOCKS],
                                  jd[:, bass.ds(g * GT, GT)].unsqueeze(2).broadcast_to([128, GT, BLOCKS]),
                                  iota_f[:, 0:BLOCKS].unsqueeze(1).broadcast_to([128, GT, BLOCKS]),
                                  ALU.is_equal).then_inc(s_coh, 1)

            def destinations():
                link(split(idx_f[1], SPAN4, qf, m4s[:, :]))
                link(mask_of(q4s[:, :, :], qf, Q4))
                eng.wait_ge(s_loht, 2 * COMMON_ARRAYS)
                split(idx_f[0], 2 * ROWS, hi_f, lo_f).then_inc(s_lohi, 2)
                link(split(idx_f[0], SPAN7, qf, m7d[:, :]))
                link(mask_of(q7d[:, :, :], qf, Q7))
                link(split(idx_f[0], ROWS, jd[:, :], rd[:, :]))
                link(split(idx_f[0], SPAN4, qf, m4d[:, :]))
                link(mask_of(q4d[:, :, :], qf, Q4))
                skewed(eng, [(0, count_group)])
                eng.wait_ge(s_cmm, NG)
                link(eng.tensor_copy(cnt[:, :], acc[1][0:ROWS, 0:BLOCKS]))

            def reciprocal_count():
                link(eng.tensor_scalar(rcnt[:, :], cnt[:, :], 1.0, None, ALU.max))
                link(eng.reciprocal(rcnt[:, :], rcnt[:, :]))

            def power(at, src, top, more=1.0):
                s, inv = sc[:, at:at + 1], sc[:, at + 1:at + 2]
                link(eng.tensor_scalar(inv, src, 2.0 ** -60, None, ALU.max))
                link(eng.tensor_scalar(inv.bitcast(i32), inv.bitcast(i32), 0x7F800000, None, ALU.bitwise_and))
                link(eng.reciprocal(s, inv))
                link(eng.tensor_scalar(s, s, top, None, ALU.mult))
                link(eng.tensor_scalar(inv, inv, more / top, None, ALU.mult))

            def message_scales():
                eng.wait_ge(s_w, s_w_all[0])
                eng.wait_ge(s_wy, 4 * GT * 16)
                for c, t in ((0, bd_e), (1, bd_y1), (2, bd_y2), (3, ea4), (4, ea8)):
                    ins = eng.tensor_reduce(amax[:, c:c + 1], t[:, :, :], AX.XY, ALU.max, apply_absolute_value=True)
                ins.then_inc(s_mx, 1)
                eng.wait_ge(s_ma, 1)
                link(eng.tensor_copy(wmax[:, :], aall[:, :]))
                link(eng.memset(amax[:, :], 0.0))
                for at, w, e, k in ((4, 1, 3, K1), (6, 2, 4, K2)):
                    link(eng.tensor_scalar(wmax[:, e:e + 1], wmax[:, e:e + 1], 1.0, F * 4.0 * k * H_SCALE, ALU.max,
                                           ALU.mult))
                    link(eng.tensor_tensor(wmax[:, e:e + 1], wmax[:, e:e + 1], wmax[:, w:w + 1], ALU.mult))
                    power(at, wmax[:, e:e + 1], PART_TOP, 1.0 / H_SCALE)

            norms = [0]

            def norm():
                link(eng.tensor_reduce(st1[:, :], X[:, :, :], AX.X, ALU.add))
                link(eng.tensor_scalar(st1[:, :], st1[:, :], 1.0 / F, None, ALU.mult))
                link(eng.tensor_tensor(Hn[:, :, :], X[:, :, :], bcj(st1), ALU.subtract))
                link(eng.tensor_tensor(W[:, :, :], Hn[:, :, :], Hn[:, :, :], ALU.mult))
                link(eng.tensor_reduce(st2[:, :], W[:, :, :], AX.X, ALU.add))
                eng.tensor_scalar(st2[:, :], st2[:, :], 1.0 / F, None, ALU.mult).then_inc(s_var, 1)
                norms[0] += 1
                eng.wait_ge(s_std, norms[0])
                link(eng.reciprocal(st2[:, :], st2[:, :]))
                link(eng.tensor_tensor(Hn[:, :, :], Hn[:, :, :], bcj(st2), ALU.mult))
                return eng.tensor_scalar(Hn[:, :, :], Hn[:, :, :], 0.0, None, ALU.max)

            def table(tab, src, scale, to_turn=False):
                hi, lo = [by_block(tab)[0:ROWS, :, k, :] if to_turn else tab[0:ROWS, k, :, :] for k in range(2)]
                link(eng.tensor_scalar(hi, src, scale, None, ALU.mult))
                return eng.scalar_tensor_tensor(lo, src, scale, hi, ALU.mult, ALU.subtract)

            def onehots(base, slot, reader, rbase, per, skips=(0, 0)):
                def onehot_group(g, b, pair):
                    w = EC - skips[b] * 128
                    eng.wait_ge(s_bc[slot][b], (base + g + (2 - b)) * 16)
                    wait_reuse(eng, reader, rbase, g, per)
                    for c in range(2):
                        ins = eng.tensor_scalar(oh[slot][b][:, c, 0:w], bc[slot][b][:, 0:w], pv[:, c:c + 1], None,
                                                ALU.is_equal)
                    ins.then_inc(s_oh[slot], 1)
                return onehot_group

            def window_onehots(xbase):
                def onehot_group(g, b, pair):
                    eng.wait_ge(s_bc[0][b], (xbase + g + (2 - b)) * 8)
                    wait_reuse(eng, s_xg, xbase, g, 1)
                    eng.tensor_scalar(oh[0][b][:, 0, :], bc[0][b][:, :], part_f[:, 0:1], None,
                                      ALU.is_equal).then_inc(s_oh[0], 1)
                return onehot_group

            def select(k, dst, per, f):
                view = bank[k][:, 0:per * HI * f].rearrange("p (t h f) -> p t f h", h=HI, f=f)
                return eng.tensor_reduce(dst, view, AX.X, ALU.max)

            def rest_select9(base):
                def select_group(g, b, pair):
                    eng.wait_ge(s_gat, (base + g + 1) * 4)
                    ins = select(2 + b, g1[b][:, ND:GT, :], NP, HID)
                    if ND0[b] < ND:
                        eng.wait_ge(s_xg, base + g + 1)
                        view = bank[b][:, MORE_AT:MORE_AT + HI * HID].rearrange("p (h f) -> p f h", f=HID)
                        ins = eng.tensor_reduce(g1[b][:, ND - 1, :], view, AX.X, ALU.max)
                    ins.then_inc(s_red, 4)
                return select_group

            def both_sides(base):
                def add_group(g, b, pair):
                    eng.wait_ge(s_gd[b], fetched_by(base, g, b))
                    eng.wait_ge(s_red, (base + g + 1) * 4)
                    eng.wait_ge(s_xg, base + g + 1)
                    if not (isinstance(g, int) and g < 1):
                        eng.wait_ge(s_in, base + g)
                    eng.tensor_tensor(gs[:, :, :], bank[b][:, 0:GT * HID].rearrange("p (t f) -> p t f", f=HID),
                                      g1[b][:, :, :], ALU.add).then_inc(s_xr, 1)
                return add_group

            def hidden(base, done):
                def relu_group(g, b, pair):
                    eng.wait_ge(done, base + g + 1)
                    wait_reuse(eng, s_tr, base, g, 1)
                    eng.tensor_scalar(h1[b][:, 0:GT * HID], gs[:, :, :].rearrange("p t f -> p (t f)"), 0.0,
                                      sc[:, 1:2], ALU.max, ALU.mult).then_inc(s_in, 1)
                return relu_group

            def select9(base):
                def select_group(g, b, pair):
                    for k in range(4):
                        eng.wait_ge(s_gat, (base + g) * 4 + (k + 1))
                        select(k, (g0, g1[0])[k // 2][:, (k % 2) * 4:(k % 2) * 4 + 4, :], 4, HID).then_inc(s_red, 1)
                    eng.wait_ge(s_red, (base + g) * 4 + 4)
                    eng.tensor_tensor(gs[:, :, :], g0[:, :, :], g1[0][:, :, :], ALU.add).then_inc(s_gs, 1)
                return select_group

            def select16(base, reader, windows=False):
                def select_group(g, b, pair):
                    wait_reuse(eng, reader, base, g, 1)
                    for k in range(2 if windows else 4):
                        n = 2 if windows else 1
                        eng.wait_ge(s_gat, (base + g) * 4 + n * (k + 1))
                        at = (ND if windows else 0) + 2 * k
                        select((2 * b if windows else 0) + k, gx[b][:, at:at + 2, :], 2, F).then_inc(s_red, n)
                return select_group

            def message(base, ybase, mbase, ea, k, per, banks=ybank):
                def message_group(g, b, pair):
                    n = GT // per
                    wait_reuse(eng, s_hi, base, g, 1)
                    for c in range(n):
                        eng.wait_ge(s_yb, g * n + (c + ybase + 1))
                        y = banks[c % len(banks)][:, 0:per * k * F].rearrange("p (t k o) -> p t k o", k=k, o=F)
                        e = ea[:, bass.ds(g * GT + c * per, per), :].unsqueeze(3)
                        eng.tensor_tensor(yw[:, c * per:(c + 1) * per, 0:k - 1, :], y[:, :, 0:k - 1, :],
                                          e.broadcast_to([128, per, k - 1, F]), ALU.mult).then_inc(s_yr, 1)
                    eng.wait_ge(s_yr, g * n + (n + ybase))
                    eng.tensor_reduce(msg[b][:, :, :], yw[:, :, 0:k, :].rearrange("p t k o -> p t o k"), AX.X,
                                      ALU.add).then_inc(s_msg, 1)
                return message_group

            def low9(base):
                def low_group(g, b, pair):
                    eng.wait_ge(s_hi, base + g + 1)
                    eng.tensor_tensor(parts[b][:, :, P9 + HID:2 * F], zr[b][:, :, :], parts[b][:, :, P9:P9 + HID],
                                      ALU.subtract).then_inc(s_lo, 1)
                return low_group

            def low16(base, src, scale):
                def low_group(g, b, pair):
                    eng.wait_ge(s_hi, base + g + 1)
                    eng.scalar_tensor_tensor(parts[b][:, :, F:2 * F], src[b][:, :, :], scale,
                                             parts[b][:, :, 0:F], ALU.mult, ALU.subtract).then_inc(s_lo, 1)
                return low_group

            def onehot_m(base, m, span):
                def onehot_group(g, b, pair):
                    wait_reuse(eng, s_sc, base, g, 1)
                    for t in range(GT):
                        ins = eng.tensor_scalar(ohm[b][:, t, 0:span], iota_m[:, 0:span],
                                                m[:, bass.ds(g * GT + t, 1)], None, ALU.is_equal)
                    ins.then_inc(s_om, 1)
                return onehot_group

            def window_sum(base, m):
                def sum_group(g, b, pair):
                    if not b:
                        return
                    start = start_of(eng, pair)
                    if not (isinstance(g, int) and g == 1):
                        eng.wait_ge(s_ac, base + g - 1)
                    eng.wait_ge(s_sc, base + g + 1)
                    to = sums_w[0:m, bass.ds(start, WIN)]
                    eng.tensor_tensor(to, acc[pair[1]][0:m, 0:WIN], to, ALU.add).then_inc(s_ac, 2)
                return sum_group

            def window_sums(m, f, p0, inv):
                per = 512 // m
                for k in range(0, BLOCKS, per):
                    n = min(per, BLOCKS - k)
                    d = bank[2 + k // per][0:ROWS, 0:n * m].rearrange("p (j f) -> p j f", f=m)
                    link(eng.tensor_scalar(W[:, k:k + n, 0:f], d[:, :, 0:f], inv, None, ALU.mult))
                    ins = eng.scalar_tensor_tensor(S[:, k:k + n, 0:f], d[:, :, f:2 * f], inv, W[:, k:k + n, 0:f],
                                                   ALU.mult, ALU.add)
                    if m > 2 * f:
                        link(ins)
                        ins = eng.tensor_copy(cnt[:, k:k + n], d[:, :, 2 * f])
                return ins

            def sums(nq, f, inv):
                blocks = BLOCKS // nq
                to = S[:, :, :].rearrange("p (q j) f -> p j q f", j=blocks)
                tmp = W[:, :, :].rearrange("p (q j) f -> p j q f", j=blocks)
                for k in range(0, blocks, 4):
                    n = min(4, blocks - k)
                    d = bank[2 + k // 4][0:ROWS, 0:n * nq * 2 * f].rearrange("p (j q s f) -> p j q s f", q=nq,
                                                                             s=2, f=f)
                    for j in range(n):
                        ins = eng.tensor_scalar(tmp[:, k + j, :, 0:f], d[:, j, :, 0, :], inv, None, ALU.mult)
                    link(ins)
                    for j in range(n):
                        ins = eng.scalar_tensor_tensor(to[:, k + j, :, 0:f], d[:, j, :, 1, :], inv,
                                                       tmp[:, k + j, :, 0:f], ALU.mult, ALU.add)
                return ins

            def sums7(inv):
                to = S[:, :, :].rearrange("p (q j) f -> p j q f", j=BLOCKS // Q7)
                tmp = W[:, :, :].rearrange("p (j q) f -> p j q f", q=Q7)
                hi, lo = [bank[2 + p][0:ROWS, 0:BLOCKS * F].rearrange("p (j q f) -> p j q f", q=Q7, f=F)
                          for p in range(2)]
                link(eng.tensor_scalar(tmp, hi, inv, None, ALU.mult))
                for j in range(BLOCKS // Q7):
                    ins = eng.scalar_tensor_tensor(to[:, j, :, :], lo[:, j, :, :], inv, tmp[:, j, :, :],
                                                   ALU.mult, ALU.add)
                return ins

            def made(f):
                return bank[1][0:ROWS, 0:BLOCKS * f].rearrange("p (j f) -> p j f", f=f)

            prologue = chained[0]

            def main(windows):
                chained[0], norms[0] = prologue, 0
                if windows:
                    eng.wait_ge(s_loht, 2 * COMMON_ARRAYS)
                    link(split(idx_f[1], SPAN7, qf, ms[:, :]))
                    link(mask_of(q7s[:, :, :], qf, Q7))
                    link(eng.tensor_scalar(qf, idx_f[1], float(WIDTH - 1), None, ALU.min))
                    eng.tensor_copy(src_i, qf).then_inc(s_srci, 1)
                    eng.wait_ge(s_srci, 1)
                    link(eng.memset(sums_w, 0.0))
                    message_scales()
                else:
                    message_scales()
                    destinations()
                norm().then_inc(s_di, 1)
                before = chained[0]
                LINKS = 22 if windows else 19
                with eng.Fori(0, ROUNDS) as r:
                    chained[0] = 0
                    chain_base[0] = r * LINKS + before
                    d = r * DENSE_PER_ROUND
                    eng.wait_ge(s_dm, d + 1)
                    eng.tensor_tensor(AB[:, :, 0:HID], made(2 * HID)[:, :, 0:HID], bcf(bias["e1"], HID), ALU.add)
                    link(eng.tensor_copy(AB[:, :, HID:2 * HID], made(2 * HID)[:, :, HID:2 * HID]))
                    eng.tensor_reduce(amax[0:ROWS, 0:1], AB[:, :, :], AX.XY, ALU.max,
                                      apply_absolute_value=True).then_inc(s_rx, 1)
                    eng.tensor_tensor(V[:, :, 0:HID], bank[3][0:ROWS, 0:BLOCKS * HID].rearrange(
                        "p (j f) -> p j f", f=HID), bcf(bias["x1"], HID), ALU.add)
                    eng.wait_ge(s_rt, r * 2 + 1)
                    eng.tensor_reduce(top1[:, :], bank[2][0:1, 0:128], AX.X, ALU.max).then_inc(s_rx, 1)
                    eng.wait_ge(s_rt, r * 2 + 2)
                    power(0, bank[2][:, 128:129], TABLE_TOP)
                    link(eng.tensor_scalar(sc[:, 8:9], sc[:, 1:2], 4.0 * HID * TABLE_TOP, 1.0, ALU.mult, ALU.add))
                    link(eng.tensor_tensor(sc[:, 8:9], sc[:, 8:9], wmax[:, 0:1], ALU.mult))
                    power(2, sc[:, 8:9], PART_TOP)
                    scaled = AB[:, :, HID:2 * HID]
                    if windows:
                        eng.tensor_scalar(scaled, scaled, sc[0:ROWS, 0:1], None, ALU.mult).then_inc(s_tf, 1)
                        eng.wait_ge(s_tf, r + 1)
                    table(tabA, AB[:, :, 0:HID], sc[0:ROWS, 0:1], windows)
                    table(tabB, scaled, 1.0 if windows else sc[0:ROWS, 0:1]).then_inc(s_tab, 1)
                    base = r * NG
                    src_side = (onehots(base, 1, s_xg, base, 1, ND0) if windows else
                                onehots(base, 1, s_gat, base, 4))
                    if windows:
                        skewed(eng, [(1, rest_select9(base)), (0, src_side), (1, both_sides(base)),
                                     (0, window_onehots(base)), (1, hidden(base, s_xr)),
                                     (4, window_sum(base, 2 * HID + 1)),
                                     (2, low9(base)), (2, onehot_m(base, rel, WIN))])
                        eng.wait_ge(s_at, r + 1)
                        window_sums(2 * HID + 1, HID, P9, sc[0:ROWS, 3:4]).then_inc(s_di, 1)
                        eng.memset(sums_w, 0.0)
                        eng.wait_ge(s_di, d + 2)
                    else:
                        skewed(eng, [(0, onehots(base, 0, s_gat, base, 4)), (0, src_side),
                                     (1, select9(base)), (1, hidden(base, s_gs)), (2, low9(base)), (2, onehot_m(base, m7d, SPAN7))])
                        eng.wait_ge(s_at, r + 1)
                        sums(Q7, HID, sc[0:ROWS, 3:4]).then_inc(s_di, 1)
                    link(eng.tensor_tensor(AB[:, :, 0:HID], cnt[:, :].unsqueeze(2).broadcast_to([ROWS, BLOCKS, HID]),
                                           bcf(bias["e3"], HID), ALU.mult))
                    eng.wait_ge(s_dm, d + 2)
                    eng.tensor_tensor(U[:, :, 0:HID], made(HID), AB[:, :, 0:HID], ALU.add).then_inc(s_di, 1)
                    eng.wait_ge(s_dm, d + 3)
                    link(eng.tensor_tensor(V[:, :, 0:HID], made(HID), V[:, :, 0:HID], ALU.add))
                    eng.tensor_scalar(V[:, :, 0:HID], V[:, :, 0:HID], 0.0, None, ALU.max).then_inc(s_di, 1)
                    eng.wait_ge(s_dm, d + 4)
                    link(eng.tensor_tensor(U[:, :, 0:HID], made(HID), bcf(bias["x2"], HID), ALU.add))
                    eng.tensor_scalar(U[:, :, 0:HID], U[:, :, 0:HID], 0.0, None, ALU.max).then_inc(s_di, 1)
                    eng.wait_ge(s_dm, d + 5)
                    eng.tensor_tensor(Hn[:, :, :], made(F), bcf(bias["x3"]), ALU.add).then_inc(s_di, 1)
                    assert chained[0] == LINKS, chained
                chained[0] = before + ROUNDS * LINKS
                chain_base[0] = 0
                nd = ROUNDS * DENSE_PER_ROUND

                eng.wait_ge(s_di, nd + 1)
                link(eng.tensor_tensor(X[:, :, :], X[:, :, :], Hn[:, :, :], ALU.add))
                link(norm())
                if windows:
                    eng.tensor_scalar(V[:, :, :], Hn[:, :, :], H_SCALE, None, ALU.mult).then_inc(s_tf, 1)
                table(tabH, Hn[:, :, :], H_SCALE).then_inc(s_tab, 1)
                reciprocal_count()
                stages = [(0, onehots(L1_BASE, 1, s_gat, L1_BASE, 4, (ND, ND)) if windows else
                           onehots(L1_BASE, 0, s_gat, L1_BASE, 4)),
                          (2, message(L1_BASE, 0, 0, ea4, K1, 4)), (1, select16(L1_BASE, s_tr, windows))]
                low = (2, low16(L1_BASE, msg, sc[:, 4:5]))
                if windows:
                    skewed(eng, stages + [(4, window_sum(L1_BASE, 2 * F)), low, (2, onehot_m(L1_BASE, rel, WIN))])
                    eng.wait_ge(s_at, ROUNDS + 1)
                    link(window_sums(2 * F, F, 0, sc[0:ROWS, 5:6]))
                else:
                    skewed(eng, stages + [low, (2, onehot_m(L1_BASE, m4d, SPAN4))])
                    eng.wait_ge(s_at, ROUNDS + 1)
                    link(sums(Q4, F, sc[0:ROWS, 5:6]))
                link(eng.tensor_tensor(W[:, :, :], S[:, :, :], bcj(rcnt), ALU.mult))
                link(eng.tensor_tensor(W[:, :, :], W[:, :, :], bcf(bias["c"]), ALU.add))
                eng.tensor_copy(U[:, :, :], W[:, :, :]).then_inc(s_di, 1)
                eng.wait_ge(s_dm, nd + 1)
                link(eng.tensor_tensor(W[:, :, :], made(F), W[:, :, :], ALU.add))
                for k in range(2):
                    if k:
                        link(eng.tensor_tensor(U[:, :, :], W[:, :, :], W[:, :, :], ALU.mult))
                    link(eng.tensor_tensor(U[:, :, :], (W, U)[k][:, :, :], bcj(nmask), ALU.mult))
                    eng.tensor_reduce(cs[:, :], U[:, :, :].rearrange("p j f -> p f j"), AX.X, ALU.add).then_inc(s_bn, 1)
                    eng.wait_ge(s_bm, k + 1)
                    ins = eng.tensor_scalar(cm[:, :], bank[1][0:ROWS, 0:F], 1.0 / N, None, ALU.mult)
                    if k == 0:
                        link(ins)
                        link(eng.tensor_tensor(W[:, :, :], W[:, :, :], bcf(cm), ALU.subtract))
                    else:
                        ins.then_inc(s_var, 1)
                norms[0] += 1
                eng.wait_ge(s_std, norms[0])
                link(eng.reciprocal(cm[:, :], cm[:, :]))
                link(eng.tensor_tensor(cm[:, :], cm[:, :], bias["g"][:, :], ALU.mult))
                link(eng.tensor_tensor(W[:, :, :], W[:, :, :], bcf(cm), ALU.mult))
                link(eng.tensor_tensor(W[:, :, :], W[:, :, :], bcf(bias["be"]), ALU.add))
                link(eng.scalar_tensor_tensor(W[:, :, :], W[:, :, :], 0.01, W[:, :, :], ALU.mult, ALU.max))
                link(eng.tensor_tensor(X[:, :, :], X[:, :, :], W[:, :, :], ALU.add))

                link(norm())
                table(tabH, Hn[:, :, :], H_SCALE, windows).then_inc(s_tab, 1)
                if windows:
                    skewed(eng, [(0, window_onehots(L1_BASE)), (4, low16(L2_BASE, msg, sc[:, 6:7])),
                                 (3, message(L2_BASE, Y2_BASE, NG, ea8, K2, 2, ybank4)),
                                 (3, onehot_m(L2_BASE, ms, SPAN7))])
                else:
                    skewed(eng, [(0, onehots(L2_BASE, 0, s_gat, L2_BASE, 4)),
                                 (2, message(L2_BASE, Y2_BASE, NG, ea8, K2, 2)),
                                 (1, select16(L2_BASE, s_tr)), (2, low16(L2_BASE, msg, sc[:, 6:7])),
                                 (2, onehot_m(L2_BASE, m4s, SPAN4))])
                eng.wait_ge(s_at, ROUNDS + 2)
                link(sums7(sc[0:ROWS, 7:8]) if windows else sums(Q4, F, sc[0:ROWS, 7:8]))
                link(eng.tensor_tensor(X[:, :, :], X[:, :, :], S[:, :, :], ALU.add))

                link(norm())
                table(tabH, Hn[:, :, :], H_SCALE, windows).then_inc(s_tab, 1)
                if windows:
                    skewed(eng, [(0, window_onehots(L2_BASE)), (2, low16(L3_BASE, gx, 1.0)),
                                 (2, onehot_m(L3_BASE, ms, SPAN7))])
                else:
                    skewed(eng, [(0, onehots(L3_BASE, 0, s_gat, L3_BASE, 4)), (1, select16(L3_BASE, s_lo)),
                                 (2, low16(L3_BASE, gx, 1.0)), (2, onehot_m(L3_BASE, m4s, SPAN4))])
                eng.wait_ge(s_at, ROUNDS + 3)
                link(sums7(1.0 / H_SCALE) if windows else sums(Q4, F, 1.0 / H_SCALE))
                AHEAD = 3
                for k in range(HI + AHEAD):
                    if k < HI:
                        for j in (2 * k, 2 * k + 1):
                            ins = eng.tensor_tensor(outer[:, j, :, :],
                                                    Hn[:, j, :].unsqueeze(2).broadcast_to([ROWS, F, F]),
                                                    S[:, j, :].unsqueeze(1).broadcast_to([ROWS, F, F]), ALU.mult)
                        ins.then_inc(s_uo, 1)
                    c = k - AHEAD
                    if c >= 0 and c % 2:
                        eng.wait_ge(s_ot, c + 1)
                        if c >= 2:
                            eng.wait_ge(s_om2, c - 1)
                        eng.tensor_copy(accs[:, 0:4 * ROWS], bank[1][:, 0:4 * ROWS]).then_inc(s_oc[1], 1)
                eng.wait_ge(s_om2, HI)
                eng.tensor_copy(U[:, :, :], bank[4][0:ROWS, 0:BLOCKS * F].rearrange("p (j f) -> p j f", f=F)) \
                   .then_inc(s_di, 1)
                eng.wait_ge(s_dm, nd + 2)
                link(eng.tensor_tensor(X[:, :, :], made(F), X[:, :, :], ALU.add))
                eng.tensor_tensor(X[:, :, :], X[:, :, :], bcf(bias["o"]), ALU.add).then_inc(s_x, 1)

            near = flag_of(eng)
            with eng.If(near != 0):
                main(True)
            with eng.Else():
                main(False)


def kernel(**a):
    import numpy as np
    import concourse.bacc as bacc
    from concourse import mybir as mb
    from concourse.bass_utils import run_bass_kernel_spmd as run

    g = lambda name: np.asarray(a[name])
    f = a["x"].shape[1]
    k1, k2 = a["edge_attr_4"].shape[1], a["edge_attr_8"].shape[1]
    arrays = [g("x"), g("src"), g("dst"), g("edge_attr_4"), g("edge_attr_8")]
    arrays += [g("L0_gnn_" + n) for n in ("fe_W1", "fe_b1", "fe_W2", "fe_b2", "fe_W3", "fe_b3",
                                          "fx_W1", "fx_b1", "fx_W2", "fx_b2", "fx_W3", "fx_b3")]
    arrays += [g("L1_gnn_enet_w").reshape(f, f, k1).transpose(0, 2, 1).reshape(f, k1 * f),
               g("L1_gnn_enet_b").reshape(f, f), g("L1_gnn_root"), g("L1_gnn_bias"), g("L1_gnn_gamma"),
               g("L1_gnn_beta"),
               g("L2_gnn_kernel").reshape(k2, f, f).transpose(2, 0, 1).reshape(f, k2 * f),
               g("L2_gnn_bias").reshape(f, f).T,
               g("L3_gnn_W_tp").reshape(f * f, f), g("L3_gnn_weight").T, g("L3_gnn_bias")]
    nc = bacc.Bacc("TRN2", target_bir_lowering=False, num_devices=1)
    feed, args = {}, []
    for i, v in enumerate(arrays):
        v = np.ascontiguousarray(v)
        feed[f"in_{i}"] = v
        args.append(nc.dram_tensor(f"in_{i}", v.shape, mb.dt.from_np(v.dtype), kind="ExternalInput").ap())
    o = nc.dram_tensor("out_x", a["x"].shape, mb.dt.float32, kind="ExternalOutput").ap()
    gnn_program(nc, *args, o)
    r = run(nc, [feed], core_ids=[0])
    return r.results[0]["out_x"]
```
